# Optimizing a Trainium2 kernel written in Bass

```python
import numpy as np
import jax
import jax.numpy as jnp

def _softmax(x, axis=-1):
    return jax.nn.softmax(x, axis=axis)

def _gelu(x):
    return jax.nn.gelu(x, approximate=True)

def _silu(x):
    return jax.nn.silu(x)

def _sigmoid(x):
    return jax.nn.sigmoid(x)

def _layernorm(x, axis=-1, eps=1e-05):
    m = jnp.mean(x, axis=axis, keepdims=True)
    v = jnp.var(x, axis=axis, keepdims=True)
    return (x - m) / jnp.sqrt(v + eps)

def _scatter_add(tgt, idx, src, axis=0):
    return tgt.at[idx].add(src)

def _segment_sum(src, seg, n):
    return jax.ops.segment_sum(src, seg, n)
kernel_name = 'mk_adaln_attn_ffn_d1_seqx_r8_027853'

def setup_inputs(seed: int=0):
    np.random.seed(seed)
    _w = jnp.asarray

    def _rec_inputs():
        import jax
        import jax.numpy as jnp
        _rk = jax.random.key(seed)
        x = -5.13e-06 + 0.01765 * jax.random.normal(jax.random.fold_in(_rk, 1), (2, 512, 128), jnp.float32)
        _lenS = 512 - jax.random.randint(jax.random.fold_in(_rk, 7), (2,), 0, max(1, 512 // 4) + 1, jnp.int32)
        _lenS2 = 512 - jax.random.randint(jax.random.fold_in(_rk, 8), (2,), 0, max(1, 512 // 4) + 1, jnp.int32)
        cond_1024 = 0.0061147 + 1.02565 * jax.random.normal(jax.random.fold_in(_rk, 11), (2, 128), jnp.float32)
        _validS = jnp.arange(512)[None, :] < _lenS[:, None]
        _validS2 = jnp.arange(512)[None, :] < _lenS2[:, None]
        _causal = jnp.tril(jnp.ones((512, 512), dtype=bool))
        mask_Bx1x1xS_ff0 = jnp.where(jnp.ones((2, 1, 1, 512), dtype=bool), 0.0, -1000000000.0).astype(jnp.float32)
        return (x, cond_1024, mask_Bx1x1xS_ff0)
    x, cond_1024, mask_Bx1x1xS_ff0 = _rec_inputs()

    def _L0_cond_setup():
        import math
        import jax, jax.numpy as jnp
        import numpy as np
        EPS = 1e-07
        MAX_TANH_ARG = 1.0 - 1e-05

        def _norm(x):
            return jnp.sqrt(jnp.sum(x * x, axis=-1, keepdims=True)).clip(EPS)

        def logmap0(x):
            n = _norm(x)
            return jnp.arctanh(jnp.clip(n, EPS, MAX_TANH_ARG)) * x / n

        def expmap0(v):
            n = _norm(v)
            return jnp.tanh(n) * v / n

        def mobius_add(x, y):
            x2 = jnp.sum(x * x, -1, keepdims=True)
            y2 = jnp.sum(y * y, -1, keepdims=True)
            xy = jnp.sum(x * y, -1, keepdims=True)
            num = (1 + 2 * xy + y2) * x + (1 - x2) * y
            den = (1 + 2 * xy + x2 * y2).clip(EPS)
            return num / den

        def plin(x, w, b):
            return expmap0(logmap0(x) @ w + b)

        def layer_norm(x, eps=1e-06):
            m = x.mean(-1, keepdims=True)
            v = ((x - m) ** 2).mean(-1, keepdims=True)
            return (x - m) / jnp.sqrt(v + eps)

        def _beta(a, b):
            return math.exp(math.lgamma(a) + math.lgamma(b) - math.lgamma(a + b))
        D, H, FF = (128, 16, 512)
        HD = D // H
        BETA_N = _beta(D / 2, 0.5)
        BETA_H = _beta(HD / 2, 0.5)

        def _to_heads(p):
            B, S, _ = p.shape
            t = logmap0(p).reshape(B, S, H, HD) * (BETA_H / BETA_N)
            return expmap0(jnp.transpose(t, (0, 2, 1, 3)))

        def _from_heads(ph):
            B, _, S, _ = ph.shape
            t = logmap0(ph) * (BETA_N / BETA_H)
            t = jnp.transpose(t, (0, 2, 1, 3)).reshape(B, S, D)
            return expmap0(t)
        key = jax.random.key(seed)
        ks = jax.random.split(key, 20)
        B, S = (4, 128)
        x = expmap0(0.02 * jax.random.normal(ks[0], (B, S, D), jnp.float32))
        t_emb = jax.random.normal(ks[1], (B, 1, D), jnp.float32)
        g = lambda k, sh: 0.02 * jax.random.normal(k, sh, jnp.float32)
        return {'x': x, 't_emb': t_emb, 'w_q': g(ks[2], (D, D)), 'b_q': jnp.zeros((D,), jnp.float32), 'w_k': g(ks[3], (D, D)), 'b_k': jnp.zeros((D,), jnp.float32), 'w_v': g(ks[4], (D, D)), 'b_v': jnp.zeros((D,), jnp.float32), 'w_o': g(ks[5], (D, D)), 'b_o': jnp.zeros((D,), jnp.float32), 'w_f1': g(ks[6], (D, FF)), 'b_f1': jnp.zeros((FF,), jnp.float32), 'w_f2': g(ks[7], (FF, D)), 'b_f2': jnp.zeros((D,), jnp.float32), 'w_ada': g(ks[8], (D, 6 * D)), 'b_ada': jnp.zeros((6 * D,), jnp.float32)}
    _L0_cond_all = _L0_cond_setup()
    _L0_cond_in = {k: v for k, v in _L0_cond_all.items() if k in ('w_q', 'b_q', 'w_k', 'b_k', 'w_v', 'b_v', 'w_o', 'b_o', 'w_f1', 'b_f1', 'w_f2', 'b_f2', 'w_ada', 'b_ada')}
    del _L0_cond_all

    def _L0_attn_setup():
        import jax, jax.numpy as jnp
        import numpy as np
        NUM_HEADS = 16
        DIM = 128
        HEAD_DIM = DIM // 2 // NUM_HEADS
        SCALE = HEAD_DIM ** (-0.5)
        NBITS_W = 4
        NBITS_ATT = 8

        def round_ste(x):
            return x + jax.lax.stop_gradient(jnp.round(x) - x)

        def quant_weight(w, alpha, nbits):
            qn, qp = (-2 ** (nbits - 1), 2 ** (nbits - 1) - 1)
            return round_ste(jnp.clip(w / alpha, qn, qp)) * alpha

        def quant_act(x, alpha, zp, nbits):
            qn, qp = (-2 ** (nbits - 1), 2 ** (nbits - 1) - 1)
            zp_r = round_ste(zp)
            xq = round_ste(jnp.clip(x / alpha + zp_r, qn, qp))
            return (xq - zp_r) * alpha
        key = jax.random.key(seed)
        ks = jax.random.split(key, 9)
        B, N = (8, 128)
        x = jax.random.normal(ks[0], (B, N, DIM), jnp.float32)
        qkv_w = jax.random.normal(ks[1], (DIM // 2 * 3, DIM), jnp.float32) * 0.02
        proj_w = jax.random.normal(ks[2], (DIM, DIM // 2), jnp.float32) * 0.02
        proj_b = jnp.zeros((DIM,), jnp.float32)
        qkv_alpha = 0.05 + 0.1 * jax.random.uniform(ks[3], (DIM // 2 * 3, 1), jnp.float32)
        proj_alpha = 0.05 + 0.1 * jax.random.uniform(ks[4], (DIM, 1), jnp.float32)
        bias_q = jnp.zeros((1, NUM_HEADS, 1, 1), jnp.float32)
        bias_k = jnp.zeros((1, NUM_HEADS, 1, 1), jnp.float32)

        def act_params(k):
            a = 0.05 + 0.1 * jax.random.uniform(k, (1, NUM_HEADS, 1, 1), jnp.float32)
            z = jnp.zeros((1, NUM_HEADS, 1, 1), jnp.float32)
            return (a, z)
        q_alpha, q_zp = act_params(ks[5])
        k_alpha, k_zp = act_params(ks[6])
        v_alpha, v_zp = act_params(ks[7])
        attn_alpha, attn_zp = act_params(ks[8])
        return dict(x=x, qkv_w=qkv_w, qkv_alpha=qkv_alpha, bias_q=bias_q, bias_k=bias_k, q_alpha=q_alpha, q_zp=q_zp, k_alpha=k_alpha, k_zp=k_zp, v_alpha=v_alpha, v_zp=v_zp, attn_alpha=attn_alpha, attn_zp=attn_zp, proj_w=proj_w, proj_b=proj_b, proj_alpha=proj_alpha)
    _L0_attn_all = _L0_attn_setup()
    _L0_attn_in = {k: v for k, v in _L0_attn_all.items() if k in ('qkv_w', 'qkv_alpha', 'bias_q', 'bias_k', 'q_alpha', 'q_zp', 'k_alpha', 'k_zp', 'v_alpha', 'v_zp', 'attn_alpha', 'attn_zp', 'proj_w', 'proj_b', 'proj_alpha')}
    del _L0_attn_all

    def _L0_cond2_setup():
        import jax, jax.numpy as jnp
        import numpy as np
        EMBED = 128
        HEADS = 16
        HDIM = EMBED // HEADS
        MASK_OUT = -10000.0

        def _split_heads(t):
            B, T, _ = t.shape
            return t.reshape(B, T, HEADS, HDIM).transpose(0, 2, 1, 3)
        key = jax.random.key(seed)
        ks = jax.random.split(key, 12)
        B, S = (4, 1023)
        scale = 0.02
        return {'word_hidden_states': jax.random.normal(ks[0], (B, S, EMBED), jnp.float32), 'image_hidden_states': jax.random.normal(ks[1], (B, EMBED), jnp.float32), 'attention_mask': jnp.zeros((B, 1, 1, S), jnp.float32), 'c_attn_w': jax.random.normal(ks[2], (EMBED, 3 * EMBED), jnp.float32) * scale, 'c_attn_b': jnp.zeros((3 * EMBED,), jnp.float32), 'c_proj_w': jax.random.normal(ks[3], (EMBED, EMBED), jnp.float32) * scale, 'c_proj_b': jnp.zeros((EMBED,), jnp.float32), 'uk_w': jax.random.normal(ks[4], (EMBED, EMBED), jnp.float32) * scale, 'uk_b': jnp.zeros((EMBED,), jnp.float32), 'uv_w': jax.random.normal(ks[5], (EMBED, EMBED), jnp.float32) * scale, 'uv_b': jnp.zeros((EMBED,), jnp.float32)}
    _L0_cond2_all = _L0_cond2_setup()
    _L0_cond2_in = {k: v for k, v in _L0_cond2_all.items() if k in ('c_attn_w', 'c_attn_b', 'c_proj_w', 'c_proj_b', 'uk_w', 'uk_b', 'uv_w', 'uv_b')}
    del _L0_cond2_all

    def _L0_ffn_setup():
        import jax, jax.numpy as jnp
        import numpy as np
        DIM = 128
        DEPTH = 2
        HEADS = 8
        DIM_HEAD = 64
        WINDOW = 64
        INNER = HEADS * DIM_HEAD
        HID = int(DIM * 4 * 2 / 3)
        B, N = (2, 1024)
        QK_SCALE = 8.0

        def shift_token(t):
            t1, t2 = jnp.split(t, 2, axis=-1)
            t2 = jnp.pad(t2, ((0, 0), (1, 0), (0, 0)))[:, :-1]
            return jnp.concatenate([t1, t2], axis=-1)

        def l2norm(t):
            return t / jnp.clip(jnp.linalg.norm(t, axis=-1, keepdims=True), 1e-12)

        def rotate_half(x):
            x1, x2 = jnp.split(x, 2, axis=-1)
            return jnp.concatenate([-x2, x1], axis=-1)

        def rotary_xpos(q, k):
            n = q.shape[-2]
            half_idx = jnp.arange(0, DIM_HEAD, 2, dtype=jnp.float32)
            inv_freq = 1.0 / 10000.0 ** (half_idx / DIM_HEAD)
            t = jnp.arange(n, dtype=jnp.float32)
            freqs = t[:, None] * inv_freq[None, :]
            freqs = jnp.concatenate([freqs, freqs], axis=-1)
            base = (half_idx + 0.4 * DIM_HEAD) / (1.4 * DIM_HEAD)
            power = (t - n // 2) / float(WINDOW // 2)
            scale = base[None, :] ** power[:, None]
            scale = jnp.concatenate([scale, scale], axis=-1)
            cos, sin = (jnp.cos(freqs), jnp.sin(freqs))
            q = q * cos * scale + rotate_half(q) * sin * scale
            k = k * cos / scale + rotate_half(k) * sin / scale
            return (q, k)

        def local_attention(q, k, v):
            b, h, n, d = q.shape
            w = n // WINDOW
            bq = q.reshape(b, h, w, WINDOW, d) * QK_SCALE
            bk = k.reshape(b, h, w, WINDOW, d)
            bv = v.reshape(b, h, w, WINDOW, d)

            def look_around(t):
                p = jnp.pad(t, ((0, 0), (0, 0), (1, 0), (0, 0), (0, 0)))
                return jnp.concatenate([p[:, :, :w], p[:, :, 1:]], axis=3)
            bk, bv = (look_around(bk), look_around(bv))
            bt = jnp.arange(n).reshape(w, WINDOW)
            btp = jnp.pad(bt, ((1, 0), (0, 0)), constant_values=-1)
            btk = jnp.concatenate([btp[:w], btp[1:]], axis=1)
            sim = jnp.einsum('bhwid,bhwjd->bhwij', bq, bk)
            i = bt[:, :, None]
            j = btk[:, None, :]
            mask = (i < j) | (i > j + WINDOW) | (j == -1)
            sim = jnp.where(mask, -jnp.finfo(sim.dtype).max, sim)
            attn = jax.nn.softmax(sim, axis=-1)
            out = jnp.einsum('bhwij,bhwjd->bhwid', attn, bv)
            return out.reshape(b, h, n, d)

        def _layer(x, wqkv, qs, ksc, wo, lg, lb, w1, b1, w2, b2):
            b, n, _ = x.shape
            h = shift_token(x)
            qkv = h @ wqkv
            q, k, v = jnp.split(qkv, 3, axis=-1)
            to_heads = lambda t: t.reshape(b, n, HEADS, DIM_HEAD).transpose(0, 2, 1, 3)
            q, k, v = (to_heads(q), to_heads(k), to_heads(v))
            q = l2norm(q) * qs
            k = l2norm(k) * ksc
            q, k = rotary_xpos(q, k)
            o = local_attention(q, k, v)
            o = o.transpose(0, 2, 1, 3).reshape(b, n, INNER)
            x = x + o @ wo
            h = shift_token(x)
            mu = h.mean(-1, keepdims=True)
            var = h.var(-1, keepdims=True)
            h = (h - mu) / jnp.sqrt(var + 1e-05) * lg + lb
            h = h @ w1 + b1
            a, g = jnp.split(h, 2, axis=-1)
            h = a * jax.nn.gelu(g, approximate=False)
            x = x + h @ w2 + b2
            return x
        key = jax.random.key(seed)
        ks = jax.random.split(key, 6)
        return {'x': jax.random.normal(ks[0], (B, N, DIM), jnp.float32), 'wqkv': jax.random.normal(ks[1], (DEPTH, DIM, 3 * INNER), jnp.float32) * 0.02, 'q_scale': jnp.ones((DEPTH, DIM_HEAD), jnp.float32), 'k_scale': jnp.ones((DEPTH, DIM_HEAD), jnp.float32), 'wo': jax.random.normal(ks[2], (DEPTH, INNER, DIM), jnp.float32) * 0.02, 'ln_g': jnp.ones((DEPTH, DIM), jnp.float32), 'ln_b': jnp.zeros((DEPTH, DIM), jnp.float32), 'w1': jax.random.normal(ks[3], (DEPTH, DIM, 2 * HID), jnp.float32) * 0.02, 'b1': jnp.zeros((DEPTH, 2 * HID), jnp.float32), 'w2': jax.random.normal(ks[4], (DEPTH, HID, DIM), jnp.float32) * 0.02, 'b2': jnp.zeros((DEPTH, DIM), jnp.float32)}
    _L0_ffn_all = _L0_ffn_setup()
    _L0_ffn_in = {k: v for k, v in _L0_ffn_all.items() if k in ('wqkv', 'q_scale', 'k_scale', 'wo', 'ln_g', 'ln_b', 'w1', 'b1', 'w2', 'b2')}
    del _L0_ffn_all
    return {'x': x, 'cond_1024': cond_1024, 'mask_Bx1x1xS_ff0': mask_Bx1x1xS_ff0, 'L0_cond_w_q': _L0_cond_in['w_q'], 'L0_cond_b_q': _L0_cond_in['b_q'], 'L0_cond_w_k': _L0_cond_in['w_k'], 'L0_cond_b_k': _L0_cond_in['b_k'], 'L0_cond_w_v': _L0_cond_in['w_v'], 'L0_cond_b_v': _L0_cond_in['b_v'], 'L0_cond_w_o': _L0_cond_in['w_o'], 'L0_cond_b_o': _L0_cond_in['b_o'], 'L0_cond_w_f1': _L0_cond_in['w_f1'], 'L0_cond_b_f1': _L0_cond_in['b_f1'], 'L0_cond_w_f2': _L0_cond_in['w_f2'], 'L0_cond_b_f2': _L0_cond_in['b_f2'], 'L0_cond_w_ada': _L0_cond_in['w_ada'], 'L0_cond_b_ada': _L0_cond_in['b_ada'], 'L0_attn_qkv_w': _L0_attn_in['qkv_w'], 'L0_attn_qkv_alpha': _L0_attn_in['qkv_alpha'], 'L0_attn_bias_q': _L0_attn_in['bias_q'], 'L0_attn_bias_k': _L0_attn_in['bias_k'], 'L0_attn_q_alpha': _L0_attn_in['q_alpha'], 'L0_attn_q_zp': _L0_attn_in['q_zp'], 'L0_attn_k_alpha': _L0_attn_in['k_alpha'], 'L0_attn_k_zp': _L0_attn_in['k_zp'], 'L0_attn_v_alpha': _L0_attn_in['v_alpha'], 'L0_attn_v_zp': _L0_attn_in['v_zp'], 'L0_attn_attn_alpha': _L0_attn_in['attn_alpha'], 'L0_attn_attn_zp': _L0_attn_in['attn_zp'], 'L0_attn_proj_w': _L0_attn_in['proj_w'], 'L0_attn_proj_b': _L0_attn_in['proj_b'], 'L0_attn_proj_alpha': _L0_attn_in['proj_alpha'], 'L0_cond2_c_attn_w': _L0_cond2_in['c_attn_w'], 'L0_cond2_c_attn_b': _L0_cond2_in['c_attn_b'], 'L0_cond2_c_proj_w': _L0_cond2_in['c_proj_w'], 'L0_cond2_c_proj_b': _L0_cond2_in['c_proj_b'], 'L0_cond2_uk_w': _L0_cond2_in['uk_w'], 'L0_cond2_uk_b': _L0_cond2_in['uk_b'], 'L0_cond2_uv_w': _L0_cond2_in['uv_w'], 'L0_cond2_uv_b': _L0_cond2_in['uv_b'], 'L0_ffn_wqkv': _L0_ffn_in['wqkv'], 'L0_ffn_q_scale': _L0_ffn_in['q_scale'], 'L0_ffn_k_scale': _L0_ffn_in['k_scale'], 'L0_ffn_wo': _L0_ffn_in['wo'], 'L0_ffn_ln_g': _L0_ffn_in['ln_g'], 'L0_ffn_ln_b': _L0_ffn_in['ln_b'], 'L0_ffn_w1': _L0_ffn_in['w1'], 'L0_ffn_b1': _L0_ffn_in['b1'], 'L0_ffn_w2': _L0_ffn_in['w2'], 'L0_ffn_b2': _L0_ffn_in['b2']}

def reference(x, cond_1024, mask_Bx1x1xS_ff0, L0_cond_w_q, L0_cond_b_q, L0_cond_w_k, L0_cond_b_k, L0_cond_w_v, L0_cond_b_v, L0_cond_w_o, L0_cond_b_o, L0_cond_w_f1, L0_cond_b_f1, L0_cond_w_f2, L0_cond_b_f2, L0_cond_w_ada, L0_cond_b_ada, L0_attn_qkv_w, L0_attn_qkv_alpha, L0_attn_bias_q, L0_attn_bias_k, L0_attn_q_alpha, L0_attn_q_zp, L0_attn_k_alpha, L0_attn_k_zp, L0_attn_v_alpha, L0_attn_v_zp, L0_attn_attn_alpha, L0_attn_attn_zp, L0_attn_proj_w, L0_attn_proj_b, L0_attn_proj_alpha, L0_cond2_c_attn_w, L0_cond2_c_attn_b, L0_cond2_c_proj_w, L0_cond2_c_proj_b, L0_cond2_uk_w, L0_cond2_uk_b, L0_cond2_uv_w, L0_cond2_uv_b, L0_ffn_wqkv, L0_ffn_q_scale, L0_ffn_k_scale, L0_ffn_wo, L0_ffn_ln_g, L0_ffn_ln_b, L0_ffn_w1, L0_ffn_b1, L0_ffn_w2, L0_ffn_b2):
    import jax
    import jax.numpy as jnp

    def _L0_cond_ref(x, t_emb, w_q, b_q, w_k, b_k, w_v, b_v, w_o, b_o, w_f1, b_f1, w_f2, b_f2, w_ada, b_ada):
        import math
        import jax, jax.numpy as jnp
        import numpy as np
        EPS = 1e-07
        MAX_TANH_ARG = 1.0 - 1e-05

        def _norm(x):
            return jnp.sqrt(jnp.sum(x * x, axis=-1, keepdims=True)).clip(EPS)

        def logmap0(x):
            n = _norm(x)
            return jnp.arctanh(jnp.clip(n, EPS, MAX_TANH_ARG)) * x / n

        def expmap0(v):
            n = _norm(v)
            return jnp.tanh(n) * v / n

        def mobius_add(x, y):
            x2 = jnp.sum(x * x, -1, keepdims=True)
            y2 = jnp.sum(y * y, -1, keepdims=True)
            xy = jnp.sum(x * y, -1, keepdims=True)
            num = (1 + 2 * xy + y2) * x + (1 - x2) * y
            den = (1 + 2 * xy + x2 * y2).clip(EPS)
            return num / den

        def plin(x, w, b):
            return expmap0(logmap0(x) @ w + b)

        def layer_norm(x, eps=1e-06):
            m = x.mean(-1, keepdims=True)
            v = ((x - m) ** 2).mean(-1, keepdims=True)
            return (x - m) / jnp.sqrt(v + eps)

        def _beta(a, b):
            return math.exp(math.lgamma(a) + math.lgamma(b) - math.lgamma(a + b))
        D, H, FF = (128, 16, 512)
        HD = D // H
        BETA_N = _beta(D / 2, 0.5)
        BETA_H = _beta(HD / 2, 0.5)

        def _to_heads(p):
            B, S, _ = p.shape
            t = logmap0(p).reshape(B, S, H, HD) * (BETA_H / BETA_N)
            return expmap0(jnp.transpose(t, (0, 2, 1, 3)))

        def _from_heads(ph):
            B, _, S, _ = ph.shape
            t = logmap0(ph) * (BETA_N / BETA_H)
            t = jnp.transpose(t, (0, 2, 1, 3)).reshape(B, S, D)
            return expmap0(t)
        ada = t_emb @ w_ada + b_ada
        sh_msa, sc_msa, g_msa, sh_mlp, sc_mlp, g_mlp = jnp.split(ada, 6, axis=-1)
        residual = x
        xn = layer_norm(logmap0(x))
        xm = expmap0(xn * (1 + sc_msa) + sh_msa)
        q = _to_heads(plin(xm, w_q, b_q))
        k = _to_heads(plin(xm, w_k, b_k))
        v = _to_heads(plin(xm, w_v, b_v))
        qt, kt, vt = (logmap0(q), logmap0(k), logmap0(v))
        scores = jnp.einsum('bhqd,bhkd->bhqk', qt, kt) / math.sqrt(HD)
        attn = jax.nn.softmax(scores, axis=-1)
        out_h = expmap0(jnp.einsum('bhqk,bhkd->bhqd', attn, vt))
        attn_out = plin(_from_heads(out_h), w_o, b_o)
        attn_t = g_msa * logmap0(attn_out)
        x = mobius_add(residual, expmap0(attn_t))
        residual = x
        xn = layer_norm(logmap0(x))
        xm = expmap0(xn * (1 + sc_mlp) + sh_mlp)
        ff = plin(plin(xm, w_f1, b_f1), w_f2, b_f2)
        ff_t = g_mlp * logmap0(ff)
        return mobius_add(residual, expmap0(ff_t))

    def _L0_attn_ref(x, qkv_w, qkv_alpha, bias_q, bias_k, q_alpha, q_zp, k_alpha, k_zp, v_alpha, v_zp, attn_alpha, attn_zp, proj_w, proj_b, proj_alpha):
        import jax, jax.numpy as jnp
        import numpy as np
        NUM_HEADS = 16
        DIM = 128
        HEAD_DIM = DIM // 2 // NUM_HEADS
        SCALE = HEAD_DIM ** (-0.5)
        NBITS_W = 4
        NBITS_ATT = 8

        def round_ste(x):
            return x + jax.lax.stop_gradient(jnp.round(x) - x)

        def quant_weight(w, alpha, nbits):
            qn, qp = (-2 ** (nbits - 1), 2 ** (nbits - 1) - 1)
            return round_ste(jnp.clip(w / alpha, qn, qp)) * alpha

        def quant_act(x, alpha, zp, nbits):
            qn, qp = (-2 ** (nbits - 1), 2 ** (nbits - 1) - 1)
            zp_r = round_ste(zp)
            xq = round_ste(jnp.clip(x / alpha + zp_r, qn, qp))
            return (xq - zp_r) * alpha
        B, N, C2 = x.shape
        C = C2 // 2
        wq = quant_weight(qkv_w, qkv_alpha, NBITS_W)
        qkv = jnp.einsum('bnc,oc->bno', x, wq)
        qkv = qkv.reshape(B, N, 3, NUM_HEADS, C // NUM_HEADS).transpose(2, 0, 3, 1, 4)
        q = qkv[0] + bias_q
        k = qkv[1] + bias_k
        v = qkv[2]
        q = quant_act(q, q_alpha, q_zp, NBITS_W) * SCALE
        k = quant_act(k, k_alpha, k_zp, NBITS_W)
        v = quant_act(v, v_alpha, v_zp, NBITS_W)
        attn = jnp.einsum('bhnd,bhmd->bhnm', q, k)
        attn = jax.nn.softmax(attn, axis=-1)
        attn = quant_act(attn, attn_alpha, attn_zp, NBITS_ATT)
        out = jnp.einsum('bhnm,bhmd->bhnd', attn, v)
        out = out.transpose(0, 2, 1, 3).reshape(B, N, C)
        wp = quant_weight(proj_w, proj_alpha, NBITS_W)
        return jnp.einsum('bnc,oc->bno', out, wp) + proj_b

    def _L0_cond2_ref(word_hidden_states, image_hidden_states, attention_mask, c_attn_w, c_attn_b, c_proj_w, c_proj_b, uk_w, uk_b, uv_w, uv_b):
        import jax, jax.numpy as jnp
        import numpy as np
        EMBED = 128
        HEADS = 16
        HDIM = EMBED // HEADS
        MASK_OUT = -10000.0

        def _split_heads(t):
            B, T, _ = t.shape
            return t.reshape(B, T, HEADS, HDIM).transpose(0, 2, 1, 3)
        B, S, _ = word_hidden_states.shape
        qkv = word_hidden_states @ c_attn_w + c_attn_b
        q_word, k_word, v_word = jnp.split(qkv, 3, axis=-1)
        img = image_hidden_states[:, None, :]
        k_img = img @ uk_w.T + uk_b
        v_img = img @ uv_w.T + uv_b
        k = jnp.concatenate([k_img, k_word], axis=1)
        v = jnp.concatenate([v_img, v_word], axis=1)
        q = _split_heads(q_word)
        k = _split_heads(k)
        v = _split_heads(v)
        scores = jnp.einsum('bhqd,bhkd->bhqk', q, k) / jnp.sqrt(jnp.float32(HDIM))
        qi = jnp.arange(S)[:, None]
        kj = jnp.arange(S + 1)[None, :]
        causal = kj <= qi + 1
        scores = jnp.where(causal[None, None], scores, jnp.float32(MASK_OUT))
        zero_col = jnp.zeros(attention_mask.shape[:-1] + (1,), attention_mask.dtype)
        mask = jnp.concatenate([zero_col, attention_mask], axis=-1)
        scores = scores + mask
        attn = jax.nn.softmax(scores, axis=-1)
        out = jnp.einsum('bhqk,bhkd->bhqd', attn, v)
        out = out.transpose(0, 2, 1, 3).reshape(B, S, EMBED)
        out = out @ c_proj_w + c_proj_b
        return out

    def _L0_ffn_ref(x, wqkv, q_scale, k_scale, wo, ln_g, ln_b, w1, b1, w2, b2):
        import jax, jax.numpy as jnp
        import numpy as np
        DIM = 128
        DEPTH = 2
        HEADS = 8
        DIM_HEAD = 64
        WINDOW = 64
        INNER = HEADS * DIM_HEAD
        HID = int(DIM * 4 * 2 / 3)
        B, N = (2, 1024)
        QK_SCALE = 8.0

        def shift_token(t):
            t1, t2 = jnp.split(t, 2, axis=-1)
            t2 = jnp.pad(t2, ((0, 0), (1, 0), (0, 0)))[:, :-1]
            return jnp.concatenate([t1, t2], axis=-1)

        def l2norm(t):
            return t / jnp.clip(jnp.linalg.norm(t, axis=-1, keepdims=True), 1e-12)

        def rotate_half(x):
            x1, x2 = jnp.split(x, 2, axis=-1)
            return jnp.concatenate([-x2, x1], axis=-1)

        def rotary_xpos(q, k):
            n = q.shape[-2]
            half_idx = jnp.arange(0, DIM_HEAD, 2, dtype=jnp.float32)
            inv_freq = 1.0 / 10000.0 ** (half_idx / DIM_HEAD)
            t = jnp.arange(n, dtype=jnp.float32)
            freqs = t[:, None] * inv_freq[None, :]
            freqs = jnp.concatenate([freqs, freqs], axis=-1)
            base = (half_idx + 0.4 * DIM_HEAD) / (1.4 * DIM_HEAD)
            power = (t - n // 2) / float(WINDOW // 2)
            scale = base[None, :] ** power[:, None]
            scale = jnp.concatenate([scale, scale], axis=-1)
            cos, sin = (jnp.cos(freqs), jnp.sin(freqs))
            q = q * cos * scale + rotate_half(q) * sin * scale
            k = k * cos / scale + rotate_half(k) * sin / scale
            return (q, k)

        def local_attention(q, k, v):
            b, h, n, d = q.shape
            w = n // WINDOW
            bq = q.reshape(b, h, w, WINDOW, d) * QK_SCALE
            bk = k.reshape(b, h, w, WINDOW, d)
            bv = v.reshape(b, h, w, WINDOW, d)

            def look_around(t):
                p = jnp.pad(t, ((0, 0), (0, 0), (1, 0), (0, 0), (0, 0)))
                return jnp.concatenate([p[:, :, :w], p[:, :, 1:]], axis=3)
            bk, bv = (look_around(bk), look_around(bv))
            bt = jnp.arange(n).reshape(w, WINDOW)
            btp = jnp.pad(bt, ((1, 0), (0, 0)), constant_values=-1)
            btk = jnp.concatenate([btp[:w], btp[1:]], axis=1)
            sim = jnp.einsum('bhwid,bhwjd->bhwij', bq, bk)
            i = bt[:, :, None]
            j = btk[:, None, :]
            mask = (i < j) | (i > j + WINDOW) | (j == -1)
            sim = jnp.where(mask, -jnp.finfo(sim.dtype).max, sim)
            attn = jax.nn.softmax(sim, axis=-1)
            out = jnp.einsum('bhwij,bhwjd->bhwid', attn, bv)
            return out.reshape(b, h, n, d)

        def _layer(x, wqkv, qs, ksc, wo, lg, lb, w1, b1, w2, b2):
            b, n, _ = x.shape
            h = shift_token(x)
            qkv = h @ wqkv
            q, k, v = jnp.split(qkv, 3, axis=-1)
            to_heads = lambda t: t.reshape(b, n, HEADS, DIM_HEAD).transpose(0, 2, 1, 3)
            q, k, v = (to_heads(q), to_heads(k), to_heads(v))
            q = l2norm(q) * qs
            k = l2norm(k) * ksc
            q, k = rotary_xpos(q, k)
            o = local_attention(q, k, v)
            o = o.transpose(0, 2, 1, 3).reshape(b, n, INNER)
            x = x + o @ wo
            h = shift_token(x)
            mu = h.mean(-1, keepdims=True)
            var = h.var(-1, keepdims=True)
            h = (h - mu) / jnp.sqrt(var + 1e-05) * lg + lb
            h = h @ w1 + b1
            a, g = jnp.split(h, 2, axis=-1)
            h = a * jax.nn.gelu(g, approximate=False)
            x = x + h @ w2 + b2
            return x
        for l in range(DEPTH):
            x = _layer(x, wqkv[l], q_scale[l], k_scale[l], wo[l], ln_g[l], ln_b[l], w1[l], b1[l], w2[l], b2[l])
        return x
    x = x + _L0_attn_ref(_L0_cond_ref(x, cond_1024[:, None, :], L0_cond_w_q, L0_cond_b_q, L0_cond_w_k, L0_cond_b_k, L0_cond_w_v, L0_cond_b_v, L0_cond_w_o, L0_cond_b_o, L0_cond_w_f1, L0_cond_b_f1, L0_cond_w_f2, L0_cond_b_f2, L0_cond_w_ada, L0_cond_b_ada), L0_attn_qkv_w, L0_attn_qkv_alpha, L0_attn_bias_q, L0_attn_bias_k, L0_attn_q_alpha, L0_attn_q_zp, L0_attn_k_alpha, L0_attn_k_zp, L0_attn_v_alpha, L0_attn_v_zp, L0_attn_attn_alpha, L0_attn_attn_zp, L0_attn_proj_w, L0_attn_proj_b, L0_attn_proj_alpha)
    x = x + _L0_ffn_ref(_L0_cond2_ref(x, cond_1024, mask_Bx1x1xS_ff0, L0_cond2_c_attn_w, L0_cond2_c_attn_b, L0_cond2_c_proj_w, L0_cond2_c_proj_b, L0_cond2_uk_w, L0_cond2_uk_b, L0_cond2_uv_w, L0_cond2_uv_b), L0_ffn_wqkv, L0_ffn_q_scale, L0_ffn_k_scale, L0_ffn_wo, L0_ffn_ln_g, L0_ffn_ln_b, L0_ffn_w1, L0_ffn_b1, L0_ffn_w2, L0_ffn_b2)
    return x

_drawn_inputs = setup_inputs


def setup_inputs(seed=0):
    import zlib

    import numpy as np

    out = dict(_drawn_inputs(seed))
    spreads = {'L0_cond_b_q': (0.0, 0.1),
     'L0_cond_b_k': (0.0, 0.1),
     'L0_cond_b_v': (0.0, 0.1),
     'L0_cond_b_o': (0.0, 0.1),
     'L0_cond_b_f1': (0.0, 0.1),
     'L0_cond_b_f2': (0.0, 0.1),
     'L0_cond_b_ada': (0.0, 0.1),
     'L0_attn_bias_q': (0.0, 0.1),
     'L0_attn_bias_k': (0.0, 0.1),
     'L0_attn_q_zp': (0.0, 0.1),
     'L0_attn_k_zp': (0.0, 0.1),
     'L0_attn_v_zp': (0.0, 0.1),
     'L0_attn_attn_zp': (0.0, 0.1),
     'L0_attn_proj_b': (0.0, 0.1),
     'L0_cond2_c_attn_b': (0.0, 0.1),
     'L0_cond2_c_proj_b': (0.0, 0.1),
     'L0_cond2_uk_b': (0.0, 2.0),
     'L0_cond2_uv_b': (0.0, 0.8),
     'L0_ffn_q_scale': (1.0, 0.6),
     'L0_ffn_k_scale': (1.0, 0.6),
     'L0_ffn_ln_g': (1.0, 0.6),
     'L0_ffn_ln_b': (0.0, 0.691),
     'L0_ffn_b1': (0.0, 0.1),
     'L0_ffn_b2': (0.0, 0.1)}
    factors = {'cond_1024': 5.383, 'L0_cond2_uk_w': 8.0, 'L0_cond2_uv_w': 5.872}
    for name, (base, spread) in spreads.items():
        noise = np.random.default_rng([zlib.crc32(name.encode()), seed]).standard_normal(out[name].shape)
        drawn = base * np.exp(spread * noise) if base else spread * noise
        out[name] = jnp.asarray(drawn.astype(out[name].dtype))
    for name, factor in factors.items():
        out[name] = (out[name] * factor).astype(out[name].dtype)
    return out
```

```python
from contextlib import ExitStack

import numpy as np
import concourse.bass as bass
from concourse import mybir

F32 = mybir.dt.float32
F16 = mybir.dt.float16
BF16 = mybir.dt.bfloat16
U8 = mybir.dt.uint8
U16 = mybir.dt.uint16
ALU = mybir.AluOpType
ACT = mybir.ActivationFunctionType
X = mybir.AxisListType.X

P = 128
B, S, D = 2, 512, 128
TB = S // P
T = B * TB
H = 16
HD = D // H
HQ = D // 2 // H
FF = 512
EPS = 1e-7
MAX_TANH = float(np.float32(1.0 - 1e-5))
REACH = float(np.arctanh(np.float64(np.float32(1.0 - 1e-5))))
SERIES_BELOW = 0.3
DH, DHD, WINDOW, DEPTH = 8, 64, 64, 2
INNER = DH * DHD
HID = int(D * 4 * 2 / 3)
ROUND = 12582912.0
U_ZERO = 1152.0
NEG_C = -30000.0
NEG_D = -1e30


def lgamma_beta(a, b):
    import math
    return math.exp(math.lgamma(a) + math.lgamma(b) - math.lgamma(a + b))


HEAD_SCALE = lgamma_beta(HD / 2, 0.5) / lgamma_beta(D / 2, 0.5)

VECTORS = [
    ("b_ada", 6 * D), ("b_qkv", 3 * D), ("b_o", D), ("b_f1", FF), ("b_f2", D),
    ("qkv_alpha", 3 * D // 2), ("proj_alpha", D), ("proj_b", D),
    ("bias_q", H), ("bias_k", H), ("q_alpha", H), ("k_alpha", H), ("v_alpha", H),
    ("q_zp", H), ("k_zp", H), ("v_zp", H), ("attn_alpha", H), ("attn_zp", H),
    ("c_attn_b", 3 * D), ("c_proj_b", D), ("uk_b", D), ("uv_b", D),
    ("q_scale", DEPTH * DHD), ("k_scale", DEPTH * DHD), ("ln_g", DEPTH * D), ("ln_b", DEPTH * D),
    ("b1", DEPTH * 2 * HID), ("b2", DEPTH * D),
]
AT, _n = {}, 0
for _name, _len in VECTORS:
    AT[_name] = (_n, _len)
    _n += _len
NVEC = _n


def build(nc, d, out):
    with ExitStack() as ctx:
        def sb(name, shape, dt=F32):
            return ctx.enter_context(nc.sbuf_tensor(name, shape, dt))

        class Semaphores(dict):
            def __missing__(self, name):
                self[name] = ctx.enter_context(nc.semaphore(name))
                return self[name]

        sem = Semaphores()
        count = {}

        def signal(ins, name, n=1):
            count[name] = count.get(name, 0) + n
            ins.then_inc(sem[name], n)
            return count[name]

        ps = ctx.enter_context(nc.psum_tensor("ps", [P, 8, 512], F32))
        ps16 = ps[:, :, :].bitcast(F16)
        psb16 = ps[:, :, :].bitcast(BF16)
        vec = sb("vec", [P, NVEC])
        x = sb("x_tok", [P, T, D])
        cst = sb("cst", [P, 2 * P + 256])
        ident = cst[:, 0:P]
        ident16 = sb("ident16", [P, P], F16)
        identb = sb("identb", [P, P], BF16)
        cmask = sb("cmask", [P, 2, P], BF16)
        dmask = sb("dmask", [P, 256], BF16)
        ones16 = sb("ones16", [P, P], F16)
        rope = sb("rope", [P, 4, TB, DHD])
        condT = sb("condT", [P, B])
        cond_b = sb("cond_b", [P, B, P])
        maskT = sb("maskT", [P, T])
        uT = sb("uT", [P, T * P])
        wide = {n: sb(n, [P, T, D]) for n in ("x1", "sq", "dev", "u")}
        staged = sb("staged", [P, 2, 1024], F16)
        o_tok = sb("o_tok", [P, T, D])
        small = {}

        def sm(name, n=T):
            if name not in small:
                small[name] = sb("s_" + name, [P, n])
            return small[name][:, :]

        arena = sb("arena", [P, 26624])
        used = [0]

        def carve(shape, dt=F32, start=None):
            n = int(np.prod(shape))
            words = n if dt == F32 else n // 2
            if start is not None:
                used[0] = start
            a = arena[:, used[0]:used[0] + words]
            used[0] += words
            assert used[0] <= 26624
            if dt != F32:
                a = a.bitcast(dt)
            names = "abcdef"[:len(shape)]
            if len(shape) > 1:
                a = a.rearrange(f"p ({' '.join(names)}) -> p {' '.join(names)}", **dict(zip(names, shape)))
            return a

        z = carve([T, 3 * D], start=0)
        zsq = carve([T, 3 * D])
        after_z = used[0]
        padq = carve([T, H * 32], F16)
        padk = carve([T, H * 32], F16)
        prob = carve([2, 2048])
        vA = carve([T, H, HD + 1])
        vB = carve([T, H, HQ + 1], F16)
        codes = carve([2, 4, 512], U16)
        codesT = carve([2, 4, 512], F16)
        outB = carve([T, H * (HQ + 1)])
        w_ada = carve([6 * D])
        w_qkv = carve([3 * D])
        w_o = carve([D])
        w_f1 = carve([FF])
        w_f2 = carve([FF // P, D])
        w_aq = carve([3 * D // 2])
        w_ap = carve([D])[0:D // 2, :]
        w_ca = carve([3 * D])
        w_cp = carve([D])
        w_img = carve([2 * D])
        ada = carve([B, 6 * D])
        img = carve([B, 2 * D])
        hid1 = carve([T, FF], start=0)
        hid1T = carve([4, T * P])
        padqC = carve([T, H * 64], BF16, start=after_z)
        padkC = carve([T, H * 64], BF16)
        probC = carve([2, 1280])
        vC = carve([T, H, HD + 1])
        outC = carve([TB, H, HD + 1])

        qkvD = carve([T, 3 * INNER], start=0)
        qTD = carve([INNER // P, T * P])
        kTD = carve([INNER // P, T * P])
        oD = carve([T, INNER])
        tmpD = oD.rearrange("p t c -> p (t c)")
        probD = carve([2, 2, 256])
        probTD = carve([2, 512])
        hidD = carve([T, 2 * HID], start=0)
        hgD = carve([T, HID])
        hidTD = carve([3, T * P], start=8192)
        w_d1 = sb("w_d1", [P, DEPTH, 3 * INNER])
        w_do = sb("w_do", [P, DEPTH, INNER // P, D])
        w_h1 = sb("w_h1", [P, DEPTH, 2 * HID])
        w_h2 = sb("w_h2", [P, DEPTH, 3, D])
        ropeL = sb("ropeL", [P, 4, TB, DHD])

        TURN = {n: i for i, n in enumerate(("a", "ao", "m", "b", "bo", "c", "co", "d0", "e0", "d1", "e1"))}
        PROJECTION = {n: i for i, n in enumerate(("a", "ao", "m", "f", "b", "bo", "c", "co"))}
        BLOCK = {"a": 0, "m": 1}

        def projected(p, t):
            return T * PROJECTION[p] + t + 1

        def v_(name):
            a, n = AT[name]
            return vec[:, a:a + n]

        def evacuate_qk(copy, i):
            which, pair, b = i // 8, i // 2 % 4, i % 2
            dst = (qTD, kTD)[which]
            return copy(dst[:, pair, b * 512:b * 512 + 512], ps[:, i % 6, :])

        def per_tile(a, n=T):
            return a.unsqueeze(1).to_broadcast([P, n, a.shape[1]])

        def per_row(a, k=D):
            return a.unsqueeze(2).to_broadcast([P, a.shape[1], k])

        block = ctx.enter_context(nc.Block())

        @block.sync
        def _(sp):
            def load(dst, src, name):
                sp.dma_start(dst, src).then_inc(sem[name], 16)
            load(x[:, :, :], d["x"].rearrange("b (t p) c -> p (b t) c", p=P), "x_in")
            load(condT[:, :], d["condT"], "ada_in")
            load(w_ada[:, :], d["w_ada"], "ada_in")
            load(cst[:, :], d["cst"], "cst_in")
            a = AT["qkv_alpha"][0]
            load(vec[:, 0:a], d["vec"][0, 0:a].partition_broadcast(P), "vec_in")
            load(w_qkv[:, :], d["w_qkv"], "w_in")
            load(w_o[:, :], d["w_o"], "w_in")
            load(w_f1[:, :], d["w_f1"], "w_in")
            load(w_f2[:, :, :], d["w_f2"].rearrange("(c p) n -> p c n", p=P), "w_in")
            load(vec[:, a:NVEC], d["vec"][0, a:NVEC].partition_broadcast(P), "vec2_in")
            load(w_aq[:, :], d["w_aqT"], "w2_in")
            load(w_ap[:, :], d["w_apT"], "w2_in")
            load(w_ca[:, :], d["w_ca"], "w2_in")
            load(w_cp[:, :], d["w_cp"], "w2_in")
            load(w_img[:, :], d["w_imgT"], "w2_in")
            load(maskT[:, :], d["maskT"], "w2_in")
            load(rope[:, :, :, :], d["rope"].rearrange("k (t p) c -> p k t c", p=P), "w2_in")
            for l in range(DEPTH):
                load(w_d1[:, l, :], d["wqkv"][l], "w3_in")
                load(w_do[:, l, :, :], d["wo"][l].rearrange("(c p) n -> p c n", p=P), "w3_in")
                load(w_h1[:, l, :], d["w1"][l], "w3_in")
                load(w_h2[:, l, 0:2, :], d["w2"][l, 0:2 * P].rearrange("(c p) n -> p c n", p=P), "w3_in")
                load(w_h2[0:HID - 2 * P, l, 2, :], d["w2"][l, 2 * P:HID], "w3_in")
            for k in range(2 * DEPTH):
                sp.wait_ge(sem["f_ready"], k + 1)
                h, f = wide["x1"], wide["u"]
                load(h[1:P, :, 64:D], f[0:P - 1, :, 64:D], "shifted")
                for b in range(B):
                    load(h[0:1, TB * b + 1:TB * b + TB, 64:D], f[P - 1:P, TB * b:TB * b + TB - 1, 64:D], "shifted")
            sp.wait_ge(sem["result"], 1)
            load(out.rearrange("b (t p) c -> p (b t) c", p=P), wide["dev"][:, :, :], "stored")
            sp.wait_ge(sem["stored"], 16)

        @block.gpsimd
        def _(pool):
            nc.gpsimd.memset(padq, 0.0).then_inc(sem["pads_clear"], 1)
            nc.gpsimd.memset(padk, 0.0).then_inc(sem["pads_clear"], 1)
            nc.gpsimd.memset(vA[:, :, :, HD:HD + 1], 1.0).then_inc(sem["vA_ones"], 1)
            nc.gpsimd.memset(vB[:, :, :, HQ:HQ + 1], 1.0).then_inc(sem["vB_ones"], 1)
            nc.gpsimd.memset(ones16[:, :], 1.0).then_inc(sem["ones16"], 1)
            nc.gpsimd.memset(codes.bitcast(U16), 0x6400).then_inc(sem["codes_high"], 1)
            pool.wait_ge(sem["projected"], projected("f", T - 1))
            nc.gpsimd.memset(padq, 0.0).then_inc(sem["pads_clear"], 1)
            nc.gpsimd.memset(padk, 0.0).then_inc(sem["pads_clear"], 1)
            pool.wait_ge(sem["codes_high"], 1)
            u8 = codes.bitcast(U8).rearrange("p n t (k c) -> p n t k c", c=2)
            for n in range(B * H):
                h = n % H
                pool.wait_ge(sem["rB"], n + 1)
                if n >= 2:
                    pool.wait_ge(sem["ptB"], 2 * (n - 1))
                for qt in range(4):
                    c = 4 * (n % 2) + qt
                    nc.gpsimd.tensor_scalar(u8[:, n % 2, qt, :, 0], prob[:, n % 2, qt * 512:qt * 512 + 512],
                                            sm("rB", 8)[:, c:c + 1], sm("zpu", H)[:, h:h + 1],
                                            ALU.mult, ALU.add).then_inc(sem["quantB"], 1)
            pool.wait_ge(sem["pvB"], B * (H + 1))
            nc.gpsimd.memset(padqC, 0.0).then_inc(sem["padsC_zero"], 1)
            nc.gpsimd.memset(padkC, 0.0).then_inc(sem["padsC_zero"], 1)
            nc.gpsimd.memset(vC[:, :, :, HD:HD + 1], 1.0).then_inc(sem["padsC_clear"], 1)
            pool.wait_ge(sem["padsC_zero"], 2)
            nc.gpsimd.memset(padqC.rearrange("p t (h s) -> p t h s", h=H)[:, :, :, 48:51], 1.0)\
                .then_inc(sem["padsC_clear"], 1)
            nc.gpsimd.memset(padkC.rearrange("p t (h s) -> p t h s", h=H)[:, :, :, 51:54], 1.0)\
                .then_inc(sem["padsC_clear"], 1)

        @block.scalar
        def _(act):
            def step(ins, name="act_step"):
                act.wait_ge(sem[name], signal(ins, name))

            def logmap_norm(p, src):
                nc.scalar.activation(wide["sq"][:, :, :], src, ACT.Square).then_inc(sem["squares"], 1)
                act.wait_ge(sem["n2"], BLOCK[p] + 1)
                nc.scalar.activation(sm("n"), sm(p + "n2"), ACT.Sqrt).then_inc(sem["n"], 1)
                act.wait_ge(sem["dev"], BLOCK[p] + 1)
                nc.scalar.activation(wide["sq"][:, :, :], wide["dev"][:, :, :], ACT.Square).then_inc(sem["squares"], 1)
                act.wait_ge(sem["ratio"], BLOCK[p] + 1)
                nc.scalar.activation(sm("ln"), sm("ratio"), ACT.Ln).then_inc(sem["ln"], 1)
                act.wait_ge(sem["var"], BLOCK[p] + 1)
                nc.scalar.activation(sm("std"), sm("var"), ACT.Sqrt).then_inc(sem["std"], 1)
                act.wait_ge(sem["u"], BLOCK[p] + 1)
                nc.scalar.activation(wide["sq"][:, :, :], wide["u"][:, :, :], ACT.Square).then_inc(sem["squares"], 1)
                act.wait_ge(sem["u2"], BLOCK[p] + 1)
                nc.scalar.activation(sm("un"), sm("u2"), ACT.Sqrt).then_inc(sem["un"], 1)

            def copy_T(p, dst=None, rows=P, n=1, k=0):
                for half in range(2):
                    act.wait_ge(sem["turned"], 2 * TURN[p] + half + 1)
                    to = (uT[0:rows, half * 512:half * 512 + 512] if dst is None
                          else dst[0:rows, half * 512:half * 512 + 512])
                    nc.scalar.activation(to, ps[0:rows, 6 + half, :], ACT.Copy).then_inc(sem["turned_copied"], 1)

            def mobius(p):
                act.wait_ge(sem["z2"], BLOCK[p] + 1)
                nc.scalar.activation(sm("zn"), sm("z2"), ACT.Sqrt).then_inc(sem["zn"], 1)
                act.wait_ge(sem["w"], BLOCK[p] + 1)
                nc.scalar.activation(wide["sq"][:, :, :], wide["dev"][:, :, :], ACT.Square).then_inc(sem["wsq"], 1)
                act.wait_ge(sem["w2"], BLOCK[p] + 1)
                nc.scalar.activation(sm("wn"), sm("w2"), ACT.Sqrt).then_inc(sem["wn"], 1)
                act.wait_ge(sem["wc"], BLOCK[p] + 1)
                nc.scalar.activation(sm("th"), sm("wc"), ACT.Tanh).then_inc(sem["th"], 1)

            act.wait_ge(sem["x_in"], 16)
            logmap_norm("a", x[:, :, :])
            copy_T("a")
            act.wait_ge(sem["zA"], 1)
            nc.scalar.activation(zsq, z, ACT.Square).then_inc(sem["zsqA"], 1)
            act.wait_ge(sem["z2A"], 1)
            nc.scalar.activation(sm("hn", 3 * T * H), sm("h2", 3 * T * H), ACT.Sqrt).then_inc(sem["hnA"], 1)
            nc.scalar.activation(sm("rn", 3 * T), sm("r2", 3 * T), ACT.Sqrt).then_inc(sem["hnA"], 1)
            for n in range(B * H):
                for half in range(2):
                    act.wait_ge(sem["stA"], 2 * n + half + 1)
                    if n >= 2:
                        act.wait_ge(sem["pvA"], n - 1)
                    nc.scalar.activation(prob[:, n % 2, half * 1024:half * 1024 + 1024],
                                         ps[:, 2 * half:2 * half + 2, :], ACT.Exp,
                                         scale=HD ** -0.5).then_inc(sem["expA"], 1)
            copy_T("ao")
            mobius("a")
            act.wait_ge(sem["x1"], 1)
            logmap_norm("m", wide["x1"][:, :, :])
            copy_T("m")
            act.wait_ge(sem["h1"], 1)
            for t in range(T):
                if t >= 2:
                    act.wait_ge(sem["f2"], t - 1)
                nc.scalar.activation(ps[:, 6 + t % 2, :], hid1[:, t, :], ACT.Square,
                                     accum_out=sm("f2")[:, t:t + 1]).then_inc(sem["f2"], 1)
            act.wait_ge(sem["f2"], T)
            nc.scalar.activation(sm("fn"), sm("f2"), ACT.Sqrt).then_inc(sem["fn"], 1)
            for g in range(8):
                act.wait_ge(sem["h1_T"], g + 1)
                nc.scalar.activation(hid1T[:, g % 4, (g // 4) * 512:(g // 4) * 512 + 512],
                                     ps[:, g % 6, :], ACT.Copy).then_inc(sem["h1_uT"], 1)
            mobius("m")
            copy_T("b")
            for n in range(B * H):
                h = n % H
                for qt in range(4):
                    if qt % 2 == 0:
                        act.wait_ge(sem["maxB"], 2 * n + qt // 2 + 1)
                    if n >= 2 and qt == 0:
                        act.wait_ge(sem["quantB"], 4 * (n - 1))
                    ins = nc.scalar.activation(prob[:, n % 2, qt * 512:qt * 512 + 512], ps[:, qt, :], ACT.Exp,
                                               scale=sm("scB", H)[:, h:h + 1],
                                               bias=sm("nbB", 8)[:, 4 * (n % 2) + qt:4 * (n % 2) + qt + 1],
                                               accum_out=sm("sumB", 8)[:, 4 * (n % 2) + qt:4 * (n % 2) + qt + 1])
                    ins.then_inc(sem["expB"], 1)
            copy_T("bo", rows=D // 2)
            copy_T("c")
            act.wait_ge(sem["imx"], 1)
            nc.scalar.activation(sm("eimg", T * H), sm("simg", T * H), ACT.Exp).then_inc(sem["eimg"], 1)
            for n in range(B * H):
                act.wait_ge(sem["stC"], n + 1)
                if n >= 2:
                    act.wait_ge(sem["pvC"], n - 1)
                nc.scalar.activation(probC[:, n % 2, :],
                                     ps[:, 3 * (n % 2):3 * (n % 2) + 3, :].rearrange("p a b -> p (a b)")[:, 0:1280],
                                     ACT.Exp).then_inc(sem["expC"], 1)
            copy_T("co")
            for l in range(DEPTH):
                copy_T(f"d{l}")
                for t in range(T):
                    act.wait_ge(sem["d_mm"], T * l + t + 1)
                    k = 3 * (t % 2)
                    nc.scalar.activation(qkvD[:, t, :], ps[:, k:k + 3, :].rearrange("p a b -> p (a b)"), ACT.Copy)\
                        .then_inc(sem["d_ev"], 1)
                act.wait_ge(sem["d_ev"], T * (l + 1))
                for b in range(B):
                    if b:
                        act.wait_ge(sem["ropeD"], 2 * B * l + 2 * b)
                    nc.scalar.activation(tmpD.rearrange("p (t c) -> p t c", t=TB), qkvD[:, TB * b:TB * b + TB, 0:1024],
                                         ACT.Square).then_inc(sem["d_sq"], 1)
                    act.wait_ge(sem["d_ss"], B * l + b + 1)
                    nc.scalar.activation(sm("dn", 64), sm("dss", 64), ACT.Sqrt).then_inc(sem["d_n"], 1)
                for i in range(8):
                    act.wait_ge(sem["qkT_D"], 16 * l + 2 * i + 1)
                    evacuate_qk(lambda o, a: nc.scalar.activation(o, a, ACT.Copy), 2 * i).then_inc(sem["qk_evA"], 1)
                for u in range(T * 4):
                    U = T * 4 * l + u
                    t, pair = divmod(u, 4)
                    first = t % TB == 0
                    act.wait_ge(sem["maxD"], U + 1)
                    if U >= 2:
                        act.wait_ge(sem["ptD"], U - 1)
                    for j in range(2):
                        c = 8 * (t % 2) + 2 * pair + j
                        k0 = P if first else 0
                        ins = nc.scalar.activation(probD[:, u % 2, j, k0:256], ps[:, 6 * (u % 2) + j, k0:256],
                                                   ACT.Exp, scale=8.0, bias=sm("nbD", 4)[:, 2 * (u % 2) + j:2 * (u % 2) + j + 1],
                                                   accum_out=sm("sumD", 16)[:, c:c + 1])
                        ins.then_inc(sem["expD"], 1)
                for g in range(8):
                    act.wait_ge(sem["o_T"], 8 * l + g + 1)
                    nc.scalar.activation(qTD[:, g % 4, (g // 4) * 512:(g // 4) * 512 + 512], ps[:, g % 6, :],
                                         ACT.Copy).then_inc(sem["o_uT"], 1)
                act.wait_ge(sem["devD"], l + 1)
                nc.scalar.activation(wide["sq"][:, :, :], wide["dev"][:, :, :], ACT.Square).then_inc(sem["lnsq"], 1)
                act.wait_ge(sem["lnvar"], l + 1)
                nc.scalar.activation(sm("std"), sm("var"), ACT.Sqrt).then_inc(sem["lnstd"], 1)
                copy_T(f"e{l}")
                for t in range(T):
                    act.wait_ge(sem["e_ev"], T * l + t + 1)
                    nc.scalar.activation(hidD[:, t, HID:2 * HID], hidD[:, t, HID:2 * HID], ACT.Gelu)\
                        .then_inc(sem["gelu"], 1)
                for g in range(6):
                    rows = P if g % 3 < 2 else HID - 2 * P
                    act.wait_ge(sem["g_T"], 6 * l + g + 1)
                    nc.scalar.activation(hidTD[0:rows, g % 3, (g // 3) * 512:(g // 3) * 512 + 512], ps[0:rows, g, :],
                                         ACT.Copy).then_inc(sem["g_uT"], 1)

        @block.vector
        def _(dve):
            V = nc.vector

            def step(ins, name="dve_step"):
                dve.wait_ge(sem[name], signal(ins, name))

            def mul(o, a, b, name="dve_step"):
                step(V.tensor_tensor(o, a, b, ALU.mult), name)

            def add(o, a, b, name="dve_step"):
                step(V.tensor_tensor(o, a, b, ALU.add), name)

            def ts(o, a, s1, op1, s2=None, op2=None, name="dve_step"):
                if op2 is None:
                    step(V.tensor_scalar(o, a, s1, None, op1), name)
                else:
                    step(V.tensor_scalar(o, a, s1, s2, op1, op2), name)

            def stt(o, a, s1, b, op1, op2, name="dve_step"):
                step(V.scalar_tensor_tensor(out=o, in0=a, scalar=s1, in1=b, op0=op1, op1=op2), name)

            def total(o, a, name="dve_step"):
                step(V.tensor_reduce(o, a, X, ALU.add), name)

            def recip(o, a, name="dve_step"):
                step(V.reciprocal(o, a), name)

            def shrink(o, norm, name="dve_step"):
                ts(o, norm, EPS, ALU.max)
                recip(o, o)
                ts(o, o, REACH, ALU.mult, 1.0, ALU.min, name)

            def logmap_norm(p, src, sc, sh):
                total(sm("s1"), src)
                ts(sm("s1"), sm("s1"), 1.0 / D, ALU.mult)
                dve.wait_ge(sem["squares"], 3 * BLOCK[p] + 1)
                total(sm(p + "n2"), wide["sq"][:, :, :], "n2")
                step(V.tensor_tensor(wide["dev"][:, :, :], src, per_row(sm("s1")), ALU.subtract), "dev")
                dve.wait_ge(sem["n"], BLOCK[p] + 1)
                ts(sm("nf"), sm("n"), EPS, ALU.max)
                ts(sm("nc"), sm("nf"), MAX_TANH, ALU.min)
                ts(sm("ratio"), sm("nc"), -1.0, ALU.mult, 1.0, ALU.add)
                recip(sm("ratio"), sm("ratio"))
                stt(sm("ratio"), sm("nc"), 1.0, sm("ratio"), ALU.add, ALU.mult, "ratio")
                mul(sm("t"), sm("nc"), sm("nc"))
                ts(sm("poly"), sm("t"), 1.0 / 13, ALU.mult)
                for k in (11, 9, 7, 5, 3):
                    stt(sm("poly"), sm("poly"), 1.0 / k, sm("t"), ALU.add, ALU.mult)
                stt(sm("poly"), sm("poly"), 1.0, sm("nc"), ALU.add, ALU.mult)
                ts(sm("pick"), sm("nc"), SERIES_BELOW, ALU.is_lt)
                dve.wait_ge(sem["ln"], BLOCK[p] + 1)
                stt(sm("poly"), sm("ln"), -0.5, sm("poly"), ALU.mult, ALU.add)
                mul(sm("poly"), sm("poly"), sm("pick"))
                stt(sm("fac"), sm("ln"), 0.5, sm("poly"), ALU.mult, ALU.add)
                recip(sm("nf"), sm("nf"))
                mul(sm("fac"), sm("fac"), sm("nf"))
                dve.wait_ge(sem["squares"], 3 * BLOCK[p] + 2)
                total(sm("var"), wide["sq"][:, :, :])
                mul(sm("t"), sm("fac"), sm("fac"))
                stt(sm("var"), sm("var"), 1.0 / D, sm("t"), ALU.mult, ALU.mult)
                ts(sm("var"), sm("var"), 1e-6, ALU.add, name="var")
                dve.wait_ge(sem["std"], BLOCK[p] + 1)
                recip(sm("std"), sm("std"))
                mul(sm("std"), sm("std"), sm("fac"))
                u = wide["u"][:, :, :]
                mul(u, wide["dev"][:, :, :], per_row(sm("std")))
                for b in range(B):
                    ub = u[:, TB * b:TB * b + TB, :]
                    mul(ub, ub, per_tile(ada[:, b, sc:sc + D], TB))
                for b in range(B):
                    ub = u[:, TB * b:TB * b + TB, :]
                    ins = V.tensor_tensor(ub, ub, per_tile(ada[:, b, sh:sh + D], TB), ALU.add)
                    if b == B - 1:
                        step(ins, "u")
                    else:
                        step(ins)
                dve.wait_ge(sem["squares"], 3 * BLOCK[p] + 3)
                total(sm("u2"), wide["sq"][:, :, :], "u2")
                dve.wait_ge(sem["un"], BLOCK[p] + 1)
                shrink(sm("us"), sm("un"))

            def mobius(p, src, gate, zin, dst, name):
                dev, sq = wide["dev"][:, :, :], wide["sq"][:, :, :]
                mul(sq, zin, zin)
                total(sm("z2"), sq, "z2")
                dve.wait_ge(sem["zn"], BLOCK[p] + 1)
                shrink(sm("zs"), sm("zn"))
                mul(dev, zin, per_row(sm("zs")))
                for b in range(B):
                    db = dev[:, TB * b:TB * b + TB, :]
                    ins = V.tensor_tensor(db, db, per_tile(ada[:, b, gate:gate + D], TB), ALU.mult)
                    step(ins, "w" if b == B - 1 else "dve_step")
                dve.wait_ge(sem["wsq"], BLOCK[p] + 1)
                total(sm("w2"), sq, "w2")
                mul(sq, src, dev)
                total(sm("xy"), sq)
                dve.wait_ge(sem["wn"], BLOCK[p] + 1)
                ts(sm("wc"), sm("wn"), EPS, ALU.max, name="wc")
                recip(sm("t"), sm("wc"))
                dve.wait_ge(sem["th"], BLOCK[p] + 1)
                mul(sm("tr"), sm("th"), sm("t"))
                mul(sm("xy"), sm("xy"), sm("tr"))
                mul(sm("y2"), sm("tr"), sm("tr"))
                mul(sm("y2"), sm("y2"), sm("w2"))
                x2 = sm(p + "n2")
                ts(sm("xy"), sm("xy"), 2.0, ALU.mult, 1.0, ALU.add)
                mul(sm("t"), x2, sm("y2"))
                add(sm("t"), sm("t"), sm("xy"))
                ts(sm("t"), sm("t"), EPS, ALU.max)
                recip(sm("t"), sm("t"))
                add(sm("xy"), sm("xy"), sm("y2"))
                mul(sm("xy"), sm("xy"), sm("t"))
                ts(sm("y2"), x2, -1.0, ALU.mult, 1.0, ALU.add)
                mul(sm("y2"), sm("y2"), sm("tr"))
                mul(sm("y2"), sm("y2"), sm("t"))
                mul(dev, dev, per_row(sm("y2")))
                mul(sq, src, per_row(sm("xy")))
                add(dst, sq, dev, name)

            def norm_o(l, t):
                dve.wait_ge(sem["pvD"], T * 4 * l + 4 * t + 4)
                rs = sm("rsumD", 8)
                recip(rs, sm("sumD", 16)[:, 8 * (t % 2):8 * (t % 2) + 8])
                mul(oD[:, t, :].rearrange("p (h c) -> p h c", h=DH), ps[:, 4 + t % 2, :].rearrange("p (h c) -> p h c", h=DH),
                    per_row(rs, DHD), "o_D")

            dve.wait_ge(sem["cst_in"], 16)
            step(V.tensor_copy(ident16[:, :], ident), "idents")
            step(V.tensor_copy(identb[:, :], ident), "idents")
            dve.wait_ge(sem["ada_in"], 32)
            for b in range(B):
                step(V.tensor_copy(cond_b[:, b, :], condT[:, b:b + 1].to_broadcast([P, P])), "cond_b")
            step(V.tensor_copy(cmask[:, 0, :], cst[:, P:2 * P]))
            dve.wait_ge(sem["cmT"], 1)
            step(V.tensor_copy(cmask[:, 1, :], ps[:, 4, 0:P]), "cmask")
            step(V.tensor_copy(dmask[:, :], cst[:, 2 * P:2 * P + 256]), "dmask")
            dve.wait_ge(sem["vec_in"], 16)
            for b in range(B):
                dve.wait_ge(sem["adaP"], b + 1)
                add(ada[:, b, 0:512], ps[:, 2 * b, :], v_("b_ada")[:, 0:512])
                add(ada[:, b, 512:768], ps[:, 2 * b + 1, 0:256], v_("b_ada")[:, 512:768])
            ts(ada[:, :, D:2 * D], ada[:, :, D:2 * D], 1.0, ALU.add)
            ts(ada[:, :, 4 * D:5 * D], ada[:, :, 4 * D:5 * D], 1.0, ALU.add)
            dve.wait_ge(sem["x_in"], 16)
            logmap_norm("a", x[:, :, :], D, 0)
            for t in range(T):
                dve.wait_ge(sem["projected"], projected("a", t))
                stt(z[:, t, :], ps[:, t % 6, 0:3 * D], sm("us")[:, t:t + 1], v_("b_qkv"), ALU.mult, ALU.add, "taken")
            signal_only = V.tensor_copy(sm("t"), sm("us"))
            step(signal_only, "zA")
            dve.wait_ge(sem["zsqA"], 1)
            total(sm("h2", 3 * T * H), zsq.rearrange("p t (h e) -> p (t h) e", e=HD))
            total(sm("r2", 3 * T), sm("h2", 3 * T * H).rearrange("p (r h) -> p r h", h=H), "z2A")
            dve.wait_ge(sem["hnA"], 2)
            shrink(sm("rs", 3 * T), sm("rn", 3 * T))
            ts(sm("rs", 3 * T), sm("rs", 3 * T), HEAD_SCALE, ALU.mult)
            hf = sm("hf", 3 * T * H)
            hn3 = sm("hn", 3 * T * H).rearrange("p (r h) -> p r h", h=H)
            hf3 = hf.rearrange("p (r h) -> p r h", h=H)
            mul(hf3, hn3, per_row(sm("rs", 3 * T), H))
            shrink(hf, hf)
            mul(hf3, hf3, per_row(sm("rs", 3 * T), H))
            mul(z.rearrange("p t (h e) -> p (t h) e", e=HD), z.rearrange("p t (h e) -> p (t h) e", e=HD),
                per_row(hf, HD))
            qz = z[:, :, 0:D].rearrange("p t (h e) -> p t h e", e=HD)
            kz = z[:, :, D:2 * D].rearrange("p t (h e) -> p t h e", e=HD)
            pq = padq.rearrange("p t (h s e) -> p t h s e", s=4, e=HD)
            pk = padk.rearrange("p t (h s e) -> p t h s e", s=4, e=HD)
            dve.wait_ge(sem["pads_clear"], 2)
            for src, pad, hi, lo in ((qz, pq, (0, 1), (2, 3)), (kz, pk, (0, 2), (1, 3))):
                step(V.tensor_copy(pad[:, :, :, hi[0], :], src))
                step(V.tensor_copy(pad[:, :, :, hi[1], :], src))
                step(V.tensor_tensor(pad[:, :, :, lo[0], :], src, pad[:, :, :, hi[0], :], ALU.subtract))
                step(V.tensor_copy(pad[:, :, :, lo[1], :], pad[:, :, :, lo[0], :]))
            dve.wait_ge(sem["vA_ones"], 1)
            step(V.tensor_copy(vA[:, :, :, 0:HD], z[:, :, 2 * D:3 * D].rearrange("p t (h e) -> p t h e", e=HD)), "padsA")

            for G in range(B * 4 + 1):
                if G < B * 4:
                    dve.wait_ge(sem["tA"], G + 1)
                    step(V.tensor_copy(staged[:, G % 2, :], ps16[:, 6 + G % 2, 0:1024]), "stagedA")
                if G >= 1:
                    b, g = divmod(G - 1, 4)
                    dve.wait_ge(sem["pvA"], 4 * G)
                    o = ps[:, 4 + (G - 1) % 2, 0:4 * 4 * (HD + 1)].rearrange("p (t h e) -> p t h e", t=TB, h=4)
                    rs = sm("rsumA", 16).rearrange("p (t h) -> p t h", h=4)
                    recip(rs, o[:, :, :, HD])
                    mul(o_tok[:, TB * b:TB * b + TB, 32 * g:32 * g + 32].rearrange("p t (h e) -> p t h e", h=4),
                        o[:, :, :, 0:HD], rs.unsqueeze(3).to_broadcast([P, TB, 4, HD]), "oA")
            for t in range(T):
                dve.wait_ge(sem["projected"], projected("ao", t))
                stt(z[:, t, 0:D], ps[:, t % 6, 0:D], 1.0 / HEAD_SCALE, v_("b_o"), ALU.mult, ALU.add, "taken")
            mobius("a", x[:, :, :], 2 * D, z[:, :, 0:D], wide["x1"][:, :, :], "x1")
            logmap_norm("m", wide["x1"][:, :, :], 4 * D, 3 * D)
            for t in range(T):
                dve.wait_ge(sem["projected"], projected("m", t))
                stt(hid1[:, t, :], ps[:, t % 6, :], sm("us")[:, t:t + 1], v_("b_f1"), ALU.mult, ALU.add, "taken")
            step(V.tensor_copy(sm("t"), sm("us")), "h1")
            dve.wait_ge(sem["fn"], 1)
            shrink(sm("fs"), sm("fn"))
            z2 = arena[:, 0:T * D].rearrange("p (t c) -> p t c", t=T)
            for t in range(T):
                dve.wait_ge(sem["projected"], projected("f", t))
                stt(z2[:, t, :], ps[:, t % 6, 0:D], sm("fs")[:, t:t + 1], v_("b_f2"), ALU.mult, ALU.add, "taken")
            mobius("m", wide["x1"][:, :, :], 5 * D, z2, wide["u"][:, :, :], "y")

            dve.wait_ge(sem["vec2_in"], 16)
            dve.wait_ge(sem["w2_in"], 16 * 7)
            for w, al, rows, n in ((w_aq, "qkv_alpha", P, 192), (w_ap, "proj_alpha", 64, D)):
                r = wide["sq"][0:rows, 0:2, :].rearrange("p a b -> p (a b)")[:, 0:n]
                recip(r, v_(al)[0:rows, :])
                mul(w[:, :], w[:, :], r)
                ts(w[:, :], w[:, :], -8.0, ALU.max, 7.0, ALU.min)
                ts(w[:, :], w[:, :], ROUND, ALU.add, ROUND, ALU.subtract)
                mul(w[:, :], w[:, :], v_(al)[0:rows, :], "w_quant")
            for name in ("q_zp", "k_zp", "v_zp", "attn_zp"):
                ts(v_(name), v_(name), ROUND, ALU.add, ROUND, ALU.subtract)
            zb = z[:, :, 0:192]
            for t in range(T):
                dve.wait_ge(sem["projected"], projected("b", t))
                step(V.tensor_copy(z[:, t, 0:192], ps[:, t % 6, 0:192]), "taken")
            for i, (al, zp, bias) in enumerate((("q_alpha", "q_zp", "bias_q"), ("k_alpha", "k_zp", "bias_k"),
                                                ("v_alpha", "v_zp", None))):
                zi = z[:, :, 64 * i:64 * i + 64].rearrange("p t (h e) -> p t h e", e=HQ)

                def by_head(a):
                    return a.unsqueeze(1).unsqueeze(3).to_broadcast([P, T, H, HQ])
                if bias is not None:
                    add(zi, zi, by_head(v_(bias)))
                recip(sm("ia", H), v_(al))
                mul(zi, zi, by_head(sm("ia", H)))
                add(zi, zi, by_head(v_(zp)))
                ts(zi, zi, -8.0, ALU.max, 7.0, ALU.min)
                ts(zi, zi, ROUND, ALU.add, ROUND, ALU.subtract)
            zi = z[:, :, 0:64].rearrange("p t (h e) -> p t h e", e=HQ)
            step(V.tensor_tensor(zi, zi, v_("q_zp").unsqueeze(1).unsqueeze(3).to_broadcast([P, T, H, HQ]), ALU.subtract))
            pq = padq.rearrange("p t (h s e) -> p t h s e", s=8, e=HQ)
            pk = padk.rearrange("p t (h s e) -> p t h s e", s=8, e=HQ)
            kz = z[:, :, 64:128].rearrange("p t (h e) -> p t h e", e=HQ)
            dve.wait_ge(sem["pads_clear"], 4)
            step(V.tensor_copy(pq[:, :, :, 0, :], zi))
            step(V.tensor_tensor(pq[:, :, :, 1, :], zi, pq[:, :, :, 0, :], ALU.subtract))
            step(V.tensor_copy(pk[:, :, :, 0, :], kz))
            step(V.tensor_copy(pk[:, :, :, 1, :], kz))
            dve.wait_ge(sem["vB_ones"], 1)
            step(V.tensor_copy(vB[:, :, :, 0:HQ], z[:, :, 128:192].rearrange("p t (h e) -> p t h e", e=HQ)))
            mul(sm("scB", H), v_("q_alpha"), v_("k_alpha"))
            ts(sm("scB", H), sm("scB", H), HQ ** -0.5, ALU.mult)
            ts(sm("zpa", H), v_("attn_zp"), U_ZERO, ALU.add)
            ts(sm("zpu", H), v_("attn_zp"), 128.0, ALU.add, name="padsB")
            for b in range(B):
                for n_ in range(H + 2):
                    n = b * H + n_
                    if n_ < H:
                        h = n_
                        if h % 4 == 0:
                            dve.wait_ge(sem["tB"], n // 4 + 1)
                            step(V.tensor_copy(staged[:, (h // 4) % 2, :], ps16[:, 7, 0:1024]), "stagedB")
                        for half in range(2):
                            dve.wait_ge(sem["stB"], 2 * n + half + 1)
                            c = 4 * (n % 2) + 2 * half
                            if n >= 2:
                                dve.wait_ge(sem["expB"], 4 * (n - 1))
                            step(V.tensor_reduce(sm("nmB", 8)[:, c:c + 2], ps[:, 2 * half:2 * half + 2, :], X, ALU.max,
                                                 negate=True))
                            ts(sm("nbB", 8)[:, c:c + 2], sm("nmB", 8)[:, c:c + 2], sm("scB", H)[:, h:h + 1], ALU.mult,
                               name="maxB")
                    if 1 <= n_ <= H:
                        h, m = n_ - 1, n - 1
                        dve.wait_ge(sem["expB"], 4 * m + 4)
                        if m >= 2:
                            dve.wait_ge(sem["quantB"], 4 * (m - 1))
                        c = 4 * (m % 2)
                        ts(sm("rB", 8)[:, c:c + 4], sm("sumB", 8)[:, c:c + 4], v_("attn_alpha")[:, h:h + 1], ALU.mult)
                        recip(sm("rB", 8)[:, c:c + 4], sm("rB", 8)[:, c:c + 4], "rB")
                    if n_ >= 2:
                        m = n - 2
                        for half in range(2):
                            dve.wait_ge(sem["ptB"], 2 * m + half + 1)
                            step(V.tensor_copy(codesT[:, m % 2, 2 * half:2 * half + 2, :],
                                               ps16[:, 4 + half, 0:1024].rearrange("p (a b) -> p a b", a=2)), "ptcB")
                dve.wait_ge(sem["pvB"], H * (b + 1) + b + 1)
                ob = outB[:, TB * b:TB * b + TB, :]
                cs = sm("colsum", H * (HQ + 1))
                step(V.tensor_copy(cs, ps[:, 6, 320:320 + H * (HQ + 1)]))
                c3 = cs.rearrange("p (h e) -> p h e", h=H)
                mul(c3, c3, sm("zpa", H).unsqueeze(2).to_broadcast([P, H, HQ + 1]))
                step(V.tensor_tensor(ob, ps[:, 6, 0:320].rearrange("p (t c) -> p t c", t=TB),
                                     cs.unsqueeze(1).to_broadcast([P, TB, H * (HQ + 1)]), ALU.subtract), "outB")
            o4 = outB.rearrange("p t (h e) -> p t h e", h=H)
            mul(sm("fa", H), v_("attn_alpha"), v_("v_alpha"))
            ob = z[:, :, 0:64].rearrange("p t (h e) -> p t h e", e=HQ)
            one = sm("one", T * H).rearrange("p (t h) -> p t h", h=H)
            mul(one, o4[:, :, :, HQ], v_("v_zp").unsqueeze(1).to_broadcast([P, T, H]))
            step(V.tensor_tensor(ob, o4[:, :, :, 0:HQ], one.unsqueeze(3).to_broadcast([P, T, H, HQ]), ALU.subtract))
            mul(ob, ob, sm("fa", H).unsqueeze(1).unsqueeze(3).to_broadcast([P, T, H, HQ]), "zB")
            for t in range(T):
                dve.wait_ge(sem["projected"], projected("bo", t))
                add(x[:, t, :], x[:, t, :], ps[:, t % 6, 0:D], "taken")
            add(x[:, :, :], x[:, :, :], per_tile(v_("proj_b")), "x2")

            for b in range(B):
                dve.wait_ge(sem["imgP"], b + 1)
                add(img[:, b, 0:D], ps[:, b, 0:D], v_("uk_b"))
                add(img[:, b, D:2 * D], ps[:, b, D:2 * D], v_("uv_b"), "img")
            for t in range(T):
                dve.wait_ge(sem["projected"], projected("c", t))
                add(z[:, t, :], ps[:, t % 6, 0:3 * D], v_("c_attn_b"), "taken")
            ts(z[:, :, 0:D], z[:, :, 0:D], HD ** -0.5, ALU.mult)
            for b in range(B):
                mul(zsq[:, TB * b:TB * b + TB, 0:D], z[:, TB * b:TB * b + TB, 0:D], per_tile(img[:, b, 0:D], TB))
            simg = sm("simg", T * H)
            s3 = simg.rearrange("p (t h) -> p t h", h=H)
            total(s3, zsq[:, :, 0:D].rearrange("p t (h e) -> p t h e", e=HD))
            pq = padqC.rearrange("p t (h s) -> p t h s", h=H)
            pk = padkC.rearrange("p t (h s) -> p t h s", h=H)

            def split(src, pad, places, e):
                left = zsq[:, :, 0:H * e].rearrange("p t (h e) -> p t h e", e=e)
                now = src
                for i, slots in enumerate(places):
                    for k in slots:
                        step(V.tensor_copy(pad[:, :, :, k:k + e], now))
                    if i + 1 < len(places):
                        k = slots[0]
                        step(V.tensor_tensor(left, now, pad[:, :, :, k:k + e], ALU.subtract))
                        now = left
            dve.wait_ge(sem["padsC_clear"], 3)
            split(z[:, :, 0:D].rearrange("p t (h e) -> p t h e", e=HD), pq, ((0, 8, 16), (24, 32), (40,)), HD)
            split(z[:, :, D:2 * D].rearrange("p t (h e) -> p t h e", e=HD), pk, ((0, 24, 40), (8, 32), (16,)), HD)
            split(maskT[:, :].unsqueeze(2).unsqueeze(3).to_broadcast([P, T, H, 1]), pk, ((48,), (49,), (50,)), 1)
            step(V.tensor_copy(vC[:, :, :, 0:HD], z[:, :, 2 * D:3 * D].rearrange("p t (h e) -> p t h e", e=HD)), "padsC")
            nmx = sm("nmx", T * H).rearrange("p (t h) -> p t h", h=H)
            PLACE = {3: (0, 0), 2: (1, 0), 0: (1, 384), 1: (2, 0)}
            for b in range(B):
                for h in range(H):
                    n = b * H + h
                    if h % 2 == 0:
                        dve.wait_ge(sem["tC"], n // 2 + 1)
                        step(V.tensor_copy(staged[:, (n // 2) % 2, :], ps16[:, 6 + (n // 2) % 2, 0:1024]), "stagedC")
                    dve.wait_ge(sem["sC"], n + 1)
                    for qt in range(4):
                        bank, col = PLACE[qt]
                        ins = V.tensor_reduce(nmx[:, TB * b + qt, h:h + 1],
                                              ps[:, 3 * (n % 2) + bank, col:col + P * (qt + 1)], X, ALU.max, negate=True)
                        if qt == 3:
                            step(ins, "maxC")
            nm = sm("nmx", T * H)
            ts(sm("one", T * H), simg, -1.0, ALU.mult)
            step(V.tensor_tensor(nm, nm, sm("one", T * H), ALU.min))
            add(simg, simg, nm, "imx")
            split(nmx.unsqueeze(3), pq, ((51,), (52,), (53,)), 1)
            ts(sm("one", T * H), nm, 1.0, ALU.mult, name="mC")
            for n in range(B * H + 1):
                if n % 2 == 0 and n < B * H:
                    dve.wait_ge(sem["t2C"], n // 2 + 1)
                    step(V.tensor_copy(staged[:, (n // 2) % 2, :], ps16[:, 7, 0:1024]), "staged2C")
                if n % 8 == 0 and n:
                    half = n // 8 % 2 ^ 1
                    dve.wait_ge(sem["pvC"], n)
                    step(V.tensor_copy(outC[:, :, 8 * half:8 * half + 8, :],
                                       ps[:, 6, 0:288].rearrange("p (t h e) -> p t h e", t=TB, h=8)), "oC")
                if n % H == 0 and n:
                    b = n // H - 1
                    dve.wait_ge(sem["eimg"], 1)
                    e3 = sm("eimg", T * H).rearrange("p (t h) -> p t h", h=H)[:, TB * b:TB * b + TB, :]
                    add(outC[:, :, :, HD], outC[:, :, :, HD], e3)
                    recip(outC[:, :, :, HD], outC[:, :, :, HD])
                    ob = o_tok[:, TB * b:TB * b + TB, :].rearrange("p t (h e) -> p t h e", e=HD)
                    for tt in range(TB):
                        mul(ob[:, tt], img[:, b, D:2 * D].rearrange("p (h e) -> p h e", e=HD), per_row(e3[:, tt, :], HD))
                    add(ob, ob, outC[:, :, :, 0:HD])
                    mul(ob, ob, outC[:, :, :, HD].unsqueeze(3).to_broadcast([P, TB, H, HD]), "ocn")
            for t in range(T):
                dve.wait_ge(sem["projected"], projected("co", t))
                add(wide["u"][:, t, :], ps[:, t % 6, 0:D], v_("c_proj_b"), "taken")
            f, h = wide["u"], wide["x1"]
            step(V.memset(h[0:1, 0:T:TB, 64:D], 0.0))
            step(V.tensor_copy(h[:, :, 0:64], f[:, :, 0:64]), "f_ready")
            for l in range(DEPTH):
                for i, name in ((0, "q_scale"), (2, "k_scale")):
                    s_ = v_(name)[:, l * DHD:(l + 1) * DHD]
                    mul(ropeL[:, i], rope[:, i], per_tile(s_, TB))
                    for a in range(2):
                        mul(ropeL[:, i + 1, :, 32 * a:32 * a + 32], rope[:, i + 1, :, 32 * a:32 * a + 32],
                            per_tile(s_[:, 32 - 32 * a:64 - 32 * a], TB))
                for b in range(B):
                    dve.wait_ge(sem["d_sq"], B * l + b + 1)
                    total(sm("dss", 64), tmpD.rearrange("p (n c) -> p n c", c=DHD), "d_ss")
                    dve.wait_ge(sem["d_n"], B * l + b + 1)
                    dn = sm("dn", 64)
                    ts(dn, dn, 1e-12, ALU.max)
                    recip(dn, dn)
                    dn3 = dn.rearrange("p (t k h) -> p t k h", t=TB, k=2)
                    for i in range(2):
                        q = qkvD[:, TB * b:TB * b + TB, 512 * i:512 * i + 512].rearrange("p t (h c) -> p t h c", h=DH)
                        t1 = tmpD[:, 0:2048].rearrange("p (t h c) -> p t h c", t=TB, h=DH)
                        t2 = tmpD[:, 2048:4096].rearrange("p (t h c) -> p t h c", t=TB, h=DH)

                        def tab(k, a, w):
                            return ropeL[:, k, :, a:a + w].unsqueeze(2).to_broadcast([P, TB, DH, w])
                        mul(t1, q, tab(2 * i, 0, 64))
                        mul(t2[:, :, :, 0:32], q[:, :, :, 32:64], tab(2 * i + 1, 0, 32))
                        mul(t2[:, :, :, 32:64], q[:, :, :, 0:32], tab(2 * i + 1, 32, 32))
                        add(t1, t1, t2)
                        mul(q, t1, dn3[:, :, i, :].unsqueeze(3).to_broadcast([P, TB, DH, DHD]), "ropeD")
                for i in range(8):
                    dve.wait_ge(sem["qkT_D"], 16 * l + 2 * i + 2)
                    step(evacuate_qk(V.tensor_copy, 2 * i + 1), "qk_evV")
                for u in range(T * 4 + 3):
                    U = T * 4 * l + u
                    if u < T * 4:
                        t, pair = divmod(u, 4)
                        k0 = P if t % TB == 0 else 0
                        dve.wait_ge(sem["sD"], U + 1)
                        c = 2 * (u % 2)
                        if U >= 2:
                            dve.wait_ge(sem["expD"], 2 * (U - 1))
                        s2 = ps[:, 6 * (u % 2):6 * (u % 2) + 2, :]
                        step(V.tensor_reduce(sm("nmD", 4)[:, c:c + 2], s2[:, :, k0:256], X, ALU.max, negate=True))
                        ts(sm("nbD", 4)[:, c:c + 2], sm("nmD", 4)[:, c:c + 2], 8.0, ALU.mult, name="maxD")
                    if 1 <= u <= T * 4:
                        dve.wait_ge(sem["ptD"], U)
                        t = (u - 1) // 4
                        pt, bank = probTD[:, (u - 1) % 2, :], ps[:, 2 + (u - 1) % 2, :]
                        if t % TB == 0:
                            pt, bank = (a.rearrange("p (a b) -> p a b", a=2)[:, :, P:256] for a in (pt, bank))
                        step(V.tensor_copy(pt, bank), "ptcD")
                    if u >= 6 and (u - 6) % 4 == 0:
                        t = (u - 6) // 4
                        norm_o(l, t)
                for t in range(T):
                    dve.wait_ge(sem["do_mm"], T * l + t + 1)
                    ins = V.tensor_tensor(f[:, t, :], f[:, t, :], ps[:, t % 6, 0:D], ALU.add)
                    step(ins, "do_ev")
                step(V.tensor_copy(h[:, :, 0:64], f[:, :, 0:64]), "f_ready")
                dve.wait_ge(sem["shifted"], 48 * (2 * l + 2))
                total(sm("s1"), h[:, :, :])
                ts(sm("s1"), sm("s1"), 1.0 / D, ALU.mult)
                dev = wide["dev"][:, :, :]
                step(V.tensor_tensor(dev, h[:, :, :], per_row(sm("s1")), ALU.subtract), "devD")
                dve.wait_ge(sem["lnsq"], l + 1)
                total(sm("var"), wide["sq"][:, :, :])
                ts(sm("var"), sm("var"), 1.0 / D, ALU.mult, 1e-5, ALU.add, "lnvar")
                dve.wait_ge(sem["lnstd"], l + 1)
                recip(sm("std"), sm("std"))
                mul(dev, dev, per_row(sm("std")))
                mul(dev, dev, per_tile(v_("ln_g")[:, l * D:(l + 1) * D]))
                add(dev, dev, per_tile(v_("ln_b")[:, l * D:(l + 1) * D]), "lnD")
                for t in range(T):
                    dve.wait_ge(sem["e_mm"], T * l + t + 1)
                    k = 2 * (t % 3)
                    add(hidD[:, t, :].rearrange("p (a b) -> p a b", a=2), ps[:, k:k + 2, 0:HID],
                        v_("b1")[:, l * 2 * HID:(l + 1) * 2 * HID].rearrange("p (a b) -> p a b", a=2), "e_ev")
                for t in range(T):
                    dve.wait_ge(sem["gelu"], T * l + t + 1)
                    mul(hgD[:, t, :], hidD[:, t, 0:HID], hidD[:, t, HID:2 * HID], "hg")
                for t in range(T):
                    dve.wait_ge(sem["g_mm"], T * l + t + 1)
                    add(f[:, t, :], f[:, t, :], ps[:, t % 6, 0:D], "g_ev")
                add(f[:, :, :], f[:, :, :], per_tile(v_("b2")[:, l * D:(l + 1) * D]))
                if l + 1 < DEPTH:
                    step(V.tensor_copy(h[:, :, 0:64], f[:, :, 0:64]), "f_ready")
                else:
                    add(wide["dev"][:, :, :], f[:, :, :], x[:, :, :], "result")

        @block.tensor
        def _(pe):
            M = nc.tensor.matmul

            def transposes(p, src, rows=P):
                for t in range(T):
                    ins = nc.tensor.transpose(ps[0:rows, 6 + t // 4, (t % 4) * P:(t % 4) * P + P], src(t), ident)
                    if t % 4 == 3:
                        ins.then_inc(sem["turned"], 1)

            def project(p, lhs, rhs, n, chunks=1):
                for t in range(T):
                    if t % 4 == 0 and p != "f":
                        pe.wait_ge(sem["turned_copied"], 2 * TURN[p] + t // 4 + 1)
                    if t >= 6:
                        pe.wait_ge(sem["taken"], projected(p, t - 6))
                    for c in range(chunks):
                        ins = M(ps[:, t % 6, 0:n], lhs(t, c), rhs(c), start=(c == 0), stop=(c == chunks - 1))
                    ins.then_inc(sem["projected"], 1)

            def tile_T(t, c=0):
                return uT[:, t * P:(t + 1) * P]

            pe.wait_ge(sem["cst_in"], 16)
            nc.tensor.transpose(ps[:, 4, 0:P], cst[:, P:2 * P], ident).then_inc(sem["cmT"], 1)
            for b in range(B):
                pe.wait_ge(sem["cond_b"], b + 1)
                M(ps[:, 2 * b, :], cond_b[:, b, :], w_ada[:, 0:512], start=True, stop=True)
                M(ps[:, 2 * b + 1, 0:256], cond_b[:, b, :], w_ada[:, 512:768], start=True, stop=True)\
                    .then_inc(sem["adaP"], 1)
            pe.wait_ge(sem["u"], 1)
            transposes("a", lambda t: wide["u"][:, t, :])
            pe.wait_ge(sem["w_in"], 64)
            project("a", tile_T, lambda c: w_qkv[:, :], 3 * D)

            pe.wait_ge(sem["padsA"], 1)

            def group_T(G, bank, padq, padk, cols, name, id16, view):
                b, g = divmod(G, cols)
                for i, pad in enumerate((padq, padk)):
                    for tt in range(TB):
                        ins = nc.tensor.transpose(view[:, bank, i * 512 + tt * P:i * 512 + tt * P + P],
                                                  pad[:, TB * b + tt, g * P:(g + 1) * P], id16)
                ins.then_inc(sem[name], 1)

            def st_a(n):
                G, j = divmod(n, 4)
                pe.wait_ge(sem["stagedA"], G + 1)
                for kt in range(4):
                    if n >= 1 and kt % 2 == 0:
                        pe.wait_ge(sem["expA"], 2 * (n - 1) + kt // 2 + 1)
                    k = staged[32 * j:32 * j + 32, G % 2, 512 + kt * P:512 + kt * P + P]
                    ins = M(ps[:, kt, :], k, staged[32 * j:32 * j + 32, G % 2, 0:512], start=True, stop=True)
                    if kt % 2 == 1:
                        ins.then_inc(sem["stA"], 1)

            def pv_a(n):
                b, h = divmod(n, H)
                G, j = divmod(n, 4)
                pe.wait_ge(sem["expA"], 2 * n + 2)
                if j == 0 and G >= 2:
                    pe.wait_ge(sem["oA"], G - 1)
                for qt in range(TB):
                    for kt in range(TB):
                        c = (qt * 4 + j) * (HD + 1)
                        ins = M(ps[:, 4 + G % 2, c:c + HD + 1],
                                prob[:, n % 2, kt * 512 + qt * P:kt * 512 + qt * P + P],
                                vA[:, TB * b + kt, h, :], start=(kt == 0), stop=(kt == TB - 1))
                ins.then_inc(sem["pvA"], 1)

            group_T(0, 6, padq, padk, 4, "tA", ident16[:, :], ps16)
            for n in range(B * H + 1):
                if n < B * H:
                    st_a(n)
                    if n % 4 == 1 and n // 4 + 1 < 8:
                        group_T(n // 4 + 1, 6 + (n // 4 + 1) % 2, padq, padk, 4, "tA", ident16[:, :], ps16)
                if n >= 1:
                    pv_a(n - 1)
            pe.wait_ge(sem["oA"], 8)
            transposes("ao", lambda t: o_tok[:, t, :])
            project("ao", tile_T, lambda c: w_o[:, :], D)
            pe.wait_ge(sem["u"], 2)
            transposes("m", lambda t: wide["u"][:, t, :])
            project("m", tile_T, lambda c: w_f1[:, :], FF)
            pe.wait_ge(sem["h1"], 1)
            for g in range(8):
                if g >= 6:
                    pe.wait_ge(sem["h1_uT"], g - 5)
                for tt in range(4):
                    t = 4 * (g // 4) + tt
                    ins = nc.tensor.transpose(ps[:, g % 6, tt * P:(tt + 1) * P], hid1[:, t, (g % 4) * P:(g % 4) * P + P],
                                              ident)
                ins.then_inc(sem["h1_T"], 1)
            pe.wait_ge(sem["h1_uT"], 8)
            project("f", lambda t, c: hid1T[:, c, t * P:(t + 1) * P], lambda c: w_f2[:, c, :], D, 4)

            pe.wait_ge(sem["y"], 1)
            transposes("b", lambda t: wide["u"][:, t, :])
            pe.wait_ge(sem["w_quant"], 2)
            project("b", tile_T, lambda c: w_aq[:, :], 192)
            pe.wait_ge(sem["padsB"], 1)

            def s_b(n):
                G, j = divmod(n, 4)
                pe.wait_ge(sem["stagedB"], G + 1)
                for qt in range(4):
                    if n >= 1:
                        pe.wait_ge(sem["expB"], 4 * (n - 1) + qt + 1)
                    r = slice(32 * j, 32 * j + 2 * HQ)
                    ins = M(ps[:, qt, :], staged[r, (G % 4) % 2, qt * P:qt * P + P], staged[r, (G % 4) % 2, 512:1024],
                            start=True, stop=True)
                    if qt % 2 == 1:
                        ins.then_inc(sem["stB"], 1)

            def pt_b(m):
                pe.wait_ge(sem["quantB"], 4 * m + 4)
                c16 = codes.bitcast(F16)
                for kt in range(4):
                    if kt % 2 == 0 and m >= 1:
                        pe.wait_ge(sem["ptcB"], 2 * (m - 1) + kt // 2 + 1)
                    for qt in range(4):
                        c = (kt % 2) * 512 + qt * P
                        ins = nc.tensor.transpose(ps16[:, 4 + kt // 2, c:c + P],
                                                  c16[:, m % 2, qt, kt * P:(kt + 1) * P], ident16[:, :])
                    if kt % 2 == 1:
                        ins.then_inc(sem["ptB"], 1)

            def pv_b(m):
                b, h = divmod(m, H)
                pe.wait_ge(sem["ptcB"], 2 * m + 2)
                if h == 0 and b == 1:
                    pe.wait_ge(sem["outB"], 1)
                for qt in range(TB):
                    for kt in range(TB):
                        c = (qt * H + h) * (HQ + 1)
                        ins = M(ps[:, 6, c:c + HQ + 1], codesT[:, m % 2, kt, qt * P:(qt + 1) * P],
                                vB[:, TB * b + kt, h, :], start=(kt == 0), stop=(kt == TB - 1))
                ins.then_inc(sem["pvB"], 1)
            pe.wait_ge(sem["codes_high"], 1)
            for b in range(B):
                for n_ in range(H + 3):
                    n = b * H + n_
                    if n_ < H:
                        if n_ % 4 == 0:
                            if n // 4 >= 1:
                                pe.wait_ge(sem["stagedB"], n // 4)
                            group_T(n // 4, 7, padq, padk, 4, "tB", ident16[:, :], ps16)
                        s_b(n)
                    if 2 <= n_ < H + 2:
                        pt_b(n - 2)
                    if n_ >= 3:
                        pv_b(n - 3)
                pe.wait_ge(sem["ones16"], 1)
                for kt in range(TB):
                    ins = M(ps[:, 6, 320:320 + H * (HQ + 1)], ones16[:, :],
                            vB[:, TB * b + kt, :, :].rearrange("p h e -> p (h e)"), start=(kt == 0), stop=(kt == TB - 1))
                ins.then_inc(sem["pvB"], 1)
            pe.wait_ge(sem["zB"], 1)
            transposes("bo", lambda t: z[:, t, 0:64], 64)
            project("bo", lambda t, c: uT[0:64, t * P:(t + 1) * P], lambda c: w_ap[:, :], D)

            pe.wait_ge(sem["x2"], 1)
            for b in range(B):
                M(ps[:, b, 0:2 * D], cond_b[:, b, :], w_img[:, :], start=True, stop=True).then_inc(sem["imgP"], 1)
            transposes("c", lambda t: x[:, t, :])
            pe.wait_ge(sem["img"], 2)
            project("c", tile_T, lambda c: w_ca[:, :], 3 * D)
            pe.wait_ge(sem["padsC"], 1)
            pe.wait_ge(sem["cmask"], 1)

            def place(tile):
                return {3: (0, 0), 2: (1, 0), 0: (1, 384), 1: (2, 0)}[tile]

            stb = staged[:, :, :].bitcast(BF16)

            def s_c(n):
                G, j = divmod(n, 2)
                pe.wait_ge(sem["stagedC"], G + 1)
                if n >= 2:
                    pe.wait_ge(sem["maxC"], n - 1)
                st = stb
                r = slice(64 * j, 64 * j + 51)
                for qt in (3, 2, 0, 1):
                    bank, col = place(qt)
                    w = P * (qt + 1)
                    o = ps[:, 3 * (n % 2) + bank, col:col + w]
                    M(o, st[r, G % 2, qt * P:qt * P + P], st[r, G % 2, 512:512 + w], start=True, stop=False)
                    ins = M(o[:, w - P:w], identb[:, :], cmask[:, 0, :], start=False, stop=True)
                ins.then_inc(sem["sC"], 1)

            for n in range(B * H):
                if n % 2 == 0:
                    g = n // 2
                    group_T(g, 6 + g % 2, padqC, padkC, 8, "tC", identb[:, :], psb16)
                s_c(n)

            def st_c(n):
                G, j = divmod(n, 2)
                pe.wait_ge(sem["staged2C"], G + 1)
                if n >= 2:
                    pe.wait_ge(sem["expC"], n - 1)
                r = slice(64 * j, 64 * j + 54)
                for i in (3, 2, 0, 1):
                    kt = 3 - i
                    bank, col = place(i)
                    w = P * (i + 1)
                    o = ps[:, 3 * (n % 2) + bank, col:col + w]
                    M(o, stb[r, G % 2, 512 + kt * P:512 + kt * P + P], stb[r, G % 2, kt * P:512], start=True, stop=False)
                    ins = M(o[:, 0:P], identb[:, :], cmask[:, 1, :], start=False, stop=True)
                ins.then_inc(sem["stC"], 1)

            def pv_c(n):
                b, h = divmod(n, H)
                pe.wait_ge(sem["expC"], n + 1)
                if h % 8 == 0 and n:
                    pe.wait_ge(sem["oC"], n // 8)
                for qt in range(TB):
                    for kt in range(qt + 1):
                        bank, col = place(3 - kt)
                        a = 512 * bank + col + (qt - kt) * P
                        c = (qt * 8 + h % 8) * (HD + 1)
                        ins = M(ps[:, 6, c:c + HD + 1], probC[:, n % 2, a:a + P], vC[:, TB * b + kt, h, :],
                                start=(kt == 0), stop=(kt == qt))
                ins.then_inc(sem["pvC"], 1)
            pe.wait_ge(sem["mC"], 1)
            for n in range(B * H + 1):
                if n < B * H:
                    if n % 2 == 0:
                        g = n // 2
                        if g:
                            pe.wait_ge(sem["staged2C"], g)
                        group_T(g, 7, padqC, padkC, 8, "t2C", identb[:, :], psb16)
                    st_c(n)
                if n >= 1:
                    pv_c(n - 1)
            pe.wait_ge(sem["ocn"], 2)
            transposes("co", lambda t: o_tok[:, t, :])
            project("co", tile_T, lambda c: w_cp[:, :], D)
            pe.wait_ge(sem["w3_in"], 16 * 5 * DEPTH)
            pe.wait_ge(sem["dmask"], 1)
            for l in range(DEPTH):
                pe.wait_ge(sem["shifted"], 48 * (2 * l + 1))
                pe.wait_ge(sem["f_ready"], 2 * l + 1)
                transposes(f"d{l}", lambda t: wide["x1"][:, t, :])
                for t in range(T):
                    if t % 4 == 0:
                        pe.wait_ge(sem["turned_copied"], 2 * TURN[f"d{l}"] + t // 4 + 1)
                    if t >= 2:
                        pe.wait_ge(sem["d_ev"], T * l + t - 1)
                    for i in range(3):
                        ins = M(ps[:, 3 * (t % 2) + i, :], tile_T(t), w_d1[:, l, 512 * i:512 * i + 512], start=True, stop=True)
                    ins.then_inc(sem["d_mm"], 1)
                pe.wait_ge(sem["ropeD"], 2 * B * (l + 1))
                for i in range(16):
                    which, pair, b = i // 8, i // 2 % 4, i % 2
                    if i >= 6:
                        pe.wait_ge(sem["qk_evV" if i % 2 else "qk_evA"], 8 * l + (i - 6) // 2 + 1)
                    for tt in range(4):
                        c = 512 * which + P * pair
                        ins = nc.tensor.transpose(ps[:, i % 6, tt * P:(tt + 1) * P], qkvD[:, TB * b + tt, c:c + P], ident)
                    ins.then_inc(sem["qkT_D"], 1)
                pe.wait_ge(sem["qk_evA"], 8 * (l + 1))
                pe.wait_ge(sem["qk_evV"], 8 * (l + 1))
                for u in range(T * 4 + 2):
                    U = T * 4 * l + u
                    if u < T * 4:
                        t, pair = divmod(u, 4)
                        k0 = P if t % TB == 0 else 0
                        if u >= 2:
                            pe.wait_ge(sem["expD"], 2 * (U - 1))
                        for j in range(2):
                            o = ps[:, 6 * (u % 2) + j, k0:256]
                            M(o, qTD[64 * j:64 * j + 64, pair, t * P:(t + 1) * P],
                              kTD[64 * j:64 * j + 64, pair, (t - 1) * P + k0:(t + 1) * P], start=True, stop=False)
                            ins = M(o, identb[:, :], dmask[:, k0:256], start=False, stop=True)
                        ins.then_inc(sem["sD"], 1)
                    if 1 <= u <= T * 4:
                        v = u - 1
                        t = v // 4
                        pe.wait_ge(sem["expD"], 2 * U)
                        if v >= 2:
                            pe.wait_ge(sem["ptcD"], U - 2)
                        for j in range(2):
                            for k in ((1,) if t % TB == 0 else (0, 1)):
                                c = 256 * j + P * k
                                ins = nc.tensor.transpose(ps[:, 2 + v % 2, c:c + P], probD[:, v % 2, j, P * k:P * k + P], ident)
                        ins.then_inc(sem["ptD"], 1)
                    if u >= 2:
                        v = u - 2
                        t, pair = divmod(v, 4)
                        pe.wait_ge(sem["ptcD"], U - 1)
                        if pair == 0 and t >= 2:
                            pe.wait_ge(sem["o_D"], T * l + t - 1)
                        ks = (1,) if t % TB == 0 else (0, 1)
                        for j in range(2):
                            hh = 2 * pair + j
                            for k in ks:
                                c = 256 * j + P * k
                                ins = M(ps[:, 4 + t % 2, DHD * hh:DHD * hh + DHD], probTD[:, v % 2, c:c + P],
                                        qkvD[:, t - 1 + k, 1024 + DHD * hh:1024 + DHD * hh + DHD],
                                        start=(k == ks[0]), stop=(k == 1))
                        ins.then_inc(sem["pvD"], 1)
                pe.wait_ge(sem["o_D"], T * (l + 1))
                for g in range(8):
                    if g >= 6:
                        pe.wait_ge(sem["o_uT"], 8 * l + g - 5)
                    for tt in range(4):
                        ins = nc.tensor.transpose(ps[:, g % 6, tt * P:(tt + 1) * P],
                                                  oD[:, 4 * (g // 4) + tt, (g % 4) * P:(g % 4) * P + P], ident)
                    ins.then_inc(sem["o_T"], 1)
                pe.wait_ge(sem["o_uT"], 8 * (l + 1))
                for t in range(T):
                    if t >= 6:
                        pe.wait_ge(sem["do_ev"], T * l + t - 5)
                    for c in range(4):
                        ins = M(ps[:, t % 6, 0:D], qTD[:, c, t * P:(t + 1) * P], w_do[:, l, c, :], start=(c == 0), stop=(c == 3))
                    ins.then_inc(sem["do_mm"], 1)
                pe.wait_ge(sem["lnD"], l + 1)
                transposes(f"e{l}", lambda t: wide["dev"][:, t, :])
                for t in range(T):
                    if t % 4 == 0:
                        pe.wait_ge(sem["turned_copied"], 2 * TURN[f"e{l}"] + t // 4 + 1)
                    if t >= 3:
                        pe.wait_ge(sem["e_ev"], T * l + t - 2)
                    for i in range(2):
                        ins = M(ps[:, 2 * (t % 3) + i, 0:HID], tile_T(t), w_h1[:, l, HID * i:HID * i + HID], start=True, stop=True)
                    ins.then_inc(sem["e_mm"], 1)
                pe.wait_ge(sem["hg"], T * (l + 1))
                for g in range(6):
                    w = P if g % 3 < 2 else HID - 2 * P
                    for tt in range(4):
                        ins = nc.tensor.transpose(ps[0:w, g, tt * P:(tt + 1) * P],
                                                  hgD[:, 4 * (g // 3) + tt, (g % 3) * P:(g % 3) * P + w], ident)
                    ins.then_inc(sem["g_T"], 1)
                pe.wait_ge(sem["g_uT"], 6 * (l + 1))
                for t in range(T):
                    if t >= 6:
                        pe.wait_ge(sem["g_ev"], T * l + t - 5)
                    for c in range(3):
                        w = P if c < 2 else HID - 2 * P
                        ins = M(ps[:, t % 6, 0:D], hidTD[0:w, c, t * P:(t + 1) * P], w_h2[0:w, l, c, :],
                                start=(c == 0), stop=(c == 2))
                    ins.then_inc(sem["g_mm"], 1)


def rope_tables():
    f = np.float32
    half = np.arange(0, DHD, 2, dtype=f)
    inv = (f(1.0) / (f(10000.0) ** (half / f(DHD)))).astype(f)
    t = np.arange(S, dtype=f)
    freqs = (t[:, None] * inv[None, :]).astype(f)
    base = ((half + f(0.4 * DHD)) / f(1.4 * DHD)).astype(f)
    power = ((t - f(S // 2)) / f(WINDOW // 2)).astype(f)
    scale = (base[None, :] ** power[:, None]).astype(f)
    cos, sin = np.cos(freqs), np.sin(freqs)

    def both(a, b):
        return np.concatenate([a, b], axis=1).astype(f)
    return np.stack([both(cos * scale, cos * scale), both(-sin * scale, sin * scale),
                     both(cos / scale, cos / scale), both(-sin / scale, sin / scale)])


def masks():
    i = np.arange(P)[:, None]
    causal = np.where(np.arange(P)[None, :] > i, NEG_C, 0.0)
    j = np.arange(256)[None, :] - P
    band = np.where((j > i) | (j < i - WINDOW), NEG_D, 0.0)
    return np.concatenate([np.eye(P), causal, band], axis=1).astype(np.float32)


def lay_out(i):
    a = {k: np.asarray(v) for k, v in i.items()}
    c, q, e, f = "L0_cond_", "L0_attn_", "L0_cond2_", "L0_ffn_"
    parts = {
        "b_ada": a[c + "b_ada"], "b_qkv": np.concatenate([a[c + "b_q"], a[c + "b_k"], a[c + "b_v"]]),
        "b_o": a[c + "b_o"], "b_f1": a[c + "b_f1"], "b_f2": a[c + "b_f2"],
        "c_attn_b": a[e + "c_attn_b"], "c_proj_b": a[e + "c_proj_b"], "uk_b": a[e + "uk_b"], "uv_b": a[e + "uv_b"],
    }
    for n in ("qkv_alpha", "proj_alpha", "proj_b", "bias_q", "bias_k", "q_alpha", "k_alpha", "v_alpha", "q_zp", "k_zp",
              "v_zp", "attn_alpha", "attn_zp"):
        parts[n] = a[q + n]
    for n in ("q_scale", "k_scale", "ln_g", "ln_b", "b1", "b2"):
        parts[n] = a[f + n]
    return {
        "x": a["x"], "condT": a["cond_1024"].T, "maskT": a["mask_Bx1x1xS_ff0"].reshape(T, P).T,
        "vec": np.concatenate([parts[n].reshape(-1) for n, _ in VECTORS])[None, :],
        "cst": masks(), "rope": rope_tables(),
        "w_ada": a[c + "w_ada"], "w_qkv": np.concatenate([a[c + "w_q"], a[c + "w_k"], a[c + "w_v"]], axis=1),
        "w_o": a[c + "w_o"], "w_f1": a[c + "w_f1"], "w_f2": a[c + "w_f2"],
        "w_aqT": a[q + "qkv_w"].T, "w_apT": a[q + "proj_w"].T, "w_ca": a[e + "c_attn_w"], "w_cp": a[e + "c_proj_w"],
        "w_imgT": np.concatenate([a[e + "uk_w"].T, a[e + "uv_w"].T], axis=1),
        "wqkv": a[f + "wqkv"], "wo": a[f + "wo"], "w1": a[f + "w1"], "w2": a[f + "w2"],
    }


def kernel(**inputs):
    import concourse.bacc as bacc
    from concourse.bass_utils import run_bass_kernel_spmd
    arrays = {"in_" + n: np.ascontiguousarray(a) for n, a in lay_out(inputs).items()}
    nc = bacc.Bacc("TRN2", target_bir_lowering=False, num_devices=1)
    d = {n[3:]: nc.dram_tensor(n, a.shape, F32, kind="ExternalInput").ap() for n, a in arrays.items()}
    out = nc.dram_tensor("out", (B, S, D), F32, kind="ExternalOutput").ap()
    build(nc, d, out)
    return run_bass_kernel_spmd(nc, [arrays], core_ids=[0]).results[0]["out"]
```

```python
from contextlib import ExitStack

import numpy as np
import concourse.bass as bass
from concourse import mybir

F32 = mybir.dt.float32
F16 = mybir.dt.float16
BF16 = mybir.dt.bfloat16
U8 = mybir.dt.uint8
U16 = mybir.dt.uint16
ALU = mybir.AluOpType
ACT = mybir.ActivationFunctionType
X = mybir.AxisListType.X

P = 128
B, S, D = 2, 512, 128
TB = S // P
T = B * TB
H = 16
HD = D // H
HQ = D // 2 // H
FF = 512
EPS = 1e-7
MAX_TANH = float(np.float32(1.0 - 1e-5))
REACH = float(np.arctanh(np.float64(np.float32(1.0 - 1e-5))))
SERIES_BELOW = 0.3
DH, DHD, WINDOW, DEPTH = 8, 64, 64, 2
INNER = DH * DHD
HID = int(D * 4 * 2 / 3)
ROUND = 12582912.0
U_ZERO = 1152.0
NEG_C = -30000.0
NEG_D = -1e30


def lgamma_beta(a, b):
    import math
    return math.exp(math.lgamma(a) + math.lgamma(b) - math.lgamma(a + b))


HEAD_SCALE = lgamma_beta(HD / 2, 0.5) / lgamma_beta(D / 2, 0.5)

VECTORS = [
    ("b_ada", 6 * D), ("b_qkv", 3 * D), ("b_o", D), ("b_f1", FF), ("b_f2", D),
    ("qkv_alpha", 3 * D // 2), ("proj_alpha", D), ("proj_b", D),
    ("bias_q", H), ("bias_k", H), ("q_alpha", H), ("k_alpha", H), ("v_alpha", H),
    ("q_zp", H), ("k_zp", H), ("v_zp", H), ("attn_alpha", H), ("attn_zp", H),
    ("c_attn_b", 3 * D), ("c_proj_b", D), ("uk_b", D), ("uv_b", D),
    ("q_scale", DEPTH * DHD), ("k_scale", DEPTH * DHD), ("ln_g", DEPTH * D), ("ln_b", DEPTH * D),
    ("b1", DEPTH * 2 * HID), ("b2", DEPTH * D),
]
AT, _n = {}, 0
for _name, _len in VECTORS:
    AT[_name] = (_n, _len)
    _n += _len
NVEC = _n


def build(nc, d, out):
    with ExitStack() as ctx:
        def sb(name, shape, dt=F32):
            return ctx.enter_context(nc.sbuf_tensor(name, shape, dt))

        class Semaphores(dict):
            def __missing__(self, name):
                self[name] = ctx.enter_context(nc.semaphore(name))
                return self[name]

        sem = Semaphores()
        count = {}

        def signal(ins, name, n=1):
            count[name] = count.get(name, 0) + n
            ins.then_inc(sem[name], n)
            return count[name]

        ps = ctx.enter_context(nc.psum_tensor("ps", [P, 8, 512], F32))
        ps16 = ps[:, :, :].bitcast(F16)
        psb16 = ps[:, :, :].bitcast(BF16)
        vec = sb("vec", [P, NVEC])
        x = sb("x_tok", [P, T, D])
        cst = sb("cst", [P, 2 * P + 256])
        ident = cst[:, 0:P]
        ident16 = sb("ident16", [P, P], F16)
        identb = sb("identb", [P, P], BF16)
        cmask = sb("cmask", [P, 2, P], BF16)
        dmask = sb("dmask", [P, 256], BF16)
        ones16 = sb("ones16", [P, P], F16)
        rope = sb("rope", [P, 4, TB, DHD])
        condT = sb("condT", [P, B])
        cond_b = sb("cond_b", [P, B, P])
        maskT = sb("maskT", [P, T])
        uT = sb("uT", [P, T * P])
        wide = {n: sb(n, [P, T, D]) for n in ("x1", "sq", "dev", "u")}
        staged = sb("staged", [P, 2, 1024], F16)
        o_tok = sb("o_tok", [P, T, D])
        small = {}

        def sm(name, n=T):
            if name not in small:
                small[name] = sb("s_" + name, [P, n])
            return small[name][:, :]

        arena = sb("arena", [P, 26624])
        used = [0]

        def carve(shape, dt=F32, start=None):
            n = int(np.prod(shape))
            words = n if dt == F32 else n // 2
            if start is not None:
                used[0] = start
            a = arena[:, used[0]:used[0] + words]
            used[0] += words
            assert used[0] <= 26624
            if dt != F32:
                a = a.bitcast(dt)
            names = "abcdef"[:len(shape)]
            if len(shape) > 1:
                a = a.rearrange(f"p ({' '.join(names)}) -> p {' '.join(names)}", **dict(zip(names, shape)))
            return a

        z = carve([T, 3 * D], start=0)
        zsq = carve([T, 3 * D])
        after_z = used[0]
        padq = carve([T, H * 32], F16)
        padk = carve([T, H * 32], F16)
        prob = carve([2, 2048])
        vB = carve([T, H, HQ + 1], F16)
        vA = carve([T, H, 32])
        codes = carve([2, 4, 512], U16, start=used[0] - T * H * 32)
        codesT = carve([2, 4, 512], F16)
        oT = carve([2, 512])
        outB = carve([T, H * (HQ + 1)])
        w_ada = carve([6 * D])
        w_qkv = carve([3 * D])
        w_o = carve([D])
        w_f1 = carve([FF])
        w_f2 = carve([FF // P, D])
        w_aq = carve([3 * D // 2])
        w_ap = carve([D])[0:D // 2, :]
        w_ca = carve([3 * D])
        w_cp = carve([D])
        w_img = carve([2 * D])
        ada = carve([B, 6 * D])
        img = carve([B, 2 * D])
        hid1 = carve([T, FF], start=0)
        hid1T = carve([4, T * P])
        padqC = carve([T, H * 64], BF16, start=after_z)
        padkC = carve([T, H * 64], BF16)
        vC = carve([T, H, 32])
        probC = carve([4, 1280], start=0)
        outC = carve([TB, H, HD + 1])

        qkvD = carve([T, 3 * INNER], start=0)
        qTD = carve([INNER // P, T * P])
        kTD = carve([INNER // P, T * P])
        oTD = carve([INNER // P, T * P])
        sqD = oTD.rearrange("p a b -> p (a b)").rearrange("p (n c) -> p n c", n=TB)
        probTD = carve([2, 512])
        hidD = carve([T, 2 * HID], start=0)
        hgD = carve([T, HID])
        hidTD = carve([3, T * P], start=8192)
        w_d1 = sb("w_d1", [P, DEPTH, 3 * INNER])
        w_do = sb("w_do", [P, DEPTH, INNER // P, D])
        w_h1 = sb("w_h1", [P, DEPTH, 2 * HID])
        w_h2 = sb("w_h2", [P, DEPTH, 3, D])
        ropeL = sb("ropeL", [P, 4, TB, DHD])

        TURN = {n: i for i, n in enumerate(("a", "ao", "m", "b", "bo", "c", "co", "d0", "e0", "d1", "e1"))}
        PROJECTION = {n: i for i, n in enumerate(("a", "ao", "m", "f", "b", "bo", "c", "co"))}
        BLOCK = {"a": 0, "m": 1}

        def projected(p, t):
            return T * PROJECTION[p] + t + 1

        def v_(name):
            a, n = AT[name]
            return vec[:, a:a + n]

        S_BANKS = (0, 1, 6, 7)
        DO_BANKS = (0, 1, 6, 7, 2, 3)

        def evacuate_qk(copy, b, i):
            return copy((qTD, kTD)[i // 4][:, i % 4, b * 512:b * 512 + 512], ps[:, S_BANKS[i % 4], :])

        def prob_d(U):
            a = (wide["sq"], wide["dev"])[U // 2 % 2][:, 4 * (U % 2):4 * (U % 2) + 4, :]
            return a.rearrange("p t c -> p (t c)").rearrange("p (j k) -> p j k", j=2)

        def rope_terms(engine, t0, n, i, t1, t2, step):
            q = qkvD[:, t0:t0 + n, 512 * i:512 * i + 512].rearrange("p t (h c) -> p t h c", h=DH)

            def tab(k, a, w):
                return ropeL[:, k, t0 % TB:t0 % TB + n, a:a + w].unsqueeze(2).to_broadcast([P, n, DH, w])
            step(engine.tensor_tensor(t1, q, tab(2 * i, 0, 64), ALU.mult))
            step(engine.tensor_tensor(t2[:, :, :, 0:32], q[:, :, :, 32:64], tab(2 * i + 1, 0, 32), ALU.mult))
            step(engine.tensor_tensor(t2[:, :, :, 32:64], q[:, :, :, 0:32], tab(2 * i + 1, 32, 32), ALU.mult))
            if i == 0:
                return engine.tensor_tensor(q, t1, t2, ALU.add)
            step(engine.tensor_tensor(t1, t1, t2, ALU.add))
            factor = sm("dn", 16 * T)[:, 16 * t0:16 * t0 + 16 * n].rearrange("p (t k h) -> p t k h", t=n, k=2)[:, :, 1, :]
            return engine.tensor_tensor(q, t1, factor.unsqueeze(3).to_broadcast([P, n, DH, DHD]), ALU.mult)

        def per_tile(a, n=T):
            return a.unsqueeze(1).to_broadcast([P, n, a.shape[1]])

        def per_row(a, k=D):
            return a.unsqueeze(2).to_broadcast([P, a.shape[1], k])

        block = ctx.enter_context(nc.Block())

        @block.sync
        def _(sp):
            def load(dst, src, name):
                sp.dma_start(dst, src).then_inc(sem[name], 16)
            load(x[:, :, :], d["x"].rearrange("b (t p) c -> p (b t) c", p=P), "x_in")
            load(condT[:, :], d["condT"], "ada_in")
            load(w_ada[:, :], d["w_ada"], "ada_in")
            load(cst[:, :], d["cst"], "cst_in")
            a = AT["qkv_alpha"][0]
            load(vec[:, 0:a], d["vec"][0, 0:a].partition_broadcast(P), "vec_in")
            load(w_qkv[:, :], d["w_qkv"], "w_in")
            load(w_o[:, :], d["w_o"], "w_in")
            load(w_f1[:, :], d["w_f1"], "w_in")
            load(w_f2[:, :, :], d["w_f2"].rearrange("(c p) n -> p c n", p=P), "w_in")
            load(vec[:, a:NVEC], d["vec"][0, a:NVEC].partition_broadcast(P), "vec2_in")
            load(w_aq[:, :], d["w_aqT"], "w2_in")
            load(w_ap[:, :], d["w_apT"], "w2_in")
            load(w_ca[:, :], d["w_ca"], "w2_in")
            load(w_cp[:, :], d["w_cp"], "w2_in")
            load(w_img[:, :], d["w_imgT"], "w2_in")
            load(maskT[:, :], d["maskT"], "w2_in")
            load(rope[:, :, :, :], d["rope"].rearrange("k (t p) c -> p k t c", p=P), "w2_in")
            for l in range(DEPTH):
                load(w_d1[:, l, :], d["wqkv"][l], "w3_in")
                load(w_do[:, l, :, :], d["wo"][l].rearrange("(c p) n -> p c n", p=P), "w3_in")
                load(w_h1[:, l, :], d["w1"][l], "w3_in")
                load(w_h2[:, l, 0:2, :], d["w2"][l, 0:2 * P].rearrange("(c p) n -> p c n", p=P), "w3_in")
                load(w_h2[0:HID - 2 * P, l, 2, :], d["w2"][l, 2 * P:HID], "w3_in")
            for k in range(2 * DEPTH):
                for b in range(B):
                    sp.wait_ge(sem["f_ready"], B * k + b + 1)
                    h, f = wide["x1"], wide["u"]
                    t0, t1 = TB * b, TB * b + TB
                    load(h[1:P, t0:t1, 64:D], f[0:P - 1, t0:t1, 64:D], f"shifted{b}")
                    load(h[0:1, t0 + 1:t1, 64:D], f[P - 1:P, t0:t1 - 1, 64:D], f"shifted{b}")
            for b in range(B):
                sp.wait_ge(sem["result"], b + 1)
                load(out[b].rearrange("(t p) c -> p t c", p=P), wide["dev"][:, TB * b:TB * b + TB, :], "stored")
            sp.wait_ge(sem["stored"], 16 * B)

        @block.gpsimd
        def _(pool):
            nc.gpsimd.memset(padq, 0.0).then_inc(sem["pads_clear"], 1)
            nc.gpsimd.memset(padk, 0.0).then_inc(sem["pads_clear"], 1)
            nc.gpsimd.memset(vA, 0.0).then_inc(sem["vA_zeros"], 1)
            pool.wait_ge(sem["vA_zeros"], 1)
            nc.gpsimd.memset(vA[:, :, :, HD:HD + 1], 1.0).then_inc(sem["vA_ones"], 1)
            nc.gpsimd.memset(vB[:, :, :, HQ:HQ + 1], 1.0).then_inc(sem["vB_ones"], 1)
            nc.gpsimd.memset(ones16[:, :], 1.0).then_inc(sem["ones16"], 1)
            pool.wait_ge(sem["projected"], projected("f", T - 1))
            nc.gpsimd.memset(codes.bitcast(U16), 0x6400).then_inc(sem["codes_high"], 1)
            nc.gpsimd.memset(padq, 0.0).then_inc(sem["pads_clear"], 1)
            nc.gpsimd.memset(padk, 0.0).then_inc(sem["pads_clear"], 1)
            pool.wait_ge(sem["codes_high"], 1)
            u8 = codes.bitcast(U8).rearrange("p n t (k c) -> p n t k c", c=2)
            for n in range(B * H):
                h = n % H
                pool.wait_ge(sem["rB"], n + 1)
                if n >= 2:
                    pool.wait_ge(sem["ptB"], 2 * (n - 1))
                for qt in range(4):
                    c = 4 * (n % 2) + qt
                    nc.gpsimd.tensor_scalar(u8[:, n % 2, qt, :, 0], prob[:, n % 2, qt * 512:qt * 512 + 512],
                                            sm("rB", 8)[:, c:c + 1], sm("zpu", H)[:, h:h + 1],
                                            ALU.mult, ALU.add).then_inc(sem["quantB"], 1)
            pool.wait_ge(sem["pvB"], B * (H + 1))
            nc.gpsimd.memset(padqC, 0.0).then_inc(sem["padsC_zero"], 1)
            nc.gpsimd.memset(padkC, 0.0).then_inc(sem["padsC_zero"], 1)
            nc.gpsimd.memset(vC, 0.0).then_inc(sem["padsC_zero"], 1)
            pool.wait_ge(sem["padsC_zero"], 3)
            nc.gpsimd.memset(vC[:, :, :, HD:HD + 1], 1.0).then_inc(sem["padsC_clear"], 1)
            nc.gpsimd.memset(padqC.rearrange("p t (h s) -> p t h s", h=H)[:, :, :, 48:51], 1.0)\
                .then_inc(sem["padsC_clear"], 1)
            nc.gpsimd.memset(padkC.rearrange("p t (h s) -> p t h s", h=H)[:, :, :, 51:54], 1.0)\
                .then_inc(sem["padsC_clear"], 1)

            def step(ins):
                pool.wait_ge(sem["pool_step"], signal(ins, "pool_step"))
            r1 = o_tok[:, :, :].rearrange("p t c -> p (t c)").rearrange("p (t h c) -> p t h c", t=2, h=DH)
            r2 = staged[:, :, :].bitcast(F32).rearrange("p a b -> p (a b)").rearrange("p (t h c) -> p t h c", t=2, h=DH)
            for l in range(DEPTH):
                pool.wait_ge(sem["ropeL"], l + 1)
                for i in range(2):
                    for c in (2, 3):
                        if i == 0:
                            pool.wait_ge(sem["d_sq"], T * l + 2 * c + 2)
                        else:
                            pool.wait_ge(sem["d_dn"], B * l + 2)
                        step(rope_terms(nc.gpsimd, 2 * c, 2, i, r1, r2, step))
                nc.gpsimd.memset(sm("pool_done", 1), 0.0).then_inc(sem["rope1"], 1)

        @block.scalar
        def _(act):
            def step(ins, name="act_step"):
                act.wait_ge(sem[name], signal(ins, name))

            def logmap_norm(p, src):
                nc.scalar.activation(wide["sq"][:, :, :], src, ACT.Square).then_inc(sem["squares"], 1)
                act.wait_ge(sem["n2"], BLOCK[p] + 1)
                nc.scalar.activation(sm("n"), sm(p + "n2"), ACT.Sqrt).then_inc(sem["n"], 1)
                act.wait_ge(sem["dev"], BLOCK[p] + 1)
                nc.scalar.activation(wide["sq"][:, :, :], wide["dev"][:, :, :], ACT.Square).then_inc(sem["squares"], 1)
                act.wait_ge(sem["ratio"], BLOCK[p] + 1)
                nc.scalar.activation(sm("ln"), sm("ratio"), ACT.Ln).then_inc(sem["ln"], 1)
                act.wait_ge(sem["var"], BLOCK[p] + 1)
                nc.scalar.activation(sm("std"), sm("var"), ACT.Sqrt).then_inc(sem["std"], 1)
                act.wait_ge(sem["u"], BLOCK[p] + 1)
                nc.scalar.activation(wide["sq"][:, :, :], wide["u"][:, :, :], ACT.Square).then_inc(sem["squares"], 1)
                act.wait_ge(sem["u2"], BLOCK[p] + 1)
                nc.scalar.activation(sm("un"), sm("u2"), ACT.Sqrt).then_inc(sem["un"], 1)

            def copy_half(p, half, rows=P):
                act.wait_ge(sem["turned"], 2 * TURN[p] + half + 1)
                nc.scalar.activation(uT[0:rows, half * 512:half * 512 + 512], ps[0:rows, 6 + half, :], ACT.Copy)\
                    .then_inc(sem["turned_copied"], 1)

            def copy_T(p, rows=P):
                for half in range(2):
                    copy_half(p, half, rows)

            def mobius(p):
                act.wait_ge(sem["z2"], BLOCK[p] + 1)
                nc.scalar.activation(sm("zn"), sm("z2"), ACT.Sqrt).then_inc(sem["zn"], 1)
                act.wait_ge(sem["w"], BLOCK[p] + 1)
                nc.scalar.activation(wide["sq"][:, :, :], wide["dev"][:, :, :], ACT.Square).then_inc(sem["wsq"], 1)
                act.wait_ge(sem["w2"], BLOCK[p] + 1)
                nc.scalar.activation(sm("wn"), sm("w2"), ACT.Sqrt).then_inc(sem["wn"], 1)
                act.wait_ge(sem["wc"], BLOCK[p] + 1)
                nc.scalar.activation(sm("th"), sm("wc"), ACT.Tanh).then_inc(sem["th"], 1)

            act.wait_ge(sem["x_in"], 16)
            logmap_norm("a", x[:, :, :])
            copy_T("a")
            act.wait_ge(sem["zA"], 1)
            nc.scalar.activation(zsq, z, ACT.Square).then_inc(sem["zsqA"], 1)
            act.wait_ge(sem["z2A"], 1)
            nc.scalar.activation(sm("hn", 3 * T * H), sm("h2", 3 * T * H), ACT.Sqrt).then_inc(sem["hnA"], 1)
            nc.scalar.activation(sm("rn", 3 * T), sm("r2", 3 * T), ACT.Sqrt).then_inc(sem["hnA"], 1)
            for n in range(B * 4 * TB):
                for half in range(2):
                    act.wait_ge(sem["stA"], 2 * n + half + 1)
                    if n >= 2:
                        act.wait_ge(sem["pvA"], n - 1)
                    nc.scalar.activation(prob[:, n % 2, half * 1024:half * 1024 + 1024],
                                         ps[:, 2 * half:2 * half + 2, :], ACT.Exp,
                                         scale=HD ** -0.5).then_inc(sem["expA"], 1)
            copy_T("ao")
            mobius("a")
            act.wait_ge(sem["x1"], 1)
            logmap_norm("m", wide["x1"][:, :, :])
            copy_T("m")
            act.wait_ge(sem["h1"], 1)
            for t in range(T):
                if t >= 2:
                    act.wait_ge(sem["f2"], t - 1)
                nc.scalar.activation(ps[:, 6 + t % 2, :], hid1[:, t, :], ACT.Square,
                                     accum_out=sm("f2")[:, t:t + 1]).then_inc(sem["f2"], 1)
            act.wait_ge(sem["f2"], T)
            nc.scalar.activation(sm("fn"), sm("f2"), ACT.Sqrt).then_inc(sem["fn"], 1)
            for g in range(8):
                act.wait_ge(sem["h1_T"], g + 1)
                nc.scalar.activation(hid1T[:, g % 4, (g // 4) * 512:(g // 4) * 512 + 512],
                                     ps[:, g % 6, :], ACT.Copy).then_inc(sem["h1_uT"], 1)
            mobius("m")
            copy_T("b")
            for n in range(B * H):
                h = n % H
                for qt in range(4):
                    if qt % 2 == 0:
                        act.wait_ge(sem["maxB"], 2 * n + qt // 2 + 1)
                    if n >= 2 and qt == 0:
                        act.wait_ge(sem["quantB"], 4 * (n - 1))
                    ins = nc.scalar.activation(prob[:, n % 2, qt * 512:qt * 512 + 512], ps[:, qt, :], ACT.Exp,
                                               scale=sm("scB", H)[:, h:h + 1],
                                               bias=sm("nbB", 8)[:, 4 * (n % 2) + qt:4 * (n % 2) + qt + 1],
                                               accum_out=sm("sumB", 8)[:, 4 * (n % 2) + qt:4 * (n % 2) + qt + 1])
                    ins.then_inc(sem["expB"], 1)
            copy_T("bo", rows=D // 2)
            copy_T("c")
            act.wait_ge(sem["imx"], 1)
            nc.scalar.activation(sm("eimg", T * H), sm("simg", T * H), ACT.Exp).then_inc(sem["eimg"], 1)
            for n in range(B * H):
                act.wait_ge(sem["stC"], n + 1)
                if n >= 4:
                    act.wait_ge(sem["pvC"], n // 2 - 1)
                nc.scalar.activation(probC[:, n % 4, :],
                                     ps[:, 3 * (n % 2):3 * (n % 2) + 3, :].rearrange("p a b -> p (a b)")[:, 0:1280],
                                     ACT.Exp).then_inc(sem["expC"], 1)
            copy_T("co")
            for l in range(DEPTH):
                for t in range(T):
                    if t % TB == 0:
                        copy_half(f"d{l}", t // TB)
                    act.wait_ge(sem["d_mm"], T * l + t + 1)
                    k = 3 * (t % 2)
                    nc.scalar.activation(qkvD[:, t, :], ps[:, k:k + 3, :].rearrange("p a b -> p (a b)"), ACT.Copy)\
                        .then_inc(sem["d_ev"], 1)
                    if t == 0 and l:
                        pass
                    if t >= TB:
                        act.wait_ge(sem["d_ss"], T * l + t - 3)
                        act.wait_ge(sem["d_ev"], T * l + t + 1)
                    nc.scalar.activation(sqD[:, t % TB, :], ps[:, k:k + 2, :].rearrange("p a b -> p (a b)"),
                                         ACT.Square).then_inc(sem["d_sq"], 1)
                    if t % TB == TB - 1:
                        b = t // TB
                        act.wait_ge(sem["d_ss"], T * l + t + 1)
                        nc.scalar.activation(sm("dn", 16 * T)[:, 64 * b:64 * b + 64], sm("dss", 16 * T)[:, 64 * b:64 * b + 64],
                                             ACT.Sqrt).then_inc(sem["d_n"], 1)
                for b in range(B):
                    for u in range(TB * 4 + 2):
                        U = T * 4 * l + TB * 4 * b + u
                        if u == 0 and b == 0 or u == TB * 4 and b == 0:
                            c = u // (TB * 4)
                            for i in (0, 2, 4, 6):
                                act.wait_ge(sem["qkT_D"], 8 * (B * l + c) + i + 1)
                                evacuate_qk(lambda o, a: nc.scalar.activation(o, a, ACT.Copy), c, i)\
                                    .then_inc(sem["qk_evA"], 1)
                        if u < TB * 4:
                            t, pair = divmod(u, 4)
                            first = t == 0
                            act.wait_ge(sem["maxD"], U + 1)
                            if U >= 4:
                                act.wait_ge(sem["ptD"], U - 3)
                            for j in range(2):
                                c = 2 * (U % 4) + j
                                h = 8 * (TB * b + t) + 2 * pair + j
                                k0 = P if first else 0
                                nc.scalar.activation(prob_d(U)[:, j, k0:256], ps[:, 6 * (u % 2) + j, k0:256], ACT.Exp,
                                                     scale=sm("dq8", 8 * T)[:, h:h + 1], bias=sm("nbD", 8)[:, c:c + 1],
                                                     accum_out=sm("sumD", 8)[:, c:c + 1]).then_inc(sem["expD"], 1)
                        if u >= 2:
                            v = u - 2
                            act.wait_ge(sem["ptD"], U - 1)
                            if U >= 4:
                                act.wait_ge(sem["pvD"], U - 3)
                            pt, bank = probTD[:, v % 2, :], ps[:, 2 + v % 2, :]
                            if v < 4:
                                pt, bank = (a.rearrange("p (a b) -> p a b", a=2)[:, :, P:256] for a in (pt, bank))
                            nc.scalar.activation(pt, bank, ACT.Copy).then_inc(sem["ptcD"], 1)
                for b in range(B):
                    r = slice(TB * b, TB * b + TB)
                    act.wait_ge(sem["devD"], B * l + b + 1)
                    nc.scalar.activation(wide["sq"][:, r, :], wide["dev"][:, r, :], ACT.Square).then_inc(sem["lnsq"], 1)
                    act.wait_ge(sem["lnvar"], B * l + b + 1)
                    nc.scalar.activation(sm("std")[:, r], sm("var")[:, r], ACT.Sqrt).then_inc(sem["lnstd"], 1)
                copy_T(f"e{l}")
                for t in range(T + 1):
                    if t < T:
                        act.wait_ge(sem["e_g"], T * l + t + 1)
                        nc.scalar.activation(hidD[:, t, HID:2 * HID], hidD[:, t, HID:2 * HID], ACT.Gelu)\
                            .then_inc(sem["gelu"], 1)
                    if t >= 1:
                        v = t - 1
                        act.wait_ge(sem["g_T"], T * l + v + 1)
                        for c in range(2):
                            rows, chunks = ((P, slice(0, 2)), (HID - 2 * P, slice(2, 3)))[c]
                            nc.scalar.activation(hidTD[0:rows, chunks, v * P:v * P + P],
                                                 ps[0:rows, 4 + v % 2, 256 * c:256 * c + (256, P)[c]]
                                                 .rearrange("p (a b) -> p a b", b=P), ACT.Copy).then_inc(sem["g_uT"], 1)

        @block.vector
        def _(dve):
            V = nc.vector

            def step(ins, name="dve_step"):
                dve.wait_ge(sem[name], signal(ins, name))

            def mul(o, a, b, name="dve_step"):
                step(V.tensor_tensor(o, a, b, ALU.mult), name)

            def add(o, a, b, name="dve_step"):
                step(V.tensor_tensor(o, a, b, ALU.add), name)

            def ts(o, a, s1, op1, s2=None, op2=None, name="dve_step"):
                if op2 is None:
                    step(V.tensor_scalar(o, a, s1, None, op1), name)
                else:
                    step(V.tensor_scalar(o, a, s1, s2, op1, op2), name)

            def stt(o, a, s1, b, op1, op2, name="dve_step"):
                step(V.scalar_tensor_tensor(out=o, in0=a, scalar=s1, in1=b, op0=op1, op1=op2), name)

            def total(o, a, name="dve_step"):
                step(V.tensor_reduce(o, a, X, ALU.add), name)

            def recip(o, a, name="dve_step"):
                step(V.reciprocal(o, a), name)

            def shrink(o, norm, name="dve_step"):
                ts(o, norm, EPS, ALU.max)
                recip(o, o)
                ts(o, o, REACH, ALU.mult, 1.0, ALU.min, name)

            def logmap_norm(p, src, sc, sh):
                total(sm("s1"), src)
                ts(sm("s1"), sm("s1"), 1.0 / D, ALU.mult)
                dve.wait_ge(sem["squares"], 3 * BLOCK[p] + 1)
                total(sm(p + "n2"), wide["sq"][:, :, :], "n2")
                step(V.tensor_tensor(wide["dev"][:, :, :], src, per_row(sm("s1")), ALU.subtract), "dev")
                dve.wait_ge(sem["n"], BLOCK[p] + 1)
                ts(sm("nf"), sm("n"), EPS, ALU.max)
                ts(sm("nc"), sm("nf"), MAX_TANH, ALU.min)
                ts(sm("ratio"), sm("nc"), -1.0, ALU.mult, 1.0, ALU.add)
                recip(sm("ratio"), sm("ratio"))
                stt(sm("ratio"), sm("nc"), 1.0, sm("ratio"), ALU.add, ALU.mult, "ratio")
                mul(sm("t"), sm("nc"), sm("nc"))
                ts(sm("poly"), sm("t"), 1.0 / 13, ALU.mult)
                for k in (11, 9, 7, 5, 3):
                    stt(sm("poly"), sm("poly"), 1.0 / k, sm("t"), ALU.add, ALU.mult)
                stt(sm("poly"), sm("poly"), 1.0, sm("nc"), ALU.add, ALU.mult)
                ts(sm("pick"), sm("nc"), SERIES_BELOW, ALU.is_lt)
                dve.wait_ge(sem["ln"], BLOCK[p] + 1)
                stt(sm("poly"), sm("ln"), -0.5, sm("poly"), ALU.mult, ALU.add)
                mul(sm("poly"), sm("poly"), sm("pick"))
                stt(sm("fac"), sm("ln"), 0.5, sm("poly"), ALU.mult, ALU.add)
                recip(sm("nf"), sm("nf"))
                mul(sm("fac"), sm("fac"), sm("nf"))
                dve.wait_ge(sem["squares"], 3 * BLOCK[p] + 2)
                total(sm("var"), wide["sq"][:, :, :])
                mul(sm("t"), sm("fac"), sm("fac"))
                stt(sm("var"), sm("var"), 1.0 / D, sm("t"), ALU.mult, ALU.mult)
                ts(sm("var"), sm("var"), 1e-6, ALU.add, name="var")
                dve.wait_ge(sem["std"], BLOCK[p] + 1)
                recip(sm("std"), sm("std"))
                mul(sm("std"), sm("std"), sm("fac"))
                u = wide["u"][:, :, :]
                mul(u, wide["dev"][:, :, :], per_row(sm("std")))
                for b in range(B):
                    ub = u[:, TB * b:TB * b + TB, :]
                    mul(ub, ub, per_tile(ada[:, b, sc:sc + D], TB))
                for b in range(B):
                    ub = u[:, TB * b:TB * b + TB, :]
                    ins = V.tensor_tensor(ub, ub, per_tile(ada[:, b, sh:sh + D], TB), ALU.add)
                    if b == B - 1:
                        step(ins, "u")
                    else:
                        step(ins)
                dve.wait_ge(sem["squares"], 3 * BLOCK[p] + 3)
                total(sm("u2"), wide["sq"][:, :, :], "u2")
                dve.wait_ge(sem["un"], BLOCK[p] + 1)
                shrink(sm("us"), sm("un"))

            def mobius(p, src, gate, zin, dst, name):
                dev, sq = wide["dev"][:, :, :], wide["sq"][:, :, :]
                mul(sq, zin, zin)
                total(sm("z2"), sq, "z2")
                dve.wait_ge(sem["zn"], BLOCK[p] + 1)
                shrink(sm("zs"), sm("zn"))
                mul(dev, zin, per_row(sm("zs")))
                for b in range(B):
                    db = dev[:, TB * b:TB * b + TB, :]
                    ins = V.tensor_tensor(db, db, per_tile(ada[:, b, gate:gate + D], TB), ALU.mult)
                    step(ins, "w" if b == B - 1 else "dve_step")
                dve.wait_ge(sem["wsq"], BLOCK[p] + 1)
                total(sm("w2"), sq, "w2")
                mul(sq, src, dev)
                total(sm("xy"), sq)
                dve.wait_ge(sem["wn"], BLOCK[p] + 1)
                ts(sm("wc"), sm("wn"), EPS, ALU.max, name="wc")
                recip(sm("t"), sm("wc"))
                dve.wait_ge(sem["th"], BLOCK[p] + 1)
                mul(sm("tr"), sm("th"), sm("t"))
                mul(sm("xy"), sm("xy"), sm("tr"))
                mul(sm("y2"), sm("tr"), sm("tr"))
                mul(sm("y2"), sm("y2"), sm("w2"))
                x2 = sm(p + "n2")
                ts(sm("xy"), sm("xy"), 2.0, ALU.mult, 1.0, ALU.add)
                mul(sm("t"), x2, sm("y2"))
                add(sm("t"), sm("t"), sm("xy"))
                ts(sm("t"), sm("t"), EPS, ALU.max)
                recip(sm("t"), sm("t"))
                add(sm("xy"), sm("xy"), sm("y2"))
                mul(sm("xy"), sm("xy"), sm("t"))
                ts(sm("y2"), x2, -1.0, ALU.mult, 1.0, ALU.add)
                mul(sm("y2"), sm("y2"), sm("tr"))
                mul(sm("y2"), sm("y2"), sm("t"))
                mul(dev, dev, per_row(sm("y2")))
                mul(sq, src, per_row(sm("xy")))
                add(dst, sq, dev, name)

            def put_o(l, t):
                dve.wait_ge(sem["pvD"], T * 4 * l + 4 * t + 4)
                step(V.tensor_copy(oTD[:, :, t * P:t * P + P], ps[:, 4 + t % 2, :].rearrange("p (a b) -> p a b", b=P)),
                     "o_D")

            dve.wait_ge(sem["cst_in"], 16)
            step(V.tensor_copy(ident16[:, :], ident), "idents")
            step(V.tensor_copy(identb[:, :], ident), "idents")
            dve.wait_ge(sem["ada_in"], 32)
            for b in range(B):
                step(V.tensor_copy(cond_b[:, b, :], condT[:, b:b + 1].to_broadcast([P, P])), "cond_b")
            step(V.tensor_copy(cmask[:, 0, :], cst[:, P:2 * P]))
            dve.wait_ge(sem["cmT"], 1)
            step(V.tensor_copy(cmask[:, 1, :], ps[:, 4, 0:P]), "cmask")
            step(V.tensor_copy(dmask[:, :], cst[:, 2 * P:2 * P + 256]), "dmask")
            dve.wait_ge(sem["vec_in"], 16)
            for b in range(B):
                dve.wait_ge(sem["adaP"], b + 1)
                add(ada[:, b, 0:512], ps[:, 2 * b, :], v_("b_ada")[:, 0:512])
                add(ada[:, b, 512:768], ps[:, 2 * b + 1, 0:256], v_("b_ada")[:, 512:768])
            ts(ada[:, :, D:2 * D], ada[:, :, D:2 * D], 1.0, ALU.add)
            ts(ada[:, :, 4 * D:5 * D], ada[:, :, 4 * D:5 * D], 1.0, ALU.add)
            dve.wait_ge(sem["x_in"], 16)
            logmap_norm("a", x[:, :, :], D, 0)
            for t in range(T):
                dve.wait_ge(sem["projected"], projected("a", t))
                stt(z[:, t, :], ps[:, t % 6, 0:3 * D], sm("us")[:, t:t + 1], v_("b_qkv"), ALU.mult, ALU.add, "taken")
            signal_only = V.tensor_copy(sm("t"), sm("us"))
            step(signal_only, "zA")
            dve.wait_ge(sem["zsqA"], 1)
            total(sm("h2", 3 * T * H), zsq.rearrange("p t (h e) -> p (t h) e", e=HD))
            total(sm("r2", 3 * T), sm("h2", 3 * T * H).rearrange("p (r h) -> p r h", h=H), "z2A")
            dve.wait_ge(sem["hnA"], 2)
            shrink(sm("rs", 3 * T), sm("rn", 3 * T))
            ts(sm("rs", 3 * T), sm("rs", 3 * T), HEAD_SCALE, ALU.mult)
            hf = sm("hf", 3 * T * H)
            hn3 = sm("hn", 3 * T * H).rearrange("p (r h) -> p r h", h=H)
            hf3 = hf.rearrange("p (r h) -> p r h", h=H)
            mul(hf3, hn3, per_row(sm("rs", 3 * T), H))
            shrink(hf, hf)
            mul(hf3, hf3, per_row(sm("rs", 3 * T), H))
            mul(z.rearrange("p t (h e) -> p (t h) e", e=HD), z.rearrange("p t (h e) -> p (t h) e", e=HD),
                per_row(hf, HD))
            qz = z[:, :, 0:D].rearrange("p t (h e) -> p t h e", e=HD)
            kz = z[:, :, D:2 * D].rearrange("p t (h e) -> p t h e", e=HD)
            pq = padq.rearrange("p t (h s e) -> p t h s e", s=4, e=HD)
            pk = padk.rearrange("p t (h s e) -> p t h s e", s=4, e=HD)
            dve.wait_ge(sem["pads_clear"], 2)
            for src, pad, hi, lo in ((qz, pq, (0, 1), (2, 3)), (kz, pk, (0, 2), (1, 3))):
                step(V.tensor_copy(pad[:, :, :, hi[0], :], src))
                step(V.tensor_copy(pad[:, :, :, hi[1], :], src))
                step(V.tensor_tensor(pad[:, :, :, lo[0], :], src, pad[:, :, :, hi[0], :], ALU.subtract))
                step(V.tensor_copy(pad[:, :, :, lo[1], :], pad[:, :, :, lo[0], :]))
            dve.wait_ge(sem["vA_ones"], 1)
            step(V.tensor_copy(vA[:, :, :, 0:HD], z[:, :, 2 * D:3 * D].rearrange("p t (h e) -> p t h e", e=HD)), "padsA")

            for G in range(B * 4 + 1):
                if G < B * 4:
                    dve.wait_ge(sem["tA"], G + 1)
                    step(V.tensor_copy(staged[:, G % 2, :], ps16[:, 6 + G % 2, 0:1024]), "stagedA")
                if G >= 1:
                    b, g = divmod(G - 1, 4)
                    dve.wait_ge(sem["pvA"], 4 * G)
                    if G >= 3:
                        dve.wait_ge(sem["oT_A"], G - 2)
                    step(V.tensor_copy(oT[:, (G - 1) % 2, :], ps[:, 4 + (G - 1) % 2, :]), "oT_A")
                    dve.wait_ge(sem["toA"], G)
                    o = ps[:, 4 + (G - 1) % 2, :].rearrange("p (t h e) -> p t h e", t=TB, h=4)
                    rs = sm("rsumA", 16).rearrange("p (t h) -> p t h", h=4)
                    recip(rs, o[:, :, :, HD])
                    mul(o_tok[:, TB * b:TB * b + TB, 32 * g:32 * g + 32].rearrange("p t (h e) -> p t h e", h=4),
                        o[:, :, :, 0:HD], rs.unsqueeze(3).to_broadcast([P, TB, 4, HD]), "oA")
            for t in range(T):
                dve.wait_ge(sem["projected"], projected("ao", t))
                stt(z[:, t, 0:D], ps[:, t % 6, 0:D], 1.0 / HEAD_SCALE, v_("b_o"), ALU.mult, ALU.add, "taken")
            mobius("a", x[:, :, :], 2 * D, z[:, :, 0:D], wide["x1"][:, :, :], "x1")
            logmap_norm("m", wide["x1"][:, :, :], 4 * D, 3 * D)
            for t in range(T):
                dve.wait_ge(sem["projected"], projected("m", t))
                stt(hid1[:, t, :], ps[:, t % 6, :], sm("us")[:, t:t + 1], v_("b_f1"), ALU.mult, ALU.add, "taken")
            step(V.tensor_copy(sm("t"), sm("us")), "h1")
            dve.wait_ge(sem["fn"], 1)
            shrink(sm("fs"), sm("fn"))
            z2 = arena[:, 0:T * D].rearrange("p (t c) -> p t c", t=T)
            for t in range(T):
                dve.wait_ge(sem["projected"], projected("f", t))
                stt(z2[:, t, :], ps[:, t % 6, 0:D], sm("fs")[:, t:t + 1], v_("b_f2"), ALU.mult, ALU.add, "taken")
            mobius("m", wide["x1"][:, :, :], 5 * D, z2, wide["u"][:, :, :], "y")

            dve.wait_ge(sem["vec2_in"], 16)
            dve.wait_ge(sem["w2_in"], 16 * 7)
            for w, al, rows, n in ((w_aq, "qkv_alpha", P, 192), (w_ap, "proj_alpha", 64, D)):
                r = wide["sq"][0:rows, 0:2, :].rearrange("p a b -> p (a b)")[:, 0:n]
                recip(r, v_(al)[0:rows, :])
                mul(w[:, :], w[:, :], r)
                ts(w[:, :], w[:, :], -8.0, ALU.max, 7.0, ALU.min)
                ts(w[:, :], w[:, :], ROUND, ALU.add, ROUND, ALU.subtract)
                mul(w[:, :], w[:, :], v_(al)[0:rows, :], "w_quant")
            for name in ("q_zp", "k_zp", "v_zp", "attn_zp"):
                ts(v_(name), v_(name), ROUND, ALU.add, ROUND, ALU.subtract)
            zb = z[:, :, 0:192]
            for t in range(T):
                dve.wait_ge(sem["projected"], projected("b", t))
                step(V.tensor_copy(z[:, t, 0:192], ps[:, t % 6, 0:192]), "taken")
            for i, (al, zp, bias) in enumerate((("q_alpha", "q_zp", "bias_q"), ("k_alpha", "k_zp", "bias_k"),
                                                ("v_alpha", "v_zp", None))):
                zi = z[:, :, 64 * i:64 * i + 64].rearrange("p t (h e) -> p t h e", e=HQ)

                def by_head(a):
                    return a.unsqueeze(1).unsqueeze(3).to_broadcast([P, T, H, HQ])
                if bias is not None:
                    add(zi, zi, by_head(v_(bias)))
                recip(sm("ia", H), v_(al))
                mul(zi, zi, by_head(sm("ia", H)))
                add(zi, zi, by_head(v_(zp)))
                ts(zi, zi, -8.0, ALU.max, 7.0, ALU.min)
                ts(zi, zi, ROUND, ALU.add, ROUND, ALU.subtract)
            zi = z[:, :, 0:64].rearrange("p t (h e) -> p t h e", e=HQ)
            step(V.tensor_tensor(zi, zi, v_("q_zp").unsqueeze(1).unsqueeze(3).to_broadcast([P, T, H, HQ]), ALU.subtract))
            pq = padq.rearrange("p t (h s e) -> p t h s e", s=8, e=HQ)
            pk = padk.rearrange("p t (h s e) -> p t h s e", s=8, e=HQ)
            kz = z[:, :, 64:128].rearrange("p t (h e) -> p t h e", e=HQ)
            dve.wait_ge(sem["pads_clear"], 4)
            step(V.tensor_copy(pq[:, :, :, 0, :], zi))
            step(V.tensor_tensor(pq[:, :, :, 1, :], zi, pq[:, :, :, 0, :], ALU.subtract))
            step(V.tensor_copy(pk[:, :, :, 0, :], kz))
            step(V.tensor_copy(pk[:, :, :, 1, :], kz))
            dve.wait_ge(sem["vB_ones"], 1)
            step(V.tensor_copy(vB[:, :, :, 0:HQ], z[:, :, 128:192].rearrange("p t (h e) -> p t h e", e=HQ)))
            mul(sm("scB", H), v_("q_alpha"), v_("k_alpha"))
            ts(sm("scB", H), sm("scB", H), HQ ** -0.5, ALU.mult)
            ts(sm("zpa", H), v_("attn_zp"), U_ZERO, ALU.add)
            ts(sm("zpu", H), v_("attn_zp"), 128.0, ALU.add, name="padsB")
            for b in range(B):
                for n_ in range(H + 2):
                    n = b * H + n_
                    if n_ < H:
                        h = n_
                        if h % 4 == 0:
                            dve.wait_ge(sem["tB"], n // 4 + 1)
                            step(V.tensor_copy(staged[:, (h // 4) % 2, :], ps16[:, 7, 0:1024]), "stagedB")
                        for half in range(2):
                            dve.wait_ge(sem["stB"], 2 * n + half + 1)
                            c = 4 * (n % 2) + 2 * half
                            if n >= 2:
                                dve.wait_ge(sem["expB"], 4 * (n - 1))
                            step(V.tensor_reduce(sm("nmB", 8)[:, c:c + 2], ps[:, 2 * half:2 * half + 2, :], X, ALU.max,
                                                 negate=True))
                            ts(sm("nbB", 8)[:, c:c + 2], sm("nmB", 8)[:, c:c + 2], sm("scB", H)[:, h:h + 1], ALU.mult,
                               name="maxB")
                    if 1 <= n_ <= H:
                        h, m = n_ - 1, n - 1
                        dve.wait_ge(sem["expB"], 4 * m + 4)
                        if m >= 2:
                            dve.wait_ge(sem["quantB"], 4 * (m - 1))
                        c = 4 * (m % 2)
                        ts(sm("rB", 8)[:, c:c + 4], sm("sumB", 8)[:, c:c + 4], v_("attn_alpha")[:, h:h + 1], ALU.mult)
                        recip(sm("rB", 8)[:, c:c + 4], sm("rB", 8)[:, c:c + 4], "rB")
                    if n_ >= 2:
                        m = n - 2
                        for half in range(2):
                            dve.wait_ge(sem["ptB"], 2 * m + half + 1)
                            step(V.tensor_copy(codesT[:, m % 2, 2 * half:2 * half + 2, :],
                                               ps16[:, 4 + half, 0:1024].rearrange("p (a b) -> p a b", a=2)), "ptcB")
                dve.wait_ge(sem["pvB"], H * (b + 1) + b + 1)
                ob = outB[:, TB * b:TB * b + TB, :]
                cs = sm("colsum", H * (HQ + 1))
                step(V.tensor_copy(cs, ps[:, 6, 320:320 + H * (HQ + 1)]))
                c3 = cs.rearrange("p (h e) -> p h e", h=H)
                mul(c3, c3, sm("zpa", H).unsqueeze(2).to_broadcast([P, H, HQ + 1]))
                step(V.tensor_tensor(ob, ps[:, 6, 0:320].rearrange("p (t c) -> p t c", t=TB),
                                     cs.unsqueeze(1).to_broadcast([P, TB, H * (HQ + 1)]), ALU.subtract), "outB")
            o4 = outB.rearrange("p t (h e) -> p t h e", h=H)
            mul(sm("fa", H), v_("attn_alpha"), v_("v_alpha"))
            ob = z[:, :, 0:64].rearrange("p t (h e) -> p t h e", e=HQ)
            one = sm("one", T * H).rearrange("p (t h) -> p t h", h=H)
            mul(one, o4[:, :, :, HQ], v_("v_zp").unsqueeze(1).to_broadcast([P, T, H]))
            step(V.tensor_tensor(ob, o4[:, :, :, 0:HQ], one.unsqueeze(3).to_broadcast([P, T, H, HQ]), ALU.subtract))
            mul(ob, ob, sm("fa", H).unsqueeze(1).unsqueeze(3).to_broadcast([P, T, H, HQ]), "zB")
            for t in range(T):
                dve.wait_ge(sem["projected"], projected("bo", t))
                add(x[:, t, :], x[:, t, :], ps[:, t % 6, 0:D], "taken")
            add(x[:, :, :], x[:, :, :], per_tile(v_("proj_b")), "x2")

            for b in range(B):
                dve.wait_ge(sem["imgP"], b + 1)
                add(img[:, b, 0:D], ps[:, b, 0:D], v_("uk_b"))
                add(img[:, b, D:2 * D], ps[:, b, D:2 * D], v_("uv_b"), "img")
            for t in range(T):
                dve.wait_ge(sem["projected"], projected("c", t))
                add(z[:, t, :], ps[:, t % 6, 0:3 * D], v_("c_attn_b"), "taken")
            ts(z[:, :, 0:D], z[:, :, 0:D], HD ** -0.5, ALU.mult)
            for b in range(B):
                mul(zsq[:, TB * b:TB * b + TB, 0:D], z[:, TB * b:TB * b + TB, 0:D], per_tile(img[:, b, 0:D], TB))
            simg = sm("simg", T * H)
            s3 = simg.rearrange("p (t h) -> p t h", h=H)
            total(s3, zsq[:, :, 0:D].rearrange("p t (h e) -> p t h e", e=HD))
            pq = padqC.rearrange("p t (h s) -> p t h s", h=H)
            pk = padkC.rearrange("p t (h s) -> p t h s", h=H)

            def split(src, pad, places, e):
                left = zsq[:, :, 0:H * e].rearrange("p t (h e) -> p t h e", e=e)
                now = src
                for i, slots in enumerate(places):
                    for k in slots:
                        step(V.tensor_copy(pad[:, :, :, k:k + e], now))
                    if i + 1 < len(places):
                        k = slots[0]
                        step(V.tensor_tensor(left, now, pad[:, :, :, k:k + e], ALU.subtract))
                        now = left
            dve.wait_ge(sem["padsC_clear"], 3)
            split(z[:, :, 0:D].rearrange("p t (h e) -> p t h e", e=HD), pq, ((0, 8, 16), (24, 32), (40,)), HD)
            split(z[:, :, D:2 * D].rearrange("p t (h e) -> p t h e", e=HD), pk, ((0, 24, 40), (8, 32), (16,)), HD)
            split(maskT[:, :].unsqueeze(2).unsqueeze(3).to_broadcast([P, T, H, 1]), pk, ((48,), (49,), (50,)), 1)
            step(V.tensor_copy(vC[:, :, :, 0:HD], z[:, :, 2 * D:3 * D].rearrange("p t (h e) -> p t h e", e=HD)), "padsC")
            nmx = sm("nmx", T * H).rearrange("p (t h) -> p t h", h=H)
            PLACE = {3: (0, 0), 2: (1, 0), 0: (1, 384), 1: (2, 0)}
            for b in range(B):
                for h in range(H):
                    n = b * H + h
                    if h % 2 == 0:
                        dve.wait_ge(sem["tC"], n // 2 + 1)
                        step(V.tensor_copy(staged[:, (n // 2) % 2, :], ps16[:, 6 + (n // 2) % 2, 0:1024]), "stagedC")
                    dve.wait_ge(sem["sC"], n + 1)
                    for qt in range(4):
                        bank, col = PLACE[qt]
                        ins = V.tensor_reduce(nmx[:, TB * b + qt, h:h + 1],
                                              ps[:, 3 * (n % 2) + bank, col:col + P * (qt + 1)], X, ALU.max, negate=True)
                        if qt == 3:
                            step(ins, "maxC")
            nm = sm("nmx", T * H)
            ts(sm("one", T * H), simg, -1.0, ALU.mult)
            step(V.tensor_tensor(nm, nm, sm("one", T * H), ALU.min))
            add(simg, simg, nm, "imx")
            split(nmx.unsqueeze(3), pq, ((51,), (52,), (53,)), 1)
            ts(sm("one", T * H), nm, 1.0, ALU.mult, name="mC")
            for m in range(B * H // 2 + 2):
                if m < B * H // 2:
                    dve.wait_ge(sem["t2C"], m + 1)
                    step(V.tensor_copy(staged[:, m % 2, :], ps16[:, 7, 0:1024]), "staged2C")
                g = m // 2 - 1
                if m % 2 == 0 and m >= 2:
                    dve.wait_ge(sem["pvC"], m)
                    step(V.tensor_copy(oT[:, g % 2, :], ps[:, 6, :]), "oT_C")
                if m % 2 == 1 and m >= 3:
                    dve.wait_ge(sem["toC"], g + 1)
                    step(V.tensor_copy(outC[:, :, 4 * (g % 4):4 * (g % 4) + 4, :],
                                       ps[:, 7, :].rearrange("p (t h e) -> p t h e", t=TB, h=4)[:, :, :, 0:HD + 1]), "oC")
                if m % 2 == 1 and m >= 3 and g % 4 == 3:
                    b = g // 4
                    dve.wait_ge(sem["eimg"], 1)
                    e3 = sm("eimg", T * H).rearrange("p (t h) -> p t h", h=H)[:, TB * b:TB * b + TB, :]
                    add(outC[:, :, :, HD], outC[:, :, :, HD], e3)
                    recip(outC[:, :, :, HD], outC[:, :, :, HD])
                    ob = o_tok[:, TB * b:TB * b + TB, :].rearrange("p t (h e) -> p t h e", e=HD)
                    for tt in range(TB):
                        mul(ob[:, tt], img[:, b, D:2 * D].rearrange("p (h e) -> p h e", e=HD), per_row(e3[:, tt, :], HD))
                    add(ob, ob, outC[:, :, :, 0:HD])
                    mul(ob, ob, outC[:, :, :, HD].unsqueeze(3).to_broadcast([P, TB, H, HD]), "ocn")
            f, h = wide["u"], wide["x1"]

            def send(b):
                step(V.tensor_copy(h[:, TB * b:TB * b + TB, 0:64], f[:, TB * b:TB * b + TB, 0:64]), "f_ready")
            step(V.memset(h[0:1, 0:T:TB, 64:D], 0.0))
            for t in range(T):
                dve.wait_ge(sem["projected"], projected("co", t))
                add(wide["u"][:, t, :], ps[:, t % 6, 0:D], v_("c_proj_b"), "taken")
                if t % TB == TB - 1:
                    send(t // TB)
            dn, dq8 = sm("dn", 16 * T), sm("dq8", 8 * T)
            for l in range(DEPTH):
                if l:
                    dve.wait_ge(sem["rope1"], l)
                for i, name in ((0, "q_scale"), (2, "k_scale")):
                    s_ = v_(name)[:, l * DHD:(l + 1) * DHD]
                    mul(ropeL[:, i], rope[:, i], per_tile(s_, TB))
                    for a in range(2):
                        mul(ropeL[:, i + 1, :, 32 * a:32 * a + 32], rope[:, i + 1, :, 32 * a:32 * a + 32],
                            per_tile(s_[:, 32 - 32 * a:64 - 32 * a], TB),
                            name="ropeL" if (i, a) == (2, 1) else "dve_step")

                def norms(t):
                    dve.wait_ge(sem["d_sq"], T * l + t + 1)
                    total(sm("dss", 16 * T)[:, 16 * t:16 * t + 16], sqD[:, t % TB, :].rearrange("p (n c) -> p n c", c=DHD),
                          "d_ss")

                def factors(b):
                    dve.wait_ge(sem["d_n"], B * l + b + 1)
                    d_ = dn[:, 64 * b:64 * b + 64]
                    ts(d_, d_, 1e-12, ALU.max)
                    recip(d_, d_)
                    ts(dq8[:, 32 * b:32 * b + 32].rearrange("p (t h) -> p t h", t=TB),
                       d_.rearrange("p (t k h) -> p t k h", t=TB, k=2)[:, :, 0, :], 8.0, ALU.mult, name="d_dn")
                r1, r2 = (a[:, 0, :].rearrange("p (t h c) -> p t h c", t=2, h=DH) for a in (qTD, kTD))
                for t in range(TB):
                    norms(t)
                    if t % 2:
                        step(rope_terms(V, t - 1, 2, 0, r1, r2, step))
                factors(0)
                for t in (0, 2):
                    step(rope_terms(V, t, 2, 1, r1, r2, step), "rope0" if t else "dve_step")
                    norms(TB + t)
                    norms(TB + t + 1)
                factors(1)
                for b in range(B):
                    for u in range(TB * 4 + 1):
                        U = T * 4 * l + TB * 4 * b + u
                        if u == 0 and b == 0 or u == TB * 4 and b == 0:
                            c = u // (TB * 4)
                            for i in (1, 3, 5, 7):
                                dve.wait_ge(sem["qkT_D"], 8 * (B * l + c) + i + 1)
                                step(evacuate_qk(V.tensor_copy, c, i), "qk_evV")
                        if u < TB * 4:
                            t, pair = divmod(u, 4)
                            k0 = P if t == 0 else 0
                            dve.wait_ge(sem["sD"], U + 1)
                            c = 2 * (U % 4)
                            if U >= 4:
                                dve.wait_ge(sem["expD"], 2 * (U - 3))
                            s2 = ps[:, 6 * (u % 2):6 * (u % 2) + 2, :]
                            nm, nb = (sm(n, 8)[:, c:c + 2] for n in ("nmD", "nbD"))
                            step(V.tensor_reduce(nm, s2[:, :, k0:256], X, ALU.max, negate=True))
                            hh = 8 * (TB * b + t) + 2 * pair
                            mul(nb, nm, dq8[:, hh:hh + 2], "maxD")
                        if u >= 1:
                            t = (u - 1) // 4
                            k0 = P if t == 0 else 0
                            dve.wait_ge(sem["expD"], 2 * U)
                            c = 2 * ((U - 1) % 4)
                            rs = sm("rsD", 2)
                            recip(rs, sm("sumD", 8)[:, c:c + 2])
                            pr = prob_d(U - 1)[:, :, k0:256]
                            mul(pr, pr, per_row(rs, 256 - k0), "normD")
                        if u >= 8 and u % 4 == 0:
                            put_o(l, TB * b + u // 4 - 2)
                    put_o(l, TB * b + TB - 1)
                for b in range(B):
                    for t in range(TB * b, TB * b + TB):
                        dve.wait_ge(sem["do_mm"], T * l + t + 1)
                        step(V.tensor_tensor(f[:, t, :], f[:, t, :], ps[:, DO_BANKS[t % 6], 0:D], ALU.add), "do_ev")
                    send(b)
                for b in range(B):
                    r = slice(TB * b, TB * b + TB)
                    dve.wait_ge(sem[f"shifted{b}"], 32 * (2 * l + 2))
                    dev = wide["dev"][:, r, :]
                    s1, var, std = (sm(n)[:, r] for n in ("s1", "var", "std"))
                    total(s1, h[:, r, :])
                    ts(s1, s1, 1.0 / D, ALU.mult)
                    step(V.tensor_tensor(dev, h[:, r, :], per_row(s1), ALU.subtract), "devD")
                    dve.wait_ge(sem["lnsq"], B * l + b + 1)
                    total(var, wide["sq"][:, r, :])
                    ts(var, var, 1.0 / D, ALU.mult, 1e-5, ALU.add, "lnvar")
                    dve.wait_ge(sem["lnstd"], B * l + b + 1)
                    recip(std, std)
                    mul(dev, dev, per_row(std))
                    mul(dev, dev, per_tile(v_("ln_g")[:, l * D:(l + 1) * D], TB))
                    add(dev, dev, per_tile(v_("ln_b")[:, l * D:(l + 1) * D], TB), "lnD")
                for t in range(T + 3):
                    if t < T:
                        dve.wait_ge(sem["e_mm"], T * l + t + 1)
                        k = 2 * (t % 2)
                        b1 = v_("b1")[:, l * 2 * HID:(l + 1) * 2 * HID]
                        add(hidD[:, t, HID:2 * HID], ps[:, k + 1, 0:HID], b1[:, HID:2 * HID], "e_g")
                        add(hidD[:, t, 0:HID], ps[:, k, 0:HID], b1[:, 0:HID], "e_ev")
                    if 1 <= t <= T:
                        dve.wait_ge(sem["gelu"], T * l + t)
                        mul(hgD[:, t - 1, :], hidD[:, t - 1, 0:HID], hidD[:, t - 1, HID:2 * HID], "hg")
                    if t >= 3:
                        v = t - 3
                        dve.wait_ge(sem["g_mm"], T * l + v + 1)
                        add(f[:, v, :], f[:, v, :], ps[:, 6 + v % 2, 0:D], "g_ev")
                        if v % TB == TB - 1:
                            b = v // TB
                            r = slice(TB * b, TB * b + TB)
                            add(f[:, r, :], f[:, r, :], per_tile(v_("b2")[:, l * D:(l + 1) * D], TB))
                            if l + 1 < DEPTH:
                                send(b)
                            else:
                                add(wide["dev"][:, r, :], f[:, r, :], x[:, r, :], "result")

        @block.tensor
        def _(pe):
            M = nc.tensor.matmul

            def transposes(p, src, rows=P, tiles=range(T)):
                for t in tiles:
                    ins = nc.tensor.transpose(ps[0:rows, 6 + t // 4, (t % 4) * P:(t % 4) * P + P], src(t), ident)
                    if t % 4 == 3:
                        ins.then_inc(sem["turned"], 1)

            def project(p, lhs, rhs, n, chunks=1):
                for t in range(T):
                    if t % 4 == 0 and p != "f":
                        pe.wait_ge(sem["turned_copied"], 2 * TURN[p] + t // 4 + 1)
                    if t >= 6:
                        pe.wait_ge(sem["taken"], projected(p, t - 6))
                    for c in range(chunks):
                        ins = M(ps[:, t % 6, 0:n], lhs(t, c), rhs(c), start=(c == 0), stop=(c == chunks - 1))
                    ins.then_inc(sem["projected"], 1)

            def tile_T(t, c=0):
                return uT[:, t * P:(t + 1) * P]

            pe.wait_ge(sem["cst_in"], 16)
            nc.tensor.transpose(ps[:, 4, 0:P], cst[:, P:2 * P], ident).then_inc(sem["cmT"], 1)
            for b in range(B):
                pe.wait_ge(sem["cond_b"], b + 1)
                M(ps[:, 2 * b, :], cond_b[:, b, :], w_ada[:, 0:512], start=True, stop=True)
                M(ps[:, 2 * b + 1, 0:256], cond_b[:, b, :], w_ada[:, 512:768], start=True, stop=True)\
                    .then_inc(sem["adaP"], 1)
            pe.wait_ge(sem["u"], 1)
            transposes("a", lambda t: wide["u"][:, t, :])
            pe.wait_ge(sem["w_in"], 64)
            project("a", tile_T, lambda c: w_qkv[:, :], 3 * D)

            pe.wait_ge(sem["padsA"], 1)

            def group_T(G, bank, padq, padk, cols, name, id16, view):
                b, g = divmod(G, cols)
                for i, pad in enumerate((padq, padk)):
                    for tt in range(TB):
                        ins = nc.tensor.transpose(view[:, bank, i * 512 + tt * P:i * 512 + tt * P + P],
                                                  pad[:, TB * b + tt, g * P:(g + 1) * P], id16)
                ins.then_inc(sem[name], 1)

            def st_a(n):
                G, kt = divmod(n, TB)
                pe.wait_ge(sem["stagedA"], G + 1)
                for j in range(4):
                    if n >= 1 and j % 2 == 0:
                        pe.wait_ge(sem["expA"], 2 * (n - 1) + j // 2 + 1)
                    k = staged[32 * j:32 * j + 32, G % 2, 512 + kt * P:512 + kt * P + P]
                    ins = M(ps[:, j, :], k, staged[32 * j:32 * j + 32, G % 2, 0:512], start=True, stop=True)
                    if j % 2 == 1:
                        ins.then_inc(sem["stA"], 1)

            def pv_a(n):
                G, kt = divmod(n, TB)
                b, g = divmod(G, 4)
                pe.wait_ge(sem["expA"], 2 * n + 2)
                if kt == 0 and G >= 2:
                    pe.wait_ge(sem["oA"], G - 1)
                for j in range(4):
                    ins = M(ps[32 * j:32 * j + 32, 4 + G % 2, :], vA[:, TB * b + kt, 4 * g + j, :],
                            prob[:, n % 2, j * 512:j * 512 + 512], start=(kt == 0), stop=(kt == TB - 1))
                ins.then_inc(sem["pvA"], 1)

            def turn_back(bank, src, name):
                for tt in range(TB):
                    ins = nc.tensor.transpose(ps[:, bank, tt * P:tt * P + P], src[:, tt * P:tt * P + P], ident)
                ins.then_inc(sem[name], 1)

            def turn_back_a(G):
                pe.wait_ge(sem["oT_A"], G + 1)
                turn_back(4 + G % 2, oT[:, G % 2, :], "toA")

            group_T(0, 6, padq, padk, 4, "tA", ident16[:, :], ps16)
            for n in range(B * 4 * TB + 1):
                if n < B * 4 * TB:
                    st_a(n)
                    if n % TB == 1 and n // TB + 1 < 8:
                        group_T(n // TB + 1, 6 + (n // TB + 1) % 2, padq, padk, 4, "tA", ident16[:, :], ps16)
                if n >= 1:
                    pv_a(n - 1)
                if n % TB == 2 and n > TB:
                    turn_back_a(n // TB - 1)
            turn_back_a(7)
            pe.wait_ge(sem["oA"], 8)
            transposes("ao", lambda t: o_tok[:, t, :])
            project("ao", tile_T, lambda c: w_o[:, :], D)
            pe.wait_ge(sem["u"], 2)
            transposes("m", lambda t: wide["u"][:, t, :])
            project("m", tile_T, lambda c: w_f1[:, :], FF)
            pe.wait_ge(sem["h1"], 1)
            for g in range(8):
                if g >= 6:
                    pe.wait_ge(sem["h1_uT"], g - 5)
                for tt in range(4):
                    t = 4 * (g // 4) + tt
                    ins = nc.tensor.transpose(ps[:, g % 6, tt * P:(tt + 1) * P], hid1[:, t, (g % 4) * P:(g % 4) * P + P],
                                              ident)
                ins.then_inc(sem["h1_T"], 1)
            pe.wait_ge(sem["h1_uT"], 8)
            project("f", lambda t, c: hid1T[:, c, t * P:(t + 1) * P], lambda c: w_f2[:, c, :], D, 4)

            pe.wait_ge(sem["y"], 1)
            transposes("b", lambda t: wide["u"][:, t, :])
            pe.wait_ge(sem["w_quant"], 2)
            project("b", tile_T, lambda c: w_aq[:, :], 192)
            pe.wait_ge(sem["padsB"], 1)

            def s_b(n):
                G, j = divmod(n, 4)
                pe.wait_ge(sem["stagedB"], G + 1)
                for qt in range(4):
                    if n >= 1:
                        pe.wait_ge(sem["expB"], 4 * (n - 1) + qt + 1)
                    r = slice(32 * j, 32 * j + 2 * HQ)
                    ins = M(ps[:, qt, :], staged[r, (G % 4) % 2, qt * P:qt * P + P], staged[r, (G % 4) % 2, 512:1024],
                            start=True, stop=True)
                    if qt % 2 == 1:
                        ins.then_inc(sem["stB"], 1)

            def pt_b(m):
                pe.wait_ge(sem["quantB"], 4 * m + 4)
                c16 = codes.bitcast(F16)
                for kt in range(4):
                    if kt % 2 == 0 and m >= 1:
                        pe.wait_ge(sem["ptcB"], 2 * (m - 1) + kt // 2 + 1)
                    for qt in range(4):
                        c = (kt % 2) * 512 + qt * P
                        ins = nc.tensor.transpose(ps16[:, 4 + kt // 2, c:c + P],
                                                  c16[:, m % 2, qt, kt * P:(kt + 1) * P], ident16[:, :])
                    if kt % 2 == 1:
                        ins.then_inc(sem["ptB"], 1)

            def pv_b(m):
                b, h = divmod(m, H)
                pe.wait_ge(sem["ptcB"], 2 * m + 2)
                if h == 0 and b == 1:
                    pe.wait_ge(sem["outB"], 1)
                for qt in range(TB):
                    for kt in range(TB):
                        c = (qt * H + h) * (HQ + 1)
                        ins = M(ps[:, 6, c:c + HQ + 1], codesT[:, m % 2, kt, qt * P:(qt + 1) * P],
                                vB[:, TB * b + kt, h, :], start=(kt == 0), stop=(kt == TB - 1))
                ins.then_inc(sem["pvB"], 1)
            pe.wait_ge(sem["codes_high"], 1)
            for b in range(B):
                for n_ in range(H + 3):
                    n = b * H + n_
                    if n_ < H:
                        if n_ % 4 == 0:
                            if n // 4 >= 1:
                                pe.wait_ge(sem["stagedB"], n // 4)
                            group_T(n // 4, 7, padq, padk, 4, "tB", ident16[:, :], ps16)
                        s_b(n)
                    if 2 <= n_ < H + 2:
                        pt_b(n - 2)
                    if n_ >= 3:
                        pv_b(n - 3)
                pe.wait_ge(sem["ones16"], 1)
                for kt in range(TB):
                    ins = M(ps[:, 6, 320:320 + H * (HQ + 1)], ones16[:, :],
                            vB[:, TB * b + kt, :, :].rearrange("p h e -> p (h e)"), start=(kt == 0), stop=(kt == TB - 1))
                ins.then_inc(sem["pvB"], 1)
            pe.wait_ge(sem["zB"], 1)
            transposes("bo", lambda t: z[:, t, 0:64], 64)
            project("bo", lambda t, c: uT[0:64, t * P:(t + 1) * P], lambda c: w_ap[:, :], D)

            pe.wait_ge(sem["x2"], 1)
            for b in range(B):
                M(ps[:, b, 0:2 * D], cond_b[:, b, :], w_img[:, :], start=True, stop=True).then_inc(sem["imgP"], 1)
            transposes("c", lambda t: x[:, t, :])
            pe.wait_ge(sem["img"], 2)
            project("c", tile_T, lambda c: w_ca[:, :], 3 * D)
            pe.wait_ge(sem["padsC"], 1)
            pe.wait_ge(sem["cmask"], 1)

            def place(tile):
                return {3: (0, 0), 2: (1, 0), 0: (1, 384), 1: (2, 0)}[tile]

            stb = staged[:, :, :].bitcast(BF16)

            def s_c(n):
                G, j = divmod(n, 2)
                pe.wait_ge(sem["stagedC"], G + 1)
                if n >= 2:
                    pe.wait_ge(sem["maxC"], n - 1)
                st = stb
                r = slice(64 * j, 64 * j + 51)
                for qt in (3, 2, 0, 1):
                    bank, col = place(qt)
                    w = P * (qt + 1)
                    o = ps[:, 3 * (n % 2) + bank, col:col + w]
                    M(o, st[r, G % 2, qt * P:qt * P + P], st[r, G % 2, 512:512 + w], start=True, stop=False)
                    ins = M(o[:, w - P:w], identb[:, :], cmask[:, 0, :], start=False, stop=True)
                ins.then_inc(sem["sC"], 1)

            for n in range(B * H):
                if n % 2 == 0:
                    g = n // 2
                    group_T(g, 6 + g % 2, padqC, padkC, 8, "tC", identb[:, :], psb16)
                s_c(n)

            def st_c(n):
                G, j = divmod(n, 2)
                pe.wait_ge(sem["staged2C"], G + 1)
                if n >= 2:
                    pe.wait_ge(sem["expC"], n - 1)
                r = slice(64 * j, 64 * j + 54)
                for i in (3, 2, 0, 1):
                    kt = 3 - i
                    bank, col = place(i)
                    w = P * (i + 1)
                    o = ps[:, 3 * (n % 2) + bank, col:col + w]
                    M(o, stb[r, G % 2, 512 + kt * P:512 + kt * P + P], stb[r, G % 2, kt * P:512], start=True, stop=False)
                    ins = M(o[:, 0:P], identb[:, :], cmask[:, 1, :], start=False, stop=True)
                ins.then_inc(sem["stC"], 1)

            def pv_c(m):
                b = 2 * m // H
                pe.wait_ge(sem["expC"], 2 * m + 2)
                if m % 2 == 0 and m:
                    pe.wait_ge(sem["oT_C"], m // 2)
                for kt in range(TB):
                    bank, col = place(3 - kt)
                    a = 512 * bank + col
                    for n in (2 * m, 2 * m + 1):
                        j = n % 4
                        ins = M(ps[32 * j:32 * j + 32, 6, P * kt:512], vC[:, TB * b + kt, n % H, :],
                                probC[:, n % 4, a:a + 512 - P * kt], start=(kt == 0), stop=(kt == TB - 1))
                ins.then_inc(sem["pvC"], 1)

            def group_2(m):
                group_T(m, 7, padqC, padkC, 8, "t2C", identb[:, :], psb16)

            pe.wait_ge(sem["mC"], 1)
            group_2(0)
            PAIRS = B * H // 2
            for m in range(PAIRS + 2):
                if m < PAIRS:
                    st_c(2 * m)
                    st_c(2 * m + 1)
                if m % 2 == 1 and m >= 3:
                    pe.wait_ge(sem["oT_C"], m // 2)
                    turn_back(7, oT[:, (m // 2 - 1) % 2, :], "toC")
                if 1 <= m <= PAIRS:
                    pv_c(m - 1)
                if m + 1 < PAIRS:
                    if m % 2 == 1 and m >= 3:
                        pe.wait_ge(sem["oC"], m // 2)
                    pe.wait_ge(sem["staged2C"], m + 1)
                    group_2(m + 1)
            pe.wait_ge(sem["ocn"], 2)
            transposes("co", lambda t: o_tok[:, t, :])
            project("co", tile_T, lambda c: w_cp[:, :], D)
            pe.wait_ge(sem["w3_in"], 16 * 5 * DEPTH)
            pe.wait_ge(sem["dmask"], 1)
            for l in range(DEPTH):
                for t in range(T):
                    if t % TB == 0:
                        b = t // TB
                        pe.wait_ge(sem[f"shifted{b}"], 32 * (2 * l + 1))
                        pe.wait_ge(sem["f_ready"], B * 2 * l + b + 1)
                        if l:
                            pe.wait_ge(sem["g_ev"], T * l - 1 + b)
                        transposes(f"d{l}", lambda t: wide["x1"][:, t, :], tiles=range(TB * b, TB * b + TB))
                        pe.wait_ge(sem["turned_copied"], 2 * TURN[f"d{l}"] + b + 1)
                        if l == 0:
                            pe.wait_ge(sem["taken"], projected("co", T - 1))
                    if t >= 2:
                        pe.wait_ge(sem["d_sq"], T * l + t - 1)
                    for i in range(3):
                        ins = M(ps[:, 3 * (t % 2) + i, :], tile_T(t), w_d1[:, l, 512 * i:512 * i + 512], start=True, stop=True)
                    ins.then_inc(sem["d_mm"], 1)

                def turn_qk(b):
                    pe.wait_ge(sem[f"rope{b}"], l + 1)
                    if b == 0:
                        pe.wait_ge(sem["d_sq"], T * (l + 1))
                        pe.wait_ge(sem["turned_copied"], 2 * TURN[f"d{l}"] + 2)
                    for i in range(8):
                        if i >= 4:
                            pe.wait_ge(sem["qk_evV" if i % 2 else "qk_evA"], 4 * (B * l + b) + (i - 4) // 2 + 1)
                        for tt in range(TB):
                            c = 512 * (i // 4) + P * (i % 4)
                            ins = nc.tensor.transpose(ps[:, S_BANKS[i % 4], tt * P:(tt + 1) * P],
                                                      qkvD[:, TB * b + tt, c:c + P], ident)
                        ins.then_inc(sem["qkT_D"], 1)

                turn_qk(0)
                for b in range(B):
                    pe.wait_ge(sem["qk_evA"], 4 * (B * l + b + 1))
                    pe.wait_ge(sem["qk_evV"], 4 * (B * l + b + 1))
                    for u in range(TB * 4 + 3):
                        U = T * 4 * l + TB * 4 * b + u
                        if u == TB * 4 and b == 0:
                            pe.wait_ge(sem["expD"], 2 * U)
                            turn_qk(1)
                        if u < TB * 4:
                            t, pair = divmod(u, 4)
                            t += TB * b
                            k0 = P if t % TB == 0 else 0
                            if u >= 2:
                                pe.wait_ge(sem["expD"], 2 * (U - 1))
                            for j in range(2):
                                o = ps[:, 6 * (u % 2) + j, k0:256]
                                M(o, qTD[64 * j:64 * j + 64, pair, t * P:(t + 1) * P],
                                  kTD[64 * j:64 * j + 64, pair, (t - 1) * P + k0:(t + 1) * P], start=True, stop=False)
                                ins = M(o, identb[:, :], dmask[:, k0:256], start=False, stop=True)
                            ins.then_inc(sem["sD"], 1)
                        if 2 <= u < TB * 4 + 2:
                            v = u - 2
                            first = v < 4
                            pe.wait_ge(sem["normD"], U - 1)
                            if U >= 4:
                                pe.wait_ge(sem["ptcD"], U - 3)
                            for j in range(2):
                                for k in ((1,) if first else (0, 1)):
                                    c = 256 * j + P * k
                                    ins = nc.tensor.transpose(ps[:, 2 + v % 2, c:c + P],
                                                              prob_d(U - 2)[:, j, P * k:P * k + P], ident)
                            ins.then_inc(sem["ptD"], 1)
                        if u >= 3:
                            v = u - 3
                            t, pair = divmod(v, 4)
                            t += TB * b
                            pe.wait_ge(sem["ptcD"], U - 2)
                            if pair == 0 and T * l + t >= 2:
                                pe.wait_ge(sem["o_D"], T * l + t - 1)
                            ks = (1,) if t % TB == 0 else (0, 1)
                            for k in ks:
                                for j in range(2):
                                    hh = 2 * pair + j
                                    c = 256 * j + P * k
                                    ins = M(ps[64 * j:64 * j + 64, 4 + t % 2, P * pair:P * pair + P],
                                            qkvD[:, t - 1 + k, 1024 + DHD * hh:1024 + DHD * hh + DHD],
                                            probTD[:, v % 2, c:c + P], start=(k == ks[0]), stop=(k == 1))
                            ins.then_inc(sem["pvD"], 1)
                for t in range(T):
                    pe.wait_ge(sem["o_D"], T * l + t + 1)
                    if t >= 6:
                        pe.wait_ge(sem["do_ev"], T * l + t - 5)
                    for c in range(4):
                        ins = M(ps[:, DO_BANKS[t % 6], 0:D], oTD[:, c, t * P:(t + 1) * P], w_do[:, l, c, :], start=(c == 0), stop=(c == 3))
                    ins.then_inc(sem["do_mm"], 1)
                for t in range(T + 3):
                    if t < T:
                        if t in (0, 2):
                            b = t // 2
                            pe.wait_ge(sem["lnD"], B * l + b + 1)
                            transposes(f"e{l}", lambda t: wide["dev"][:, t, :], tiles=range(TB * b, TB * b + TB))
                        if t % TB == 0:
                            pe.wait_ge(sem["turned_copied"], 2 * TURN[f"e{l}"] + t // TB + 1)
                        if t >= 2:
                            pe.wait_ge(sem["e_ev"], T * l + t - 1)
                        for i in range(2):
                            ins = M(ps[:, 2 * (t % 2) + i, 0:HID], tile_T(t), w_h1[:, l, HID * i:HID * i + HID], start=True, stop=True)
                        ins.then_inc(sem["e_mm"], 1)
                    if 2 <= t < T + 2:
                        v = t - 2
                        pe.wait_ge(sem["hg"], T * l + v + 1)
                        if v >= 2:
                            pe.wait_ge(sem["g_uT"], 2 * (T * l + v - 1))
                        for c in range(3):
                            w = P if c < 2 else HID - 2 * P
                            ins = nc.tensor.transpose(ps[0:w, 4 + v % 2, c * P:(c + 1) * P], hgD[:, v, c * P:c * P + w], ident)
                        ins.then_inc(sem["g_T"], 1)
                    if t >= 3:
                        v = t - 3
                        pe.wait_ge(sem["g_uT"], 2 * (T * l + v + 1))
                        if v >= 2:
                            pe.wait_ge(sem["g_ev"], T * l + v - 1)
                        for c in range(3):
                            w = P if c < 2 else HID - 2 * P
                            ins = M(ps[:, 6 + v % 2, 0:D], hidTD[0:w, c, v * P:(v + 1) * P],
                                    w_h2[0:w, l, c, :], start=(c == 0), stop=(c == 2))
                        ins.then_inc(sem["g_mm"], 1)


def rope_tables():
    f = np.float32
    half = np.arange(0, DHD, 2, dtype=f)
    inv = (f(1.0) / (f(10000.0) ** (half / f(DHD)))).astype(f)
    t = np.arange(S, dtype=f)
    freqs = (t[:, None] * inv[None, :]).astype(f)
    base = ((half + f(0.4 * DHD)) / f(1.4 * DHD)).astype(f)
    power = ((t - f(S // 2)) / f(WINDOW // 2)).astype(f)
    scale = (base[None, :] ** power[:, None]).astype(f)
    cos, sin = np.cos(freqs), np.sin(freqs)

    def both(a, b):
        return np.concatenate([a, b], axis=1).astype(f)
    return np.stack([both(cos * scale, cos * scale), both(-sin * scale, sin * scale),
                     both(cos / scale, cos / scale), both(-sin / scale, sin / scale)])


def masks():
    i = np.arange(P)[:, None]
    causal = np.where(np.arange(P)[None, :] > i, NEG_C, 0.0)
    j = np.arange(256)[None, :] - P
    band = np.where((j > i) | (j < i - WINDOW), NEG_D, 0.0)
    return np.concatenate([np.eye(P), causal, band], axis=1).astype(np.float32)


def lay_out(i):
    a = {k: np.asarray(v) for k, v in i.items()}
    c, q, e, f = "L0_cond_", "L0_attn_", "L0_cond2_", "L0_ffn_"
    parts = {
        "b_ada": a[c + "b_ada"], "b_qkv": np.concatenate([a[c + "b_q"], a[c + "b_k"], a[c + "b_v"]]),
        "b_o": a[c + "b_o"], "b_f1": a[c + "b_f1"], "b_f2": a[c + "b_f2"],
        "c_attn_b": a[e + "c_attn_b"], "c_proj_b": a[e + "c_proj_b"], "uk_b": a[e + "uk_b"], "uv_b": a[e + "uv_b"],
    }
    for n in ("qkv_alpha", "proj_alpha", "proj_b", "bias_q", "bias_k", "q_alpha", "k_alpha", "v_alpha", "q_zp", "k_zp",
              "v_zp", "attn_alpha", "attn_zp"):
        parts[n] = a[q + n]
    for n in ("q_scale", "k_scale", "ln_g", "ln_b", "b1", "b2"):
        parts[n] = a[f + n]
    return {
        "x": a["x"], "condT": a["cond_1024"].T, "maskT": a["mask_Bx1x1xS_ff0"].reshape(T, P).T,
        "vec": np.concatenate([parts[n].reshape(-1) for n, _ in VECTORS])[None, :],
        "cst": masks(), "rope": rope_tables(),
        "w_ada": a[c + "w_ada"], "w_qkv": np.concatenate([a[c + "w_q"], a[c + "w_k"], a[c + "w_v"]], axis=1),
        "w_o": a[c + "w_o"], "w_f1": a[c + "w_f1"], "w_f2": a[c + "w_f2"],
        "w_aqT": a[q + "qkv_w"].T, "w_apT": a[q + "proj_w"].T, "w_ca": a[e + "c_attn_w"], "w_cp": a[e + "c_proj_w"],
        "w_imgT": np.concatenate([a[e + "uk_w"].T, a[e + "uv_w"].T], axis=1),
        "wqkv": a[f + "wqkv"], "wo": a[f + "wo"], "w1": a[f + "w1"], "w2": a[f + "w2"],
    }


def kernel(**inputs):
    import concourse.bacc as bacc
    from concourse.bass_utils import run_bass_kernel_spmd
    arrays = {"in_" + n: np.ascontiguousarray(a) for n, a in lay_out(inputs).items()}
    nc = bacc.Bacc("TRN2", target_bir_lowering=False, num_devices=1)
    d = {n[3:]: nc.dram_tensor(n, a.shape, F32, kind="ExternalInput").ap() for n, a in arrays.items()}
    out = nc.dram_tensor("out", (B, S, D), F32, kind="ExternalOutput").ap()
    build(nc, d, out)
    return run_bass_kernel_spmd(nc, [arrays], core_ids=[0]).results[0]["out"]
```

```python
from contextlib import ExitStack

import numpy as np
import concourse.bass as bass
from concourse import mybir

F32 = mybir.dt.float32
F16 = mybir.dt.float16
BF16 = mybir.dt.bfloat16
U8 = mybir.dt.uint8
U16 = mybir.dt.uint16
ALU = mybir.AluOpType
ACT = mybir.ActivationFunctionType
X = mybir.AxisListType.X

P = 128
B, S, D = 2, 512, 128
TB = S // P
T = B * TB
H = 16
HD = D // H
HQ = D // 2 // H
FF = 512
EPS = 1e-7
MAX_TANH = float(np.float32(1.0 - 1e-5))
REACH = float(np.arctanh(np.float64(np.float32(1.0 - 1e-5))))
SERIES_BELOW = 0.3
DH, DHD, WINDOW, DEPTH = 8, 64, 64, 2
INNER = DH * DHD
HID = int(D * 4 * 2 / 3)
ROUND = 12582912.0
U_ZERO = 1152.0
NEG_C = -30000.0
NEG_D = -1e30


def lgamma_beta(a, b):
    import math
    return math.exp(math.lgamma(a) + math.lgamma(b) - math.lgamma(a + b))


HEAD_SCALE = lgamma_beta(HD / 2, 0.5) / lgamma_beta(D / 2, 0.5)

VECTORS = [
    ("b_ada", 6 * D), ("b_qkv", 3 * D), ("b_o", D), ("b_f1", FF), ("b_f2", D),
    ("qkv_alpha", 3 * D // 2), ("proj_alpha", D), ("proj_b", D),
    ("bias_q", H), ("bias_k", H), ("q_alpha", H), ("k_alpha", H), ("v_alpha", H),
    ("q_zp", H), ("k_zp", H), ("v_zp", H), ("attn_alpha", H), ("attn_zp", H),
    ("c_attn_b", 3 * D), ("c_proj_b", D), ("uk_b", D), ("uv_b", D),
    ("q_scale", DEPTH * DHD), ("k_scale", DEPTH * DHD), ("ln_g", DEPTH * D), ("ln_b", DEPTH * D),
    ("b1", DEPTH * 2 * HID), ("b2", DEPTH * D),
]
AT, _n = {}, 0
for _name, _len in VECTORS:
    AT[_name] = (_n, _len)
    _n += _len
NVEC = _n


def build(nc, d, out):
    with ExitStack() as ctx:
        def sb(name, shape, dt=F32):
            return ctx.enter_context(nc.sbuf_tensor(name, shape, dt))

        class Semaphores(dict):
            def __missing__(self, name):
                self[name] = ctx.enter_context(nc.semaphore(name))
                return self[name]

        sem = Semaphores()
        count = {}

        def signal(ins, name, n=1):
            count[name] = count.get(name, 0) + n
            ins.then_inc(sem[name], n)
            return count[name]

        ps = ctx.enter_context(nc.psum_tensor("ps", [P, 8, 512], F32))
        ps16 = ps[:, :, :].bitcast(F16)
        psb16 = ps[:, :, :].bitcast(BF16)
        vec = sb("vec", [P, NVEC])
        x = sb("x_tok", [P, T, D])
        cst = sb("cst", [P, 2 * P + 256])
        ident = cst[:, 0:P]
        ident16 = sb("ident16", [P, P], F16)
        identb = sb("identb", [P, P], BF16)
        cmask = sb("cmask", [P, P], BF16)
        dmask = sb("dmask", [P, 256], BF16)
        ones16 = sb("ones16", [P, P], F16)
        rope = sb("rope", [P, 4, TB, DHD])
        primed = sb("primed", [P, 8])
        condT = sb("condT", [P, B])
        cond_b = sb("cond_b", [P, B, P])
        maskT = sb("maskT", [P, T])
        uT = sb("uT", [P, T * P])
        wide = {n: sb(n, [P, T, D]) for n in ("x1", "sq", "dev", "u")}
        staged = sb("staged", [P, 2, 1024], F16)
        o_tok = sb("o_tok", [P, T, D])
        small = {}

        def sm(name, n=T):
            if name not in small:
                small[name] = sb("s_" + name, [P, n])
            return small[name][:, :]

        arena = sb("arena", [P, 26624])
        used = [0]

        def carve(shape, dt=F32, start=None):
            n = int(np.prod(shape))
            words = n if dt == F32 else n // 2
            if start is not None:
                used[0] = start
            a = arena[:, used[0]:used[0] + words]
            used[0] += words
            assert used[0] <= 26624
            if dt != F32:
                a = a.bitcast(dt)
            names = "abcdef"[:len(shape)]
            if len(shape) > 1:
                a = a.rearrange(f"p ({' '.join(names)}) -> p {' '.join(names)}", **dict(zip(names, shape)))
            return a

        z = carve([T, 3 * D], start=0)
        zsq = carve([T, 3 * D])
        after_z = used[0]
        padq = carve([T, H * 32], F16)
        padk = carve([T, H * 32], F16)
        prob = carve([2, 2048])
        vB = carve([T, H, HQ + 1], F16)
        vA = carve([T, H, 32])
        codes = carve([4, 4, 512], U16, start=used[0] - T * H * 32)
        oT = carve([2, 512])
        outB = carve([T, H * (HQ + 1)])
        before_w = used[0]
        w_ada = carve([6 * D])
        w_qkv = carve([3 * D])
        w_o = carve([D])
        w_f1 = carve([FF])
        w_f2 = carve([FF // P, D])
        w_aq = carve([3 * D // 2])
        w_ap = carve([D])[0:D // 2, :]
        w_ca = carve([3 * D])
        w_cp = carve([D])
        w_img = carve([2 * D])
        ada = carve([B, 6 * D])
        img = carve([B, 2 * D])
        codesT = carve([2, 4, 512], F16, start=T * 3 * D)
        hid1 = carve([T, FF], start=0)
        zF = arena[:, 0:T * D].rearrange("p (t c) -> p t c", t=T)
        hid1T = carve([4, T * P])
        padqC = carve([T, H * 64], BF16, start=after_z)
        padkC = carve([T, H * 64], BF16)
        vC = carve([T, H, 32])
        probTC_V = carve([4, 256], start=0)
        outC = carve([TB, H, HD + 1], start=T * 3 * D)
        probC = carve([2, 1280], start=before_w)

        qkvD = carve([T, 3 * INNER], start=0)
        qTD = carve([INNER // P, T * P])
        kTD = carve([INNER // P, T * P])
        oTD = carve([INNER // P, T * P])
        sqD = oTD.rearrange("p a b -> p (a b)").rearrange("p (n c) -> p n c", n=TB)
        probTD = carve([2, 512])
        hidD = carve([T, 2 * HID], start=0)
        hgD = carve([T, HID])
        hidTD = carve([3, T * P], start=8192)
        w_d1 = sb("w_d1", [P, DEPTH, 3 * INNER])
        w_do = sb("w_do", [P, DEPTH, INNER // P, D])
        w_h1 = sb("w_h1", [P, DEPTH, 2 * HID])
        w_h2 = sb("w_h2", [P, DEPTH, 3, D])
        ropeL = sb("ropeL", [P, 4, TB, DHD])

        TURN = {n: i for i, n in enumerate(("a", "ao", "m", "b", "bo", "c", "co", "d0", "e0", "d1", "e1"))}
        PROJECTION = {n: i for i, n in enumerate(("a", "ao", "m", "f", "b", "bo", "c", "co"))}
        BLOCK = {"a": 0, "m": 1}

        def projected(p, t):
            return T * PROJECTION[p] + t + 1

        def v_(name):
            a, n = AT[name]
            return vec[:, a:a + n]

        def copy_codes(copy, m, half):
            return copy(codesT[:, m % 2, 2 * half:2 * half + 2, :],
                        ps16[:, 4 + half, 0:1024].rearrange("p (a b) -> p a b", a=2))

        Q_SLOTS = ((0, 8, 16), (24, 32), (40,))
        K_SLOTS = ((0, 24, 40), (8, 32), (16,))

        def twice_a(engine, b, copy):
            for i, (pad, pairs) in enumerate(((padq, ((0, 1), (2, 3))), (padk, ((0, 2), (1, 3))))):
                a = pad[:, TB * b:TB * b + TB, :].rearrange("p t (h s e) -> p t h s e", s=4, e=HD)
                for (src, dst), name in zip(pairs, ("highA", "lowA")):
                    engine.wait_ge(sem[name], 2 * b + i + 1)
                    copy(a[:, :, :, dst, :], a[:, :, :, src, :]).then_inc(sem[f"twiceA{b}"], 1)

        def keys_and_values_b(engine, b, copy):
            r = slice(TB * b, TB * b + TB)
            engine.wait_ge(sem["roundedB"], b + 1)
            k, v = (z[:, r, c:c + 64].rearrange("p t (h e) -> p t h e", e=HQ) for c in (64, 128))
            pads = padk[:, r, :].rearrange("p t (h s e) -> p t h s e", s=8, e=HQ)
            for i in range(2):
                copy(pads[:, :, :, i, :], k).then_inc(sem[f"kvB{b}"], 1)
            copy(vB[:, r, :, 0:HQ], v).then_inc(sem[f"kvB{b}"], 1)

        def prob_t(n):
            return wide[("sq", "dev", "x1", "u")[n % 4]][:, :, :].rearrange("p t c -> p (t c)")

        def again_c(engine, b, copy):
            for k, (pad, slots) in enumerate(((padqC, Q_SLOTS), (padkC, K_SLOTS))):
                a = pad[:, TB * b:TB * b + TB, :].rearrange("p t (h s) -> p t h s", h=H)
                for i in range(2):
                    engine.wait_ge(sem["partC"], 6 * b + 3 * k + i + 1)
                    first = slots[i][0]
                    for c in slots[i][1:]:
                        copy(a[:, :, :, c:c + HD], a[:, :, :, first:first + HD]).then_inc(sem[f"againC{b}"], 1)

        def place(tile):
            return {3: (0, 0), 2: (1, 0), 0: (1, 384), 1: (2, 0)}[tile]

        def at(tile):
            bank, col = place(tile)
            return 512 * bank + col

        nmx, simg, eimg = (sm(n, T * H).rearrange("p (t h) -> p t h", h=H) for n in ("nmx", "simg", "eimg"))

        S_BANKS = (0, 1, 6, 7)
        devL = o_tok[:, :, :]
        sqL = staged[:, :, :].bitcast(F32).rearrange("p a (b c) -> p (a b) c", c=D)

        def evacuate_qk(copy, b, i):
            return copy((qTD, kTD)[i // 4][:, i % 4, b * 512:b * 512 + 512], ps[:, S_BANKS[i % 4], :])

        def prob_d(U):
            a = (wide["sq"], wide["dev"])[U // 2 % 2][:, 4 * (U % 2):4 * (U % 2) + 4, :]
            return a.rearrange("p t c -> p (t c)").rearrange("p (j k) -> p j k", j=2)

        def rope_terms(engine, t0, n, i, t1, t2, step):
            q = qkvD[:, t0:t0 + n, 512 * i:512 * i + 512].rearrange("p t (h c) -> p t h c", h=DH)

            def tab(k, a, w):
                return ropeL[:, k, t0 % TB:t0 % TB + n, a:a + w].unsqueeze(2).to_broadcast([P, n, DH, w])
            step(engine.tensor_tensor(t1, q, tab(2 * i, 0, 64), ALU.mult))
            step(engine.tensor_tensor(t2[:, :, :, 0:32], q[:, :, :, 32:64], tab(2 * i + 1, 0, 32), ALU.mult))
            step(engine.tensor_tensor(t2[:, :, :, 32:64], q[:, :, :, 0:32], tab(2 * i + 1, 32, 32), ALU.mult))
            return engine.tensor_tensor(q if i == 0 else t1, t1, t2, ALU.add)

        def scale_k(engine, t0, n, t1):
            k = qkvD[:, t0:t0 + n, 512:1024].rearrange("p t (h c) -> p t h c", h=DH)
            factor = sm("dn", 16 * T)[:, 16 * t0:16 * t0 + 16 * n].rearrange("p (t k h) -> p t k h", t=n, k=2)[:, :, 1, :]
            return engine.tensor_tensor(k, t1, factor.unsqueeze(3).to_broadcast([P, n, DH, DHD]), ALU.mult)

        def per_tile(a, n=T):
            return a.unsqueeze(1).to_broadcast([P, n, a.shape[1]])

        def per_row(a, k=D):
            return a.unsqueeze(2).to_broadcast([P, a.shape[1], k])

        block = ctx.enter_context(nc.Block())

        @block.sync
        def _(sp):
            def load(dst, src, name):
                sp.dma_start(dst, src).then_inc(sem[name], 16)
            load(x[:, :, :], d["x"].rearrange("b (t p) c -> p (b t) c", p=P), "x_in")
            load(condT[:, :], d["condT"], "ada_in")
            load(w_ada[:, :], d["w_ada"], "ada_in")
            load(cst[:, :], d["cst"], "cst_in")
            a = AT["qkv_alpha"][0]
            load(vec[:, 0:a], d["vec"][0, 0:a].partition_broadcast(P), "vec_in")
            load(w_qkv[:, :], d["w_qkv"], "w_in")
            load(w_o[:, :], d["w_o"], "w_in")
            load(w_f1[:, :], d["w_f1"], "w_in")
            load(w_f2[:, :, :], d["w_f2"].rearrange("(c p) n -> p c n", p=P), "w_in")
            load(vec[:, a:NVEC], d["vec"][0, a:NVEC].partition_broadcast(P), "vec2_in")
            load(w_aq[:, :], d["w_aqT"], "w2_in")
            load(w_ap[:, :], d["w_apT"], "w2_in")
            load(w_ca[:, :], d["w_ca"], "w2_in")
            load(w_cp[:, :], d["w_cp"], "w2_in")
            load(w_img[:, :], d["w_imgT"], "w2_in")
            load(maskT[:, :], d["maskT"], "w2_in")
            load(rope[:, :, :, :], d["rope"].rearrange("k (t p) c -> p k t c", p=P), "w2_in")
            for l in range(DEPTH):
                load(w_d1[:, l, :], d["wqkv"][l], "w3_in")
                load(w_do[:, l, :, :], d["wo"][l].rearrange("(c p) n -> p c n", p=P), "w3_in")
                load(w_h1[:, l, :], d["w1"][l], "w3_in")
                load(w_h2[:, l, 0:2, :], d["w2"][l, 0:2 * P].rearrange("(c p) n -> p c n", p=P), "w3_in")
                load(w_h2[0:HID - 2 * P, l, 2, :], d["w2"][l, 2 * P:HID], "w3_in")
            for k in range(2 * DEPTH):
                for b in range(B):
                    sp.wait_ge(sem["f_ready"], B * k + b + 1)
                    h, f = wide["x1"], wide["u"]
                    t0, t1 = TB * b, TB * b + TB
                    load(h[1:P, t0:t1, 64:D], f[0:P - 1, t0:t1, 64:D], f"shifted{b}")
                    load(h[0:1, t0 + 1:t1, 64:D], f[P - 1:P, t0:t1 - 1, 64:D], f"shifted{b}")
            for b in range(B):
                sp.wait_ge(sem["result"], b + 1)
                load(out[b].rearrange("(t p) c -> p t c", p=P), wide["dev"][:, TB * b:TB * b + TB, :], "stored")
            sp.wait_ge(sem["stored"], 16 * B)

        @block.gpsimd
        def _(pool):
            def step(ins, name="pool_step"):
                pool.wait_ge(sem[name], signal(ins, name))
            nc.gpsimd.memset(ones16[:, :], 1.0).then_inc(sem["ones16"], 1)
            nc.gpsimd.memset(padq, 0.0).then_inc(sem["pads_clear"], 1)
            nc.gpsimd.memset(padk, 0.0).then_inc(sem["pads_clear"], 1)
            nc.gpsimd.memset(vA, 0.0).then_inc(sem["vA_zeros"], 1)
            pool.wait_ge(sem["vA_zeros"], 1)
            nc.gpsimd.memset(vA[:, :, :, HD:HD + 1], 1.0).then_inc(sem["vA_ones"], 1)
            nc.gpsimd.memset(vB[:, :, :, HQ:HQ + 1], 1.0).then_inc(sem["vB_ones"], 1)
            for b in range(B):
                pool.wait_ge(sem["hfA"], b + 1)
                r = slice(TB * b, TB * b + TB)
                nc.gpsimd.tensor_tensor(vA[:, r, :, 0:HD], z[:, r, 2 * D:3 * D].rearrange("p t (h e) -> p t h e", e=HD),
                                        sm("one", T * H).rearrange("p (t h) -> p t h", h=H)[:, r, :].unsqueeze(3)
                                        .to_broadcast([P, TB, H, HD]), ALU.mult).then_inc(sem["vA"], 1)
            twice_a(pool, 1, nc.gpsimd.tensor_copy)
            pool.wait_ge(sem["pvA"], B * 4 * TB)
            nc.gpsimd.memset(codes.bitcast(U16), 0x6400).then_inc(sem["codes_high"], 1)
            nc.gpsimd.memset(padk, 0.0).then_inc(sem["pads_clear"], 1)
            pool.wait_ge(sem["projected"], projected("f", T - 1))
            nc.gpsimd.memset(padq, 0.0).then_inc(sem["pads_clear"], 1)
            pool.wait_ge(sem["codes_high"], 1)
            u8 = codes.bitcast(U8).rearrange("p n t (k c) -> p n t k c", c=2)
            for n in range(B * H):
                if n == 7:
                    keys_and_values_b(pool, 1, nc.gpsimd.tensor_copy)
                pool.wait_ge(sem["rB"], n + 1)
                if n >= 4:
                    pool.wait_ge(sem["ptB"], 2 * (n - 3))
                for j in range(4):
                    c = 4 * (n % 2) + j
                    h = 4 * (n // TB % 4) + j
                    nc.gpsimd.tensor_scalar(u8[:, n % 4, j, :, 0], prob[:, n % 2, j * 512:j * 512 + 512],
                                            sm("rB", 8)[:, c:c + 1], sm("zpu", H)[:, h:h + 1],
                                            ALU.mult, ALU.add).then_inc(sem["quantB"], 1)
            pool.wait_ge(sem["colsumB"], B)
            nc.gpsimd.memset(padqC.rearrange("p t (h s) -> p t h s", h=H)[:, :, :, 48:64], 1.0)\
                .then_inc(sem["padsC_clear"], 1)
            nc.gpsimd.memset(padkC.rearrange("p t (h s) -> p t h s", h=H)[:, :, :, 51:64], 0.0)\
                .then_inc(sem["padsC_clear"], 1)
            nc.gpsimd.memset(vC[:, :, :, HD + 1:32], 0.0).then_inc(sem["padsC_clear"], 1)
            nc.gpsimd.memset(vC[:, :, :, HD:HD + 1], 1.0).then_inc(sem["padsC_clear"], 1)
            pk = padkC.rearrange("p t (h s) -> p t h s", h=H)
            pool.wait_ge(sem["w2_in"], 16 * 7)
            mask = maskT[:, :].unsqueeze(2).unsqueeze(3).to_broadcast([P, T, H, 1])
            left = sm("mask_left", T * H).rearrange("p (t h e) -> p t h e", t=T, h=H)
            for i in range(3):
                step(nc.gpsimd.tensor_copy(pk[:, :, :, 48 + i:49 + i], mask if i == 0 else left), "maskC")
                if i < 2:
                    step(nc.gpsimd.tensor_tensor(left, mask if i == 0 else left, pk[:, :, :, 48 + i:49 + i], ALU.subtract))
            pool.wait_ge(sem["padsC_clear"], 4)
            for b in range(B):
                pool.wait_ge(sem["qC"], b + 1)
                r = slice(TB * b, TB * b + TB)
                nc.gpsimd.tensor_tensor(zsq[:, r, D:2 * D], z[:, r, 0:D], per_tile(img[:, b, 0:D], TB), ALU.mult)\
                    .then_inc(sem["zimg"], 1)
                nc.gpsimd.tensor_copy(vC[:, r, :, 0:HD], z[:, r, 2 * D:3 * D].rearrange("p t (h e) -> p t h e", e=HD))\
                    .then_inc(sem["vC"], 1)
            again_c(pool, 1, nc.gpsimd.tensor_copy)
            r1 = o_tok[:, :, :].rearrange("p t c -> p (t c)").rearrange("p (t h c) -> p t h c", t=2, h=DH)
            r2 = staged[:, :, :].bitcast(F32).rearrange("p a b -> p (a b)").rearrange("p (t h c) -> p t h c", t=2, h=DH)
            for l in range(DEPTH):
                pool.wait_ge(sem["ropeL"], l + 1)
                for c in range(4):
                    pool.wait_ge(sem["d_sq"], T * l + 2 * c + 2)
                    step(rope_terms(nc.gpsimd, 2 * c, 2, 0, r1, r2, step), "ropeQ")
                pool.wait_ge(sem["d_dn"], B * l + 2)
                for c in (2, 3):
                    step(rope_terms(nc.gpsimd, 2 * c, 2, 1, r1, r2, step))
                    step(scale_k(nc.gpsimd, 2 * c, 2, r1), "rope1")

        @block.scalar
        def _(act):
            loads = []

            def load_table(function):
                loads.append(function)
                k = len(loads) - 1
                nc.scalar.activation(primed[:, k:k + 1], ones16[:, 0:1], function)

            def squares(src, t, out, name):
                nc.scalar.activation(wide["sq"][:, t, :], src[:, t, :], ACT.Square, accum_out=sm(out)[:, t:t + 1])\
                    .then_inc(sem[name], 1)

            def logmap_norm(p, src, source, value):
                n = BLOCK[p]
                for t in range(T):
                    act.wait_ge(sem[source], value(t))
                    squares(src, t, p + "n2", "n2")
                act.wait_ge(sem["n2"], T * (n + 1))
                nc.scalar.activation(sm("n"), sm(p + "n2"), ACT.Sqrt).then_inc(sem["n"], 1)
                load_table(ACT.Ln)
                act.wait_ge(sem["dev"], n + 1)
                for t in range(T):
                    squares(wide["dev"], t, "dev2", "dev2")
                act.wait_ge(sem["ratio"], n + 1)
                nc.scalar.activation(sm("ln"), sm("ratio"), ACT.Ln).then_inc(sem["ln"], 1)
                act.wait_ge(sem["var"], n + 1)
                nc.scalar.activation(sm("std"), sm("var"), ACT.Sqrt).then_inc(sem["std"], 1)
                for b in range(B):
                    act.wait_ge(sem["u"], B * n + b + 1)
                    for t in range(TB * b, TB * b + TB):
                        squares(wide["u"], t, "u2", "u2")
                    if b == 0:
                        copy_half(p, 0)
                act.wait_ge(sem["u2"], T * (n + 1))
                nc.scalar.activation(sm("un"), sm("u2"), ACT.Sqrt).then_inc(sem["un"], 1)
                copy_half(p, 1)

            def copy_half(p, half, rows=P):
                act.wait_ge(sem["turned"], 2 * TURN[p] + half + 1)
                nc.scalar.activation(uT[0:rows, half * 512:half * 512 + 512], ps[0:rows, 6 + half, :], ACT.Copy)\
                    .then_inc(sem["turned_copied"], 1)

            def copy_T(p, rows=P):
                for half in range(2):
                    copy_half(p, half, rows)

            def mobius(p, src, zin, projection):
                n = BLOCK[p]
                for t in range(T):
                    act.wait_ge(sem["taken"], projected(projection, t))
                    squares(zin, t, "z2", "z2")
                act.wait_ge(sem["z2"], T * (n + 1))
                nc.scalar.activation(sm("zn"), sm("z2"), ACT.Sqrt).then_inc(sem["zn"], 1)
                for b in range(B):
                    act.wait_ge(sem["w"], B * n + b + 1)
                    for t in range(TB * b, TB * b + TB):
                        squares(wide["dev"], t, "dev2", "wsq")
                act.wait_ge(sem["w2"], n + 1)
                nc.scalar.activation(sm("wn"), sm("w2"), ACT.Sqrt).then_inc(sem["wn"], 1)
                act.wait_ge(sem["wc"], n + 1)
                nc.scalar.activation(sm("th"), sm("wc"), ACT.Tanh).then_inc(sem["th"], 1)
                load_table(ACT.Sqrt if p == "a" else ACT.Exp)
                act.wait_ge(sem["sf"], n + 1)
                for t in range(T):
                    nc.scalar.activation(wide["sq"][:, t, :], src[:, t, :], ACT.Copy, scale=sm("xy")[:, t:t + 1])\
                        .then_inc(sem["scaled"], 1)

            act.wait_ge(sem["ones16"], 1)
            load_table(ACT.Sqrt)
            logmap_norm("a", x, "x_in", lambda t: 16)
            for t in range(T):
                act.wait_ge(sem["taken"], projected("a", t))
                nc.scalar.activation(zsq[:, t, :], z[:, t, :], ACT.Square).then_inc(sem["zsqA"], 1)
            for b in range(B):
                act.wait_ge(sem["z2A"], b + 1)
                for name, sq, k in (("hn", "h2", 3 * H), ("rn", "r2", 3)):
                    r = slice(k * TB * b, k * TB * (b + 1))
                    nc.scalar.activation(sm(name, k * T)[:, r], sm(sq, k * T)[:, r], ACT.Sqrt).then_inc(sem["hnA"], 1)
            twice_a(act, 0, lambda o, a: nc.scalar.activation(o, a, ACT.Copy))
            for n in range(B * 4 * TB):
                for half in range(2):
                    act.wait_ge(sem["stA"], 2 * n + half + 1)
                    if n >= 2:
                        act.wait_ge(sem["pvA"], n - 1)
                    nc.scalar.activation(prob[:, n % 2, half * 1024:half * 1024 + 1024],
                                         ps[:, 2 * half:2 * half + 2, :], ACT.Exp,
                                         scale=HD ** -0.5).then_inc(sem["expA"], 1)
            load_table(ACT.Sqrt)
            copy_T("ao")
            mobius("a", x, z[:, :, 0:D], "ao")
            logmap_norm("m", wide["x1"], "x1", lambda t: t + 1)
            for half in range(2):
                for t in range(TB * half, TB * half + TB):
                    act.wait_ge(sem["taken"], projected("m", t))
                    if t >= 2:
                        act.wait_ge(sem["f2"], t - 1)
                    nc.scalar.activation(wide["sq"][:, 4 * (t % 2):4 * (t % 2) + 4, :].rearrange("p a b -> p (a b)"),
                                         hid1[:, t, :], ACT.Square, accum_out=sm("f2")[:, t:t + 1]).then_inc(sem["f2"], 1)
                for g in range(4 * half, 4 * half + 4):
                    act.wait_ge(sem["h1_T"], g + 1)
                    nc.scalar.activation(hid1T[:, g % 4, (g // 4) * 512:(g // 4) * 512 + 512],
                                         ps[:, 6 + g % 2, :], ACT.Copy).then_inc(sem["h1_uT"], 1)
            act.wait_ge(sem["f2"], T)
            nc.scalar.activation(sm("fn"), sm("f2"), ACT.Sqrt).then_inc(sem["fn"], 1)
            mobius("m", wide["x1"], zF, "f")
            copy_T("b")
            keys_and_values_b(act, 0, lambda o, a: nc.scalar.activation(o, a, ACT.Copy))

            def codes_half(m):
                act.wait_ge(sem["ptB"], 2 * m + 1)
                if m >= 2:
                    act.wait_ge(sem["pvB"], m - 1)
                copy_codes(lambda o, a: nc.scalar.activation(o, a, ACT.Copy), m, 0).then_inc(sem["ptcB0"], 1)
            for n in range(B * H):
                for j in range(4):
                    h = 4 * (n // TB % 4) + j
                    c = 4 * (n % 2) + j
                    if j % 2 == 0:
                        act.wait_ge(sem["maxB"], 2 * n + j // 2 + 1)
                    if n >= 2:
                        act.wait_ge(sem["quantB"], 4 * (n - 2) + j + 1)
                    nc.scalar.activation(prob[:, n % 2, j * 512:j * 512 + 512], ps[:, j, :], ACT.Exp,
                                         scale=sm("scB", H)[:, h:h + 1], bias=sm("nbB", 8)[:, c:c + 1],
                                         accum_out=sm("sumB", 8)[:, c:c + 1]).then_inc(sem["expB"], 1)
                    if j == 1 and n >= 3:
                        codes_half(n - 3)
            codes_half(B * H - 3)
            codes_half(B * H - 2)
            codes_half(B * H - 1)
            copy_T("bo", rows=D // 2)
            copy_T("c")
            again_c(act, 0, lambda o, a: nc.scalar.activation(o, a, ACT.Copy))
            for n in range(B * H + 1):
                b, h = divmod(n, H)
                if n < B * H:
                    for i, qt in enumerate((3, 2, 0, 1)):
                        if i < 2:
                            act.wait_ge(sem["maxC"], 2 * n + i + 1)
                        if n >= 2 and i == 0:
                            act.wait_ge(sem["ptC"], 2 * (n - 1))
                        bank, col = place(qt)
                        w = P * (qt + 1)
                        nc.scalar.activation(probC[:, n % 2, at(qt):at(qt) + w], ps[:, bank, col:col + w], ACT.Exp,
                                             bias=nmx[:, TB * b + qt, h:h + 1]).then_inc(sem["expC"], 1)
                if n >= 1:
                    m = n - 1
                    act.wait_ge(sem["ptC"], 2 * m + 1)
                    if m >= 4:
                        act.wait_ge(sem["pvC"], m // 2 - 1)
                    nc.scalar.activation(prob_t(m), ps[:, 3:5, :].rearrange("p a b -> p (a b)"), ACT.Copy).then_inc(sem["ptC_A"], 1)
                if n >= 1 and n % H == 0:
                    b = n // H - 1
                    act.wait_ge(sem["imx"], b + 1)
                    nc.scalar.activation(eimg[:, TB * b:TB * b + TB, :], simg[:, TB * b:TB * b + TB, :], ACT.Exp)\
                        .then_inc(sem["eimg"], 1)
            load_table(ACT.Sqrt)
            copy_T("co")
            for l in range(DEPTH):
                def squares_d(b):
                    r = slice(TB * b, TB * b + TB)
                    act.wait_ge(sem["devD"], B * l + b + 1)
                    nc.scalar.activation(sqL[:, r, :], devL[:, r, :], ACT.Square).then_inc(sem["lnsq"], 1)

                def roots_d(b):
                    r = slice(TB * b, TB * b + TB)
                    act.wait_ge(sem["lnvar"], B * l + b + 1)
                    nc.scalar.activation(sm("std")[:, r], sm("var")[:, r], ACT.Sqrt).then_inc(sem["lnstd"], 1)

                def turned_qk(b):
                    for i in (0, 2, 4, 6):
                        act.wait_ge(sem["qkT_D"], 8 * (B * l + b) + i + 1)
                        evacuate_qk(lambda o, a: nc.scalar.activation(o, a, ACT.Copy), b, i).then_inc(sem["qk_evA"], 1)
                for t in range(T):
                    if t in (0, 2):
                        copy_half(f"d{l}", t // 2)
                    act.wait_ge(sem["d_mm"], T * l + t + 1)
                    k = 3 * (t % 2)
                    nc.scalar.activation(qkvD[:, t, :], ps[:, k:k + 3, :].rearrange("p a b -> p (a b)"), ACT.Copy)\
                        .then_inc(sem["d_ev"], 1)
                    if t >= TB:
                        act.wait_ge(sem["d_ss"], T * l + t - 3)
                    act.wait_ge(sem["d_ev"], T * l + t + 1)
                    nc.scalar.activation(sqD[:, t % TB, :], qkvD[:, t, 0:2 * INNER], ACT.Square).then_inc(sem["d_sq"], 1)
                    if t in (TB, T - 1):
                        if t == T - 1:
                            turned_qk(0)
                        b = t // (T - 1)
                        act.wait_ge(sem["d_ss"], T * l + TB * (b + 1))
                        nc.scalar.activation(sm("dn", 16 * T)[:, 64 * b:64 * b + 64], sm("dss", 16 * T)[:, 64 * b:64 * b + 64],
                                             ACT.Sqrt).then_inc(sem["d_n"], 1)
                for b in range(B):
                    for u in range(TB * 4 + 2):
                        U = T * 4 * l + TB * 4 * b + u
                        if u == TB * 4 and b == 0:
                            turned_qk(1)
                        if u < TB * 4:
                            t, pair = divmod(u, 4)
                            first = t == 0
                            act.wait_ge(sem["maxD"], U + 1)
                            if U >= 4:
                                act.wait_ge(sem["ptD"], U - 3)
                            for j in range(2):
                                c = 2 * (U % 4) + j
                                h = 8 * (TB * b + t) + 2 * pair + j
                                k0 = P if first else WINDOW
                                nc.scalar.activation(prob_d(U)[:, j, k0:256], ps[:, 6 * (u % 2) + j, k0:256], ACT.Exp,
                                                     scale=sm("dq8", 8 * T)[:, h:h + 1], bias=sm("nbD", 8)[:, c:c + 1],
                                                     accum_out=sm("sumD", 8)[:, c:c + 1]).then_inc(sem["expD"], 1)
                        if b == 1 and u == 9:
                            squares_d(0)
                        if u >= 2:
                            v = u - 2
                            act.wait_ge(sem["ptD"], U - 1)
                            if U >= 4:
                                act.wait_ge(sem["pvD"], U - 3)
                            pt, bank = probTD[:, v % 2, :], ps[:, 2 + v % 2, :]
                            if v < 4:
                                pt, bank = (a.rearrange("p (a b) -> p a b", a=2)[:, :, P:256] for a in (pt, bank))
                            nc.scalar.activation(pt, bank, ACT.Copy).then_inc(sem["ptcD"], 1)
                roots_d(0)
                copy_half(f"e{l}", 0)
                for t in range(T + 1):
                    if t < T:
                        act.wait_ge(sem["e_g"], T * l + t + 1)
                        nc.scalar.activation(hidD[:, t, HID:2 * HID], hidD[:, t, HID:2 * HID], ACT.Gelu)\
                            .then_inc(sem["gelu"], 1)
                    if t == 3:
                        copy_half(f"e{l}", 1)
                    if t >= 1:
                        v = t - 1
                        act.wait_ge(sem["g_T"], T * l + v + 1)
                        for c in range(2):
                            rows, chunks = ((P, slice(0, 2)), (HID - 2 * P, slice(2, 3)))[c]
                            nc.scalar.activation(hidTD[0:rows, chunks, v * P:v * P + P],
                                                 ps[0:rows, 4 + v % 2, 256 * c:256 * c + (256, P)[c]]
                                                 .rearrange("p (a b) -> p a b", b=P), ACT.Copy).then_inc(sem["g_uT"], 1)
                    if t == 1:
                        squares_d(1)
                    if t == 2:
                        roots_d(1)

        @block.vector
        def _(dve):
            V = nc.vector

            def step(ins, name="dve_step"):
                dve.wait_ge(sem[name], signal(ins, name))

            def free(ins, name="dve_step"):
                signal(ins, name)

            def taken(t, ins):
                signal(ins, "taken")
                if t % TB == TB - 1:
                    dve.wait_ge(sem["taken"], count["taken"])

            def mul(o, a, b, name="dve_step"):
                step(V.tensor_tensor(o, a, b, ALU.mult), name)

            def add(o, a, b, name="dve_step"):
                step(V.tensor_tensor(o, a, b, ALU.add), name)

            def ts(o, a, s1, op1, s2=None, op2=None, name="dve_step"):
                if op2 is None:
                    step(V.tensor_scalar(o, a, s1, None, op1), name)
                else:
                    step(V.tensor_scalar(o, a, s1, s2, op1, op2), name)

            def stt(o, a, s1, b, op1, op2, name="dve_step"):
                step(V.scalar_tensor_tensor(out=o, in0=a, scalar=s1, in1=b, op0=op1, op1=op2), name)

            def total(o, a, name="dve_step"):
                step(V.tensor_reduce(o, a, X, ALU.add), name)

            def recip(o, a, name="dve_step"):
                step(V.reciprocal(o, a), name)

            def shrink(o, norm, name="dve_step"):
                ts(o, norm, EPS, ALU.max)
                recip(o, o)
                ts(o, o, REACH, ALU.mult, 1.0, ALU.min, name)

            def centre(src):
                total(sm("s1"), src)
                ts(sm("s1"), sm("s1"), 1.0 / D, ALU.mult)
                step(V.tensor_tensor(wide["dev"][:, :, :], src, per_row(sm("s1")), ALU.subtract), "dev")

            def lengths(p):
                dve.wait_ge(sem["n"], BLOCK[p] + 1)
                ts(sm("nf"), sm("n"), EPS, ALU.max)
                ts(sm("nc"), sm("nf"), MAX_TANH, ALU.min)
                ts(sm("ratio"), sm("nc"), -1.0, ALU.mult, 1.0, ALU.add)
                recip(sm("ratio"), sm("ratio"))
                stt(sm("ratio"), sm("nc"), 1.0, sm("ratio"), ALU.add, ALU.mult, "ratio")
                mul(sm("t"), sm("nc"), sm("nc"))
                ts(sm("poly"), sm("t"), 1.0 / 13, ALU.mult)
                for k in (11, 9, 7, 5, 3):
                    stt(sm("poly"), sm("poly"), 1.0 / k, sm("t"), ALU.add, ALU.mult)
                stt(sm("poly"), sm("poly"), 1.0, sm("nc"), ALU.add, ALU.mult)
                ts(sm("pick"), sm("nc"), SERIES_BELOW, ALU.is_lt)
                dve.wait_ge(sem["ln"], BLOCK[p] + 1)
                stt(sm("poly"), sm("ln"), -0.5, sm("poly"), ALU.mult, ALU.add)
                mul(sm("poly"), sm("poly"), sm("pick"))
                stt(sm("fac"), sm("ln"), 0.5, sm("poly"), ALU.mult, ALU.add)
                recip(sm("nf"), sm("nf"))
                mul(sm("fac"), sm("fac"), sm("nf"))
                mul(sm("t"), sm("fac"), sm("fac"))
                dve.wait_ge(sem["dev2"], T * (BLOCK[p] + 1))
                stt(sm("var"), sm("dev2"), 1.0 / D, sm("t"), ALU.mult, ALU.mult)
                ts(sm("var"), sm("var"), 1e-6, ALU.add, name="var")

            def modulate(p, sc, sh):
                dve.wait_ge(sem["std"], BLOCK[p] + 1)
                recip(sm("std"), sm("std"))
                mul(sm("std"), sm("std"), sm("fac"))
                u = wide["u"][:, :, :]
                for b in range(B):
                    for t in range(TB * b, TB * b + TB):
                        free(V.scalar_tensor_tensor(out=u[:, t, :], in0=wide["dev"][:, t, :], scalar=sm("std")[:, t:t + 1],
                                                    in1=ada[:, b, sc:sc + D], op0=ALU.mult, op1=ALU.mult))
                    dve.wait_ge(sem["dve_step"], count["dve_step"])
                    ub = u[:, TB * b:TB * b + TB, :]
                    step(V.tensor_tensor(ub, ub, per_tile(ada[:, b, sh:sh + D], TB), ALU.add), "u")
                dve.wait_ge(sem["un"], BLOCK[p] + 1)
                shrink(sm("us"), sm("un"))

            def mobius(p, src, gate, zin, dst, name):
                dev, sq = wide["dev"][:, :, :], wide["sq"][:, :, :]
                for b in range(B):
                    r = slice(TB * b, TB * b + TB)
                    step(V.tensor_tensor(dev[:, r, :], zin[:, r, :], per_tile(ada[:, b, gate:gate + D], TB), ALU.mult), "w")
                mul(dst, src, dev)
                total(sm("xy"), dst)
                dve.wait_ge(sem["zn"], BLOCK[p] + 1)
                shrink(sm("zs"), sm("zn"))
                mul(sm("zs2"), sm("zs"), sm("zs"))
                dve.wait_ge(sem["wsq"], T * (BLOCK[p] + 1))
                mul(sm("w2"), sm("dev2"), sm("zs2"), "w2")
                mul(sm("xy"), sm("xy"), sm("zs"))
                dve.wait_ge(sem["wn"], BLOCK[p] + 1)
                ts(sm("wc"), sm("wn"), EPS, ALU.max, name="wc")
                recip(sm("t"), sm("wc"))
                dve.wait_ge(sem["th"], BLOCK[p] + 1)
                mul(sm("tr"), sm("th"), sm("t"))
                mul(sm("xy"), sm("xy"), sm("tr"))
                mul(sm("y2"), sm("tr"), sm("tr"))
                mul(sm("y2"), sm("y2"), sm("w2"))
                x2 = sm(p + "n2")
                ts(sm("xy"), sm("xy"), 2.0, ALU.mult, 1.0, ALU.add)
                mul(sm("t"), x2, sm("y2"))
                add(sm("t"), sm("t"), sm("xy"))
                ts(sm("t"), sm("t"), EPS, ALU.max)
                recip(sm("t"), sm("t"))
                add(sm("xy"), sm("xy"), sm("y2"))
                mul(sm("xy"), sm("xy"), sm("t"), "sf")
                ts(sm("y2"), x2, -1.0, ALU.mult, 1.0, ALU.add)
                mul(sm("tr"), sm("tr"), sm("zs"))
                mul(sm("y2"), sm("y2"), sm("tr"))
                mul(sm("y2"), sm("y2"), sm("t"))
                for t in range(T):
                    dve.wait_ge(sem["scaled"], T * BLOCK[p] + t + 1)
                    signal(V.scalar_tensor_tensor(out=dst[:, t, :], in0=dev[:, t, :], scalar=sm("y2")[:, t:t + 1],
                                                  in1=sq[:, t, :], op0=ALU.mult, op1=ALU.add), name)
                dve.wait_ge(sem[name], T)

            def put_o(l, t):
                dve.wait_ge(sem["pvD"], T * 4 * l + 4 * t + 4)
                free(V.tensor_copy(oTD[:, :, t * P:t * P + P], ps[:, 4 + t % 2, :].rearrange("p (a b) -> p a b", b=P)),
                     "o_D")

            dve.wait_ge(sem["x_in"], 16)
            centre(x[:, :, :])
            dve.wait_ge(sem["cst_in"], 16)
            step(V.tensor_copy(ident16[:, :], ident), "idents")
            step(V.tensor_copy(identb[:, :], ident), "idents")
            dve.wait_ge(sem["ada_in"], 32)
            for b in range(B):
                step(V.tensor_copy(cond_b[:, b, :], condT[:, b:b + 1].to_broadcast([P, P])), "cond_b")
            lengths("a")
            dve.wait_ge(sem["vec_in"], 16)
            for b in range(B):
                dve.wait_ge(sem["adaP"], b + 1)
                add(ada[:, b, 0:512], ps[:, 2 * b, :], v_("b_ada")[:, 0:512])
                add(ada[:, b, 512:768], ps[:, 2 * b + 1, 0:256], v_("b_ada")[:, 512:768])
            ts(ada[:, :, D:2 * D], ada[:, :, D:2 * D], 1.0, ALU.add)
            ts(ada[:, :, 4 * D:5 * D], ada[:, :, 4 * D:5 * D], 1.0, ALU.add)
            modulate("a", D, 0)

            def norms_a(b):
                dve.wait_ge(sem["zsqA"], TB * (b + 1))
                h2 = sm("h2", 3 * T * H)[:, 3 * H * TB * b:3 * H * TB * (b + 1)]
                total(h2, zsq[:, TB * b:TB * b + TB, :].rearrange("p t (h e) -> p (t h) e", e=HD))
                total(sm("r2", 3 * T)[:, 3 * TB * b:3 * TB * (b + 1)], h2.rearrange("p (r h) -> p r h", h=H), "z2A")

            for t in range(T):
                dve.wait_ge(sem["projected"], projected("a", t))
                taken(t, V.scalar_tensor_tensor(out=z[:, t, :], in0=ps[:, t % 6, 0:3 * D], scalar=sm("us")[:, t:t + 1],
                                                in1=v_("b_qkv"), op0=ALU.mult, op1=ALU.add))
                if t == T - 3:
                    norms_a(0)

            def heads_a(b):
                def part(name, k):
                    return sm(name, k * T)[:, k * TB * b:k * TB * (b + 1)]
                r = slice(TB * b, TB * b + TB)
                dve.wait_ge(sem["hnA"], 2 * (b + 1))
                rs, hf = part("rs", 3), part("hf", 3 * H)
                shrink(rs, part("rn", 3))
                ts(rs, rs, HEAD_SCALE, ALU.mult)
                hf3 = hf.rearrange("p (r h) -> p r h", h=H)
                mul(hf3, part("hn", 3 * H).rearrange("p (r h) -> p r h", h=H), per_row(rs, H))
                shrink(hf, hf)
                mul(hf3, hf3, per_row(rs, H))
                hf4 = hf.rearrange("p (t g) -> p t g", t=TB)
                step(V.tensor_copy(sm("one", T * H).rearrange("p (t h) -> p t h", h=H)[:, r, :],
                                   hf4[:, :, 2 * H:3 * H]), "hfA")
                zqk = z[:, r, 0:2 * D].rearrange("p t (h e) -> p t h e", e=HD)
                mul(zqk, zqk, hf4[:, :, 0:2 * H].unsqueeze(3).to_broadcast([P, TB, 2 * H, HD]))
                dve.wait_ge(sem["pads_clear"], 2)
                for pad, hi, lo, c in ((padq, 0, 2, 0), (padk, 0, 1, D)):
                    src = z[:, r, c:c + D].rearrange("p t (h e) -> p t h e", e=HD)
                    a = pad[:, r, :].rearrange("p t (h s e) -> p t h s e", s=4, e=HD)
                    step(V.tensor_copy(a[:, :, :, hi, :], src), "highA")
                    step(V.tensor_tensor(a[:, :, :, lo, :], src, a[:, :, :, hi, :], ALU.subtract), "lowA")
            norms_a(1)
            heads_a(0)

            def quantise_weights(i):
                dve.wait_ge(sem["vec2_in"], 16)
                dve.wait_ge(sem["w2_in"], 16 * 7)
                for w, al, rows, n in (((w_aq, "qkv_alpha", P, 192), (w_ap, "proj_alpha", 64, D))[i],):
                    r = wide["sq"][0:rows, 0:2, :].rearrange("p a b -> p (a b)")[:, 0:n]
                    recip(r, v_(al)[0:rows, :])
                    mul(w[:, :], w[:, :], r)
                    ts(w[:, :], w[:, :], -8.0, ALU.max, 7.0, ALU.min)
                    ts(w[:, :], w[:, :], ROUND, ALU.add, ROUND, ALU.subtract)
                    mul(w[:, :], w[:, :], v_(al)[0:rows, :], "w_quant")
                for name in (("q_zp", "k_zp"), ("v_zp", "attn_zp"))[i]:
                    ts(v_(name), v_(name), ROUND, ALU.add, ROUND, ALU.subtract)

            for G in range(B * 4 + 1):
                if G < B * 4:
                    dve.wait_ge(sem["tA"], G + 1)
                    free(V.tensor_copy(staged[:, G % 2, :], ps16[:, 6 + G % 2, 0:1024]), "stagedA")
                if G == 0:
                    heads_a(1)
                if G == 1:
                    step(V.tensor_copy(cmask[:, :], cst[:, P:2 * P]), "cmask")
                    step(V.tensor_copy(dmask[:, :], cst[:, 2 * P:2 * P + 256]), "dmask")
                if G in (1, 5):
                    quantise_weights(G // 4)
                if G == 7:
                    recip(sm("ia", 3 * H), vec[:, AT["q_alpha"][0]:AT["q_alpha"][0] + 3 * H])
                    mul(sm("fa", H), v_("attn_alpha"), v_("v_alpha"))
                    mul(sm("scB", H), v_("q_alpha"), v_("k_alpha"))
                    ts(sm("scB", H), sm("scB", H), HQ ** -0.5, ALU.mult)
                    ts(sm("zpa", H), v_("attn_zp"), U_ZERO, ALU.add)
                    ts(sm("zpu", H), v_("attn_zp"), 128.0, ALU.add, name="zpu")
                if G >= 1:
                    b, g = divmod(G - 1, 4)
                    dve.wait_ge(sem["pvA"], 4 * G)
                    if G >= 3:
                        dve.wait_ge(sem["oT_A"], G - 2)
                    free(V.tensor_copy(oT[:, (G - 1) % 2, :], ps[:, 4 + (G - 1) % 2, :]), "oT_A")
                    dve.wait_ge(sem["toA"], G)
                    o = ps[:, 4 + (G - 1) % 2, :].rearrange("p (t h e) -> p t h e", t=TB, h=4)
                    rs = sm("rsumA", 16).rearrange("p (t h) -> p t h", h=4)
                    recip(rs, o[:, :, :, HD])
                    mul(o_tok[:, TB * b:TB * b + TB, 32 * g:32 * g + 32].rearrange("p t (h e) -> p t h e", h=4),
                        o[:, :, :, 0:HD], rs.unsqueeze(3).to_broadcast([P, TB, 4, HD]), "oA")
            for t in range(T):
                dve.wait_ge(sem["projected"], projected("ao", t))
                taken(t, V.scalar_tensor_tensor(out=z[:, t, 0:D], in0=ps[:, t % 6, 0:D], scalar=1.0 / HEAD_SCALE,
                                                in1=v_("b_o"), op0=ALU.mult, op1=ALU.add))
            mobius("a", x[:, :, :], 2 * D, z[:, :, 0:D], wide["x1"][:, :, :], "x1")
            centre(wide["x1"][:, :, :])
            lengths("m")
            modulate("m", 4 * D, 3 * D)
            for t in range(T):
                dve.wait_ge(sem["projected"], projected("m", t))
                taken(t, V.scalar_tensor_tensor(out=hid1[:, t, :], in0=ps[:, t % 6, :], scalar=sm("us")[:, t:t + 1],
                                                in1=v_("b_f1"), op0=ALU.mult, op1=ALU.add))
            dve.wait_ge(sem["fn"], 1)
            shrink(sm("fs"), sm("fn"))
            for t in range(T):
                dve.wait_ge(sem["projected"], projected("f", t))
                taken(t, V.scalar_tensor_tensor(out=zF[:, t, :], in0=ps[:, t % 6, 0:D], scalar=sm("fs")[:, t:t + 1],
                                                in1=v_("b_f2"), op0=ALU.mult, op1=ALU.add))
            mobius("m", wide["x1"][:, :, :], 5 * D, zF, wide["u"][:, :, :], "y")

            def vectors(name, n):
                return vec[:, AT[name][0]:AT[name][0] + n]

            def heads_b(b):
                return z[:, TB * b:TB * b + TB, 0:192].rearrange("p t (h e) -> p t h e", e=HQ)

            def by_head(a):
                return a.unsqueeze(1).unsqueeze(3).to_broadcast([P, TB, a.shape[1], HQ])

            def scale_b(b):
                if b == 0:
                    dve.wait_ge(sem["dve_step"], count["dve_step"])
                mul(heads_b(b), heads_b(b), by_head(sm("ia", 3 * H)))
                add(heads_b(b), heads_b(b), by_head(vectors("q_zp", 3 * H)))

            def round_b(b):
                dve.wait_ge(sem["pads_clear"], 4)
                ts(heads_b(b), heads_b(b), -8.0, ALU.max, 7.0, ALU.min)
                ts(heads_b(b), heads_b(b), ROUND, ALU.add, ROUND, ALU.subtract, "roundedB")

            def parts_b(b):
                q = heads_b(b)[:, :, 0:H, :]
                a = padq[:, TB * b:TB * b + TB, :].rearrange("p t (h s e) -> p t h s e", s=8, e=HQ)
                step(V.tensor_tensor(q, q, by_head(v_("q_zp")), ALU.subtract))
                step(V.tensor_copy(a[:, :, :, 0, :], q))
                step(V.tensor_tensor(a[:, :, :, 1, :], q, a[:, :, :, 0, :], ALU.subtract), "padsB")

            for t in range(T):
                dve.wait_ge(sem["projected"], projected("b", t))
                free(V.tensor_copy(z[:, t, 128:192], ps[:, t % 6, 128:192]))
                taken(t, V.tensor_tensor(z[:, t, 0:128].rearrange("p (h e) -> p h e", e=HQ),
                                         ps[:, t % 6, 0:128].rearrange("p (h e) -> p h e", e=HQ),
                                         per_row(vectors("bias_q", 2 * H), HQ), ALU.add))
                if t == T - 3:
                    scale_b(0)
            round_b(0)
            parts_b(0)

            def rates(m):
                dve.wait_ge(sem["expB"], 4 * m + 4)
                if m >= 2:
                    dve.wait_ge(sem["quantB"], 4 * (m - 1))
                c, h = 4 * (m % 2), 4 * (m // TB % 4)
                r = sm("rB", 8)[:, c:c + 4]
                mul(r, sm("sumB", 8)[:, c:c + 4], v_("attn_alpha")[:, h:h + 4])
                free(V.reciprocal(r, r), "rB")

            def codes_half(m):
                dve.wait_ge(sem["ptB"], 2 * m + 2)
                free(copy_codes(V.tensor_copy, m, 1), "ptcB1")

            def stage_b(G):
                dve.wait_ge(sem["tB"], G + 1)
                free(V.tensor_copy(staged[:, G % 2, :], ps16[:, 7, 0:1024]), "stagedB")

            def values_b(b):
                r = slice(TB * b, TB * b + TB)
                o4 = outB[:, r, :].rearrange("p t (h e) -> p t h e", h=H)
                o = z[:, r, 0:64].rearrange("p t (h e) -> p t h e", e=HQ)
                one = sm("one", T * H).rearrange("p (t h) -> p t h", h=H)[:, r, :]
                mul(one, o4[:, :, :, HQ], v_("v_zp").unsqueeze(1).to_broadcast([P, TB, H]))
                step(V.tensor_tensor(o, o4[:, :, :, 0:HQ], one.unsqueeze(3).to_broadcast([P, TB, H, HQ]), ALU.subtract))
                mul(o, o, by_head(sm("fa", H)), "zB")
            stage_b(0)
            for n in range(B * H + 5):
                if n < B * H:
                    for half in range(2):
                        dve.wait_ge(sem["stB"], 2 * n + half + 1)
                        c = 4 * (n % 2) + 2 * half
                        h = 4 * (n // TB % 4) + 2 * half
                        if n >= 2:
                            dve.wait_ge(sem["expB"], 4 * (n - 1))
                        nm, nb = (sm(name, 8)[:, c:c + 2] for name in ("nmB", "nbB"))
                        step(V.tensor_reduce(nm, ps[:, 2 * half:2 * half + 2, :], X, ALU.max, negate=True))
                        free(V.tensor_tensor(nb, nm, sm("scB", H)[:, h:h + 2], ALU.mult), "maxB")
                        if half == 0 and n >= 1:
                            rates(n - 1)
                        if half == 0 and n >= 3:
                            codes_half(n - 3)
                    if n == H + 6:
                        values_b(0)
                    if n in (9, 10):
                        xb = x[:, TB * (n - 9):TB * (n - 8), :]
                        add(xb, xb, per_tile(v_("proj_b"), TB))
                    if n == 3:
                        scale_b(1)
                    if n == 5:
                        round_b(1)
                    if n == 7:
                        parts_b(1)
                    if n % TB == 2 and n // TB + 1 < B * 4:
                        stage_b(n // TB + 1)
                if n == B * H:
                    rates(n - 1)
                if B * H <= n < B * H + 3:
                    codes_half(n - 3)
                if n in (H + 4, B * H + 4):
                    b = n // H - 1
                    dve.wait_ge(sem["colsumB"], b + 1)
                    ob = outB[:, TB * b:TB * b + TB, :]
                    cs = sm("colsum", H * (HQ + 1))
                    step(V.tensor_copy(cs, ps[:, 6, 320:320 + H * (HQ + 1)]))
                    c3 = cs.rearrange("p (h e) -> p h e", h=H)
                    mul(c3, c3, sm("zpa", H).unsqueeze(2).to_broadcast([P, H, HQ + 1]))
                    step(V.tensor_tensor(ob, ps[:, 6, 0:320].rearrange("p (t c) -> p t c", t=TB),
                                         cs.unsqueeze(1).to_broadcast([P, TB, H * (HQ + 1)]), ALU.subtract), "outB")
            values_b(1)
            for b in range(B):
                dve.wait_ge(sem["imgP"], b + 1)
                add(img[:, b, 0:D], ps[:, 2 + b, 0:D], v_("uk_b"))
                add(img[:, b, D:2 * D], ps[:, 2 + b, D:2 * D], v_("uv_b"), "img")
            for t in range(T):
                dve.wait_ge(sem["projected"], projected("bo", t))
                taken(t, V.tensor_tensor(x[:, t, :], x[:, t, :], ps[:, t % 6, 0:D], ALU.add))

            def scale_c(b):
                q = z[:, TB * b:TB * b + TB, 0:D]
                ts(q, q, HD ** -0.5, ALU.mult, name="qC")
            for t in range(T):
                dve.wait_ge(sem["projected"], projected("c", t))
                taken(t, V.tensor_tensor(z[:, t, :], ps[:, t % 6, 0:3 * D], v_("c_attn_b"), ALU.add))
                if t == T - 3:
                    scale_c(0)
            scale_c(1)

            def split(b, i):
                r = slice(TB * b, TB * b + TB)
                pad = (padqC, padkC)[i][:, r, :].rearrange("p t (h s) -> p t h s", h=H)
                left = zsq[:, r, 0:D].rearrange("p t (h e) -> p t h e", e=HD)
                now = z[:, r, D * i:D * i + D].rearrange("p t (h e) -> p t h e", e=HD)
                for n, slots in enumerate((Q_SLOTS, K_SLOTS)[i]):
                    k = slots[0]
                    step(V.tensor_copy(pad[:, :, :, k:k + HD], now), "partC")
                    if n < 2:
                        step(V.tensor_tensor(left, now, pad[:, :, :, k:k + HD], ALU.subtract))
                        now = left
            nsimg = sm("nsimg", T * H).rearrange("p (t h) -> p t h", h=H)

            def image_scores(b):
                r = slice(TB * b, TB * b + TB)
                dve.wait_ge(sem["zimg"], b + 1)
                total(simg[:, r, :], zsq[:, r, D:2 * D].rearrange("p t (h e) -> p t h e", e=HD))
                ts(nsimg[:, r, :], simg[:, r, :], -1.0, ALU.mult)
            dve.wait_ge(sem["padsC_clear"], 4)
            split(0, 0)
            split(0, 1)
            image_scores(0)

            def stage_c(g):
                dve.wait_ge(sem["tC"], g + 1)
                free(V.tensor_copy(staged[:, g % 2, :], ps16[:, 7, 0:1024]), "stagedC")

            stage_c(0)
            for n in range(B * H + 4):
                b, h = divmod(n, H)
                if n < B * H:
                    for i, tiles in enumerate(((3,), (2, 0, 1))):
                        dve.wait_ge(sem["sC"], 2 * n + i + 1)
                        for qt in tiles:
                            bank, col = place(qt)
                            ins = V.tensor_reduce(nmx[:, TB * b + qt, h:h + 1], ps[:, bank, col:col + P * (qt + 1)], X,
                                                  ALU.max, negate=True)
                            if qt == tiles[-1]:
                                step(ins)
                        r = slice(TB * b + min(tiles), TB * b + max(tiles) + 1)
                        free(V.tensor_tensor(nmx[:, r, h], nmx[:, r, h], nsimg[:, r, h], ALU.min), "maxC")
                    if n % 2 == 0 and n + 2 < B * H:
                        stage_c(n // 2 + 1)
                    if n in (2, 3):
                        split(1, n - 2)
                    if n == 4:
                        image_scores(1)
                    if h == H - 1:
                        r = slice(TB * b, TB * b + TB)
                        dve.wait_ge(sem["maxC"], 2 * n + 2)
                        add(simg[:, r, :], simg[:, r, :], nmx[:, r, :], "imx")
                if 1 <= n <= B * H:
                    m = n - 1
                    dve.wait_ge(sem["ptC"], 2 * m + 2)
                    if m == 0:
                        dve.wait_ge(sem["vC"], 1)
                    if m >= 4:
                        dve.wait_ge(sem["pvC"], m // 2 - 1)
                    free(V.tensor_copy(probTC_V[:, m % 4, :], ps[:, 5, 0:256]), "ptC_V")
                if n in (H + 2, B * H + 2):
                    b = n // H - 1
                    r = slice(TB * b, TB * b + TB)
                    dve.wait_ge(sem["eimg"], b + 1)
                    mul(o_tok[:, r, :].rearrange("p t (h e) -> p t h e", e=HD),
                        img[:, b, D:2 * D].rearrange("p (h e) -> p h e", e=HD).unsqueeze(1).to_broadcast([P, TB, H, HD]),
                        eimg[:, r, :].unsqueeze(3).to_broadcast([P, TB, H, HD]))
                g = (n - 6) // 4
                if n >= 6 and (n - 6) % 4 == 0:
                    dve.wait_ge(sem["pvC"], 2 * g + 2)
                    free(V.tensor_copy(oT[:, g % 2, :], ps[:, 6, :]), "oT_C")
                if n >= 7 and (n - 7) % 4 == 0:
                    g = (n - 7) // 4
                    dve.wait_ge(sem["toC"], g + 1)
                    step(V.tensor_copy(outC[:, :, 4 * (g % 4):4 * (g % 4) + 4, :],
                                       ps[:, 7, :].rearrange("p (t h e) -> p t h e", t=TB, h=4)[:, :, :, 0:HD + 1]), "oC")
                    if g % 4 == 3:
                        b = g // 4
                        e3 = eimg[:, TB * b:TB * b + TB, :]
                        add(outC[:, :, :, HD], outC[:, :, :, HD], e3)
                        recip(outC[:, :, :, HD], outC[:, :, :, HD])
                        ob = o_tok[:, TB * b:TB * b + TB, :].rearrange("p t (h e) -> p t h e", e=HD)
                        add(ob, ob, outC[:, :, :, 0:HD])
                        mul(ob, ob, outC[:, :, :, HD].unsqueeze(3).to_broadcast([P, TB, H, HD]), "ocn")
            f, h = wide["u"], wide["x1"]

            def send(b):
                step(V.tensor_copy(h[:, TB * b:TB * b + TB, 0:64], f[:, TB * b:TB * b + TB, 0:64]), "f_ready")
            step(V.memset(h[0:1, 0:T:TB, 64:D], 0.0))
            for t in range(T):
                dve.wait_ge(sem["projected"], projected("co", t))
                taken(t, V.tensor_tensor(wide["u"][:, t, :], ps[:, t % 6, 0:D], v_("c_proj_b"), ALU.add))
                if t % TB == TB - 1:
                    send(t // TB)
            dn, dq8 = sm("dn", 16 * T), sm("dq8", 8 * T)
            for l in range(DEPTH):
                if l:
                    dve.wait_ge(sem["rope1"], 2 * l)
                for i, name in ((0, "q_scale"), (2, "k_scale")):
                    s_ = v_(name)[:, l * DHD:(l + 1) * DHD]
                    mul(ropeL[:, i], rope[:, i], per_tile(s_, TB))
                    for a in range(2):
                        mul(ropeL[:, i + 1, :, 32 * a:32 * a + 32], rope[:, i + 1, :, 32 * a:32 * a + 32],
                            per_tile(s_[:, 32 - 32 * a:64 - 32 * a], TB),
                            name="ropeL" if (i, a) == (2, 1) else "dve_step")

                def norms(t):
                    dve.wait_ge(sem["d_sq"], T * l + t + 1)
                    free(V.tensor_reduce(sm("dss", 16 * T)[:, 16 * t:16 * t + 16],
                                         sqD[:, t % TB, :].rearrange("p (n c) -> p n c", c=DHD), X, ALU.add), "d_ss")

                def factors(b):
                    dve.wait_ge(sem["d_n"], B * l + b + 1)
                    d_ = dn[:, 64 * b:64 * b + 64]
                    ts(d_, d_, 1e-12, ALU.max)
                    recip(d_, d_)
                    ts(dq8[:, 32 * b:32 * b + 32].rearrange("p (t h) -> p t h", t=TB),
                       d_.rearrange("p (t k h) -> p t k h", t=TB, k=2)[:, :, 0, :], 8.0, ALU.mult, name="d_dn")
                for a in (wide["sq"], wide["dev"]) if l == 0 else ():
                    step(V.memset(a[:, :, :].rearrange("p t c -> p (t c)").rearrange("p (n k) -> p n k", k=256)[:, :, 0:WINDOW],
                                  0.0), "outside")
                for t in range(TB):
                    norms(t)
                    if t % 2:
                        r1, r2 = (a[:, t // 2, :].rearrange("p (t h c) -> p t h c", t=2, h=DH) for a in (qTD, kTD))
                        step(rope_terms(V, t - 1, 2, 1, r1, r2, step))
                factors(0)
                for t in (0, 2):
                    r1 = qTD[:, t // 2, :].rearrange("p (t h c) -> p t h c", t=2, h=DH)
                    ins = scale_k(V, t, 2, r1)
                    signal(ins, "rope0")

                def add_o(b):
                    r = slice(TB * b, TB * b + TB)
                    dve.wait_ge(sem["do_mm"], T * l + TB * b + TB)
                    add(f[:, r, :], f[:, r, :], ps[:, 5 - b, :].rearrange("p (t c) -> p t c", t=TB), "do_ev")
                    send(b)

                def less_mean(b):
                    r = slice(TB * b, TB * b + TB)
                    dve.wait_ge(sem[f"shifted{b}"], 32 * (2 * l + 2))
                    total(sm("s1")[:, r], h[:, r, :])
                    ts(sm("s1")[:, r], sm("s1")[:, r], 1.0 / D, ALU.mult)
                    step(V.tensor_tensor(devL[:, r, :], h[:, r, :], per_row(sm("s1")[:, r]), ALU.subtract), "devD")

                def variance(b):
                    r = slice(TB * b, TB * b + TB)
                    dve.wait_ge(sem["lnsq"], B * l + b + 1)
                    total(sm("var")[:, r], sqL[:, r, :])
                    ts(sm("var")[:, r], sm("var")[:, r], 1.0 / D, ALU.mult, 1e-5, ALU.add, "lnvar")

                def normalise(b):
                    r = slice(TB * b, TB * b + TB)
                    dev = devL[:, r, :]
                    dve.wait_ge(sem["lnstd"], B * l + b + 1)
                    recip(sm("std")[:, r], sm("std")[:, r])
                    for t in range(TB * b, TB * b + TB):
                        free(V.scalar_tensor_tensor(out=devL[:, t, :], in0=devL[:, t, :], scalar=sm("std")[:, t:t + 1],
                                                    in1=v_("ln_g")[:, l * D:(l + 1) * D], op0=ALU.mult, op1=ALU.mult))
                    dve.wait_ge(sem["dve_step"], count["dve_step"])
                    add(dev, dev, per_tile(v_("ln_b")[:, l * D:(l + 1) * D], TB), "lnD")

                def turned_qk(b, i):
                    dve.wait_ge(sem["qkT_D"], 8 * (B * l + b) + i + 1)
                    free(evacuate_qk(V.tensor_copy, b, i), "qk_evV")
                norms(TB)
                norms(TB + 1)
                for t in range(TB, T):
                    if t + 2 < T:
                        norms(t + 2)
                    turned_qk(0, 2 * (t - TB) + 1)
                factors(1)
                for b in range(B):
                    for u in range(TB * 4 + 1):
                        U = T * 4 * l + TB * 4 * b + u
                        if u == TB * 4 and b == 0:
                            for i in (1, 3, 5, 7):
                                turned_qk(1, i)
                        if u < TB * 4:
                            t, pair = divmod(u, 4)
                            k0 = P if t == 0 else WINDOW
                            dve.wait_ge(sem["sD"], U + 1)
                            c = 2 * (U % 4)
                            if U >= 4:
                                dve.wait_ge(sem["expD"], 2 * (U - 3))
                            s2 = ps[:, 6 * (u % 2):6 * (u % 2) + 2, :]
                            nm, nb = (sm(n, 8)[:, c:c + 2] for n in ("nmD", "nbD"))
                            step(V.tensor_reduce(nm, s2[:, :, k0:256], X, ALU.max, negate=True))
                            hh = 8 * (TB * b + t) + 2 * pair
                            free(V.tensor_tensor(nb, nm, dq8[:, hh:hh + 2], ALU.mult), "maxD")
                        if u >= 1:
                            t = (u - 1) // 4
                            k0 = P if t == 0 else WINDOW
                            dve.wait_ge(sem["expD"], 2 * U)
                            c = 2 * ((U - 1) % 4)
                            rs = sm("rsD", 8)[:, c:c + 2]
                            recip(rs, sm("sumD", 8)[:, c:c + 2])
                            pr = prob_d(U - 1)[:, :, k0:256]
                            free(V.tensor_tensor(pr, pr, per_row(rs, 256 - k0), ALU.mult), "normD")
                        if u >= 8 and u % 4 == 0:
                            put_o(l, TB * b + u // 4 - 2)
                        if b == 1 and u == 4:
                            add_o(0)
                        if b == 1 and u == 8:
                            less_mean(0)
                        if b == 1 and u == 10:
                            variance(0)
                    put_o(l, TB * b + TB - 1)
                normalise(0)
                add_o(1)
                for t in range(T + 3):
                    if t < T:
                        dve.wait_ge(sem["e_mm"], T * l + t + 1)
                        k = 2 * (t % 2)
                        b1 = v_("b1")[:, l * 2 * HID:(l + 1) * 2 * HID]
                        free(V.tensor_tensor(hidD[:, t, HID:2 * HID], ps[:, k + 1, 0:HID], b1[:, HID:2 * HID], ALU.add),
                             "e_g")
                        free(V.tensor_tensor(hidD[:, t, 0:HID], ps[:, k, 0:HID], b1[:, 0:HID], ALU.add), "e_ev")
                    if 1 <= t <= T:
                        dve.wait_ge(sem["gelu"], T * l + t)
                        dve.wait_ge(sem["e_ev"], T * l + t)
                        free(V.tensor_tensor(hgD[:, t - 1, :], hidD[:, t - 1, 0:HID], hidD[:, t - 1, HID:2 * HID],
                                             ALU.mult), "hg")
                    if t in (1, 2):
                        (less_mean, variance)[t - 1](1)
                    if t >= 3:
                        v = t - 3
                        dve.wait_ge(sem["g_mm"], T * l + v + 1)
                        free(V.tensor_tensor(f[:, v, :], f[:, v, :], ps[:, 6 + v % 2, 0:D], ALU.add), "g_ev")
                        if v % TB == TB - 1:
                            dve.wait_ge(sem["g_ev"], T * l + v + 1)
                            b = v // TB
                            r = slice(TB * b, TB * b + TB)
                            add(f[:, r, :], f[:, r, :], per_tile(v_("b2")[:, l * D:(l + 1) * D], TB))
                            if l + 1 < DEPTH:
                                send(b)
                            else:
                                add(wide["dev"][:, r, :], f[:, r, :], x[:, r, :], "result")
                    if t == 3:
                        normalise(1)

        @block.tensor
        def _(pe):
            M = nc.tensor.matmul

            def transposes(p, src, rows=P, tiles=range(T)):
                for t in tiles:
                    ins = nc.tensor.transpose(ps[0:rows, 6 + t // 4, (t % 4) * P:(t % 4) * P + P], src(t), ident)
                    if t % 4 == 3:
                        ins.then_inc(sem["turned"], 1)

            def project(p, lhs, rhs, n, chunks=1):
                for t in range(T):
                    if t % 4 == 0 and p != "f":
                        pe.wait_ge(sem["turned_copied"], 2 * TURN[p] + t // 4 + 1)
                    if t >= 6:
                        pe.wait_ge(sem["taken"], projected(p, t - 6))
                    for c in range(chunks):
                        ins = M(ps[:, t % 6, 0:n], lhs(t, c), rhs(c), start=(c == 0), stop=(c == chunks - 1))
                    ins.then_inc(sem["projected"], 1)

            def tile_T(t, c=0):
                return uT[:, t * P:(t + 1) * P]

            pe.wait_ge(sem["cst_in"], 16)
            for b in range(B):
                pe.wait_ge(sem["cond_b"], b + 1)
                M(ps[:, 2 * b, :], cond_b[:, b, :], w_ada[:, 0:512], start=True, stop=True)
                M(ps[:, 2 * b + 1, 0:256], cond_b[:, b, :], w_ada[:, 512:768], start=True, stop=True)\
                    .then_inc(sem["adaP"], 1)
            for b in range(B):
                pe.wait_ge(sem["u"], b + 1)
                transposes("a", lambda t: wide["u"][:, t, :], tiles=range(TB * b, TB * b + TB))
            pe.wait_ge(sem["w_in"], 64)
            project("a", tile_T, lambda c: w_qkv[:, :], 3 * D)

            def parts_a(b):
                pe.wait_ge(sem["lowA"], 2 * (b + 1))
                pe.wait_ge(sem[f"twiceA{b}"], 4)

            def group_T(G, bank, padq, padk, cols, name, id16, view):
                b, g = divmod(G, cols)
                for i, pad in enumerate((padq, padk)):
                    for tt in range(TB):
                        ins = nc.tensor.transpose(view[:, bank, i * 512 + tt * P:i * 512 + tt * P + P],
                                                  pad[:, TB * b + tt, g * P:(g + 1) * P], id16)
                ins.then_inc(sem[name], 1)

            def st_a(n):
                G, kt = divmod(n, TB)
                pe.wait_ge(sem["stagedA"], G + 1)
                for j in range(4):
                    if n >= 1 and j % 2 == 0:
                        pe.wait_ge(sem["expA"], 2 * (n - 1) + j // 2 + 1)
                    k = staged[32 * j:32 * j + 32, G % 2, 512 + kt * P:512 + kt * P + P]
                    ins = M(ps[:, j, :], k, staged[32 * j:32 * j + 32, G % 2, 0:512], start=True, stop=True)
                    if j % 2 == 1:
                        ins.then_inc(sem["stA"], 1)

            def pv_a(n):
                G, kt = divmod(n, TB)
                b, g = divmod(G, 4)
                pe.wait_ge(sem["expA"], 2 * n + 2)
                if n == 0:
                    pe.wait_ge(sem["vA_ones"], 1)
                if n % (4 * TB) == 0:
                    pe.wait_ge(sem["vA"], b + 1)
                if kt == 0 and G >= 2:
                    pe.wait_ge(sem["oA"], G - 1)
                for j in range(4):
                    ins = M(ps[32 * j:32 * j + 32, 4 + G % 2, :], vA[:, TB * b + kt, 4 * g + j, :],
                            prob[:, n % 2, j * 512:j * 512 + 512], start=(kt == 0), stop=(kt == TB - 1))
                ins.then_inc(sem["pvA"], 1)

            def turn_back(bank, src, name):
                for tt in range(TB):
                    ins = nc.tensor.transpose(ps[:, bank, tt * P:tt * P + P], src[:, tt * P:tt * P + P], ident)
                ins.then_inc(sem[name], 1)

            def turn_back_a(G):
                pe.wait_ge(sem["oT_A"], G + 1)
                turn_back(4 + G % 2, oT[:, G % 2, :], "toA")

            parts_a(0)
            group_T(0, 6, padq, padk, 4, "tA", ident16[:, :], ps16)
            for n in range(B * 4 * TB + 1):
                if n < B * 4 * TB:
                    st_a(n)
                    if n % TB == 1 and n // TB + 1 < 8:
                        if n // TB + 1 == 4:
                            parts_a(1)
                        group_T(n // TB + 1, 6 + (n // TB + 1) % 2, padq, padk, 4, "tA", ident16[:, :], ps16)
                if n >= 1:
                    pv_a(n - 1)
                if n % TB == 2 and n > TB:
                    turn_back_a(n // TB - 1)
            turn_back_a(7)
            pe.wait_ge(sem["oA"], 8)
            transposes("ao", lambda t: o_tok[:, t, :])
            project("ao", tile_T, lambda c: w_o[:, :], D)
            for b in range(B):
                pe.wait_ge(sem["u"], B + b + 1)
                transposes("m", lambda t: wide["u"][:, t, :], tiles=range(TB * b, TB * b + TB))
            project("m", tile_T, lambda c: w_f1[:, :], FF)
            for g in range(8):
                pe.wait_ge(sem["taken"], projected("m", TB * (g // 4) + TB - 1))
                if g >= 2:
                    pe.wait_ge(sem["h1_uT"], g - 1)
                for tt in range(4):
                    t = 4 * (g // 4) + tt
                    ins = nc.tensor.transpose(ps[:, 6 + g % 2, tt * P:(tt + 1) * P], hid1[:, t, (g % 4) * P:(g % 4) * P + P],
                                              ident)
                ins.then_inc(sem["h1_T"], 1)
            pe.wait_ge(sem["h1_uT"], 8)
            project("f", lambda t, c: hid1T[:, c, t * P:(t + 1) * P], lambda c: w_f2[:, c, :], D, 4)

            pe.wait_ge(sem["y"], T)
            transposes("b", lambda t: wide["u"][:, t, :])
            pe.wait_ge(sem["w_quant"], 2)
            project("b", tile_T, lambda c: w_aq[:, :], 192)

            def s_b(n, heads):
                G, qt = divmod(n, TB)
                pe.wait_ge(sem["stagedB"], G + 1)
                for j in heads:
                    if n >= 1:
                        pe.wait_ge(sem["expB"], 4 * (n - 1) + j + 1)
                    r = slice(32 * j, 32 * j + 2 * HQ)
                    ins = M(ps[:, j, :], staged[r, G % 2, qt * P:qt * P + P], staged[r, G % 2, 512:1024],
                            start=True, stop=True)
                    if j % 2 == 1:
                        ins.then_inc(sem["stB"], 1)

            def pt_b(m):
                c16 = codes.bitcast(F16)
                for j in range(4):
                    pe.wait_ge(sem["quantB"], 4 * m + j + 1)
                    if j % 2 == 0 and m >= 1:
                        pe.wait_ge(sem[f"ptcB{j // 2}"], m)
                    for kt in range(TB):
                        c = (j % 2) * 512 + kt * P
                        ins = nc.tensor.transpose(ps16[:, 4 + j // 2, c:c + P],
                                                  c16[:, m % 4, j, kt * P:(kt + 1) * P], ident16[:, :])
                    if j % 2 == 1:
                        ins.then_inc(sem["ptB"], 1)

            def pv_b(m):
                G, qt = divmod(m, TB)
                b, g = divmod(G, 4)
                if m == H:
                    pe.wait_ge(sem["outB"], 1)
                for j in range(4):
                    if j % 2 == 0:
                        pe.wait_ge(sem[f"ptcB{j // 2}"], m + 1)
                    h = 4 * g + j
                    for kt in range(TB):
                        c = (qt * H + h) * (HQ + 1)
                        ins = M(ps[:, 6, c:c + HQ + 1], codesT[:, m % 2, j, kt * P:(kt + 1) * P],
                                vB[:, TB * b + kt, h, :], start=(kt == 0), stop=(kt == TB - 1))
                ins.then_inc(sem["pvB"], 1)
            pe.wait_ge(sem["codes_high"], 1)
            pe.wait_ge(sem["ones16"], 1)

            def parts_b(b):
                pe.wait_ge(sem["padsB"], b + 1)
                pe.wait_ge(sem[f"kvB{b}"], 3)
            pe.wait_ge(sem["vB_ones"], 1)
            parts_b(0)
            group_T(0, 7, padq, padk, 4, "tB", ident16[:, :], ps16)
            for n in range(B * H + 4):
                if n < B * H:
                    s_b(n, (0, 1))
                if 3 <= n < B * H + 3:
                    pt_b(n - 3)
                if n < B * H:
                    s_b(n, (2, 3))
                    if n % TB == 1 and n // TB + 1 < B * 4:
                        if n // TB + 1 == 4:
                            parts_b(1)
                        group_T(n // TB + 1, 7, padq, padk, 4, "tB", ident16[:, :], ps16)
                if n >= 4:
                    pv_b(n - 4)
                if n > 4 and (n - 3) % H == 0:
                    b = (n - 3) // H - 1
                    for kt in range(TB):
                        ins = M(ps[:, 6, 320:320 + H * (HQ + 1)], ones16[:, :],
                                vB[:, TB * b + kt, :, :].rearrange("p h e -> p (h e)"), start=(kt == 0), stop=(kt == TB - 1))
                    ins.then_inc(sem["colsumB"], 1)
            for b in range(B):
                M(ps[:, 2 + b, 0:2 * D], cond_b[:, b, :], w_img[:, :], start=True, stop=True).then_inc(sem["imgP"], 1)
            pe.wait_ge(sem["zB"], B)
            transposes("bo", lambda t: z[:, t, 0:64], 64)
            pe.wait_ge(sem["img"], 2)
            project("bo", lambda t, c: uT[0:64, t * P:(t + 1) * P], lambda c: w_ap[:, :], D)

            for b in range(B):
                pe.wait_ge(sem["taken"], projected("bo", TB * b + TB - 1))
                transposes("c", lambda t: x[:, t, :], tiles=range(TB * b, TB * b + TB))
            project("c", tile_T, lambda c: w_ca[:, :], 3 * D)

            def parts_c(b):
                pe.wait_ge(sem["partC"], 6 * (b + 1))
                pe.wait_ge(sem[f"againC{b}"], 6)
            parts_c(0)
            pe.wait_ge(sem["maskC"], 3)
            pe.wait_ge(sem["cmask"], 1)

            stb = staged[:, :, :].bitcast(BF16)

            def s_c(n, parts):
                G, j = divmod(n, 2)
                pe.wait_ge(sem["stagedC"], G + 1)
                r = slice(64 * j, 64 * j + 51)
                for qt, read in ((3, 1), (2, 3), (0, 3), (1, 4))[parts]:
                    if n >= 1 and qt:
                        pe.wait_ge(sem["expC"], 4 * (n - 1) + read)
                    bank, col = place(qt)
                    w = P * (qt + 1)
                    o = ps[:, bank, col:col + w]
                    M(o, stb[r, G % 2, qt * P:qt * P + P], stb[r, G % 2, 512:512 + w], start=True, stop=False)
                    ins = M(o[:, w - P:w], identb[:, :], cmask[:, :], start=False, stop=True)
                    if qt in (3, 1):
                        ins.then_inc(sem["sC"], 1)

            def t_c(n):
                pe.wait_ge(sem["expC"], 4 * n + 4)
                if n >= 1:
                    pe.wait_ge(sem["ptC_A"], n)
                    pe.wait_ge(sem["ptC_V"], n)
                for kt in (0, 1, 3, 2):
                    bank, col = place(3 - kt)
                    for qt in range(kt, TB):
                        c = col + (qt - kt) * P
                        a = at(qt) + kt * P
                        ins = nc.tensor.transpose(ps[:, 3 + bank, c:c + P], probC[:, n % 2, a:a + P], ident)
                    if kt in (3, 2):
                        ins.then_inc(sem["ptC"], 1)

            def pv_c(m):
                b = 2 * m // H
                if m % (H // 2) == 0:
                    pe.wait_ge(sem["vC"], b + 1)
                pe.wait_ge(sem["ptC_A"], 2 * m + 2)
                pe.wait_ge(sem["ptC_V"], 2 * m + 2)
                if m % 2 == 0 and m:
                    pe.wait_ge(sem["oT_C"], m // 2)
                for kt in range(TB):
                    for n in (2 * m, 2 * m + 1):
                        j = n % 4
                        a = at(3 - kt)
                        pt = prob_t(n)
                        if a >= 1024:
                            pt, a = probTC_V[:, n % 4, :], a - 1024
                        ins = M(ps[32 * j:32 * j + 32, 6, P * kt:512], vC[:, TB * b + kt, n % H, :],
                                pt[:, a:a + 512 - P * kt], start=(kt == 0), stop=(kt == TB - 1))
                ins.then_inc(sem["pvC"], 1)

            group_T(0, 7, padqC, padkC, 8, "tC", identb[:, :], psb16)
            s_c(0, slice(0, 1))
            for n in range(B * H + 4):
                if n < B * H:
                    s_c(n, slice(1, 4))
                    if n % 2 == 0 and n + 2 < B * H:
                        if n >= 8 and n % 4 == 0:
                            pe.wait_ge(sem["oC"], (n - 4) // 4)
                        if n // 2 + 1 == H // 2:
                            parts_c(1)
                        group_T(n // 2 + 1, 7, padqC, padkC, 8, "tC", identb[:, :], psb16)
                if 1 <= n <= B * H:
                    t_c(n - 1)
                if n + 1 < B * H:
                    s_c(n + 1, slice(0, 1))
                if n >= 7 and (n - 7) % 4 == 0:
                    g = (n - 7) // 4
                    pe.wait_ge(sem["oT_C"], g + 1)
                    if n // 2 + 1 <= B * H // 2:
                        pe.wait_ge(sem["stagedC"], n // 2 + 1)
                    turn_back(7, oT[:, g % 2, :], "toC")
                if n >= 3 and n % 2 == 1 and n < B * H + 2:
                    pv_c((n - 3) // 2)
            pe.wait_ge(sem["ocn"], B)
            transposes("co", lambda t: o_tok[:, t, :])
            project("co", tile_T, lambda c: w_cp[:, :], D)
            pe.wait_ge(sem["w3_in"], 16 * 5 * DEPTH)
            pe.wait_ge(sem["dmask"], 1)
            for l in range(DEPTH):
                for t in range(T):
                    if t in (0, 2):
                        b = t // 2
                        pe.wait_ge(sem[f"shifted{b}"], 32 * (2 * l + 1))
                        pe.wait_ge(sem["f_ready"], B * 2 * l + b + 1)
                        if l:
                            pe.wait_ge(sem["g_ev"], T * l - 1 + b)
                        transposes(f"d{l}", lambda t: wide["x1"][:, t, :], tiles=range(TB * b, TB * b + TB))
                    if t % TB == 0:
                        pe.wait_ge(sem["turned_copied"], 2 * TURN[f"d{l}"] + t // TB + 1)
                        if l == 0:
                            pe.wait_ge(sem["taken"], projected("co", T - 1))
                    if t >= 2:
                        pe.wait_ge(sem["d_ev"], T * l + t - 1)
                    for i in range(3):
                        ins = M(ps[:, 3 * (t % 2) + i, :], tile_T(t), w_d1[:, l, 512 * i:512 * i + 512], start=True, stop=True)
                    ins.then_inc(sem["d_mm"], 1)

                def turn_qk(b):
                    pe.wait_ge(sem[f"rope{b}"], 2 * (l + 1))
                    pe.wait_ge(sem["ropeQ"], 4 * l + 2 * (b + 1))
                    if b == 0:
                        pe.wait_ge(sem["d_ev"], T * (l + 1))
                        pe.wait_ge(sem["turned_copied"], 2 * TURN[f"d{l}"] + 2)
                    for i in range(8):
                        if i >= 4:
                            pe.wait_ge(sem["qk_evV" if i % 2 else "qk_evA"], 4 * (B * l + b) + (i - 4) // 2 + 1)
                        for tt in range(TB):
                            c = 512 * (i // 4) + P * (i % 4)
                            ins = nc.tensor.transpose(ps[:, S_BANKS[i % 4], tt * P:(tt + 1) * P],
                                                      qkvD[:, TB * b + tt, c:c + P], ident)
                        ins.then_inc(sem["qkT_D"], 1)

                def project_o(t):
                    pe.wait_ge(sem["o_D"], T * l + TB * (t // TB) + TB)
                    for c in range(4):
                        ins = M(ps[:, 5 - t // TB, (t % TB) * P:(t % TB) * P + P], oTD[:, c, t * P:(t + 1) * P],
                                w_do[:, l, c, :], start=(c == 0), stop=(c == 3))
                    ins.then_inc(sem["do_mm"], 1)

                turn_qk(0)
                for b in range(B):
                    pe.wait_ge(sem["qk_evA"], 4 * (B * l + b + 1))
                    pe.wait_ge(sem["qk_evV"], 4 * (B * l + b + 1))
                    for u in range(TB * 4 + 3):
                        U = T * 4 * l + TB * 4 * b + u
                        if u == TB * 4 and b == 0:
                            pe.wait_ge(sem["expD"], 2 * U)
                            turn_qk(1)
                        if u < TB * 4:
                            t, pair = divmod(u, 4)
                            t += TB * b
                            k0 = P if t % TB == 0 else WINDOW
                            if u >= 2:
                                pe.wait_ge(sem["expD"], 2 * (U - 1))
                            for j in range(2):
                                M(ps[:, 6 * (u % 2) + j, k0:256], qTD[64 * j:64 * j + 64, pair, t * P:(t + 1) * P],
                                  kTD[64 * j:64 * j + 64, pair, (t - 1) * P + k0:(t + 1) * P], start=True, stop=False)
                            for j in range(2):
                                ins = M(ps[:, 6 * (u % 2) + j, k0:256], identb[:, :], dmask[:, k0:256],
                                        start=False, stop=True)
                            ins.then_inc(sem["sD"], 1)
                        if b == 1 and u < TB:
                            project_o(u)
                        if 2 <= u < TB * 4 + 2:
                            v = u - 2
                            first = v < 4
                            pe.wait_ge(sem["normD"], U - 1)
                            if l == 0 and U < 4:
                                pe.wait_ge(sem["outside"], 2)
                            if U >= 4:
                                pe.wait_ge(sem["ptcD"], U - 3)
                            for j in range(2):
                                for k in ((1,) if first else (0, 1)):
                                    c = 256 * j + P * k
                                    ins = nc.tensor.transpose(ps[:, 2 + v % 2, c:c + P],
                                                              prob_d(U - 2)[:, j, P * k:P * k + P], ident)
                            ins.then_inc(sem["ptD"], 1)
                        if u >= 3:
                            v = u - 3
                            t, pair = divmod(v, 4)
                            t += TB * b
                            pe.wait_ge(sem["ptcD"], U - 2)
                            if pair == 0 and T * l + t >= 2:
                                pe.wait_ge(sem["o_D"], T * l + t - 1)
                            if pair == 0 and t == TB + 1:
                                pe.wait_ge(sem["do_ev"], B * l + 1)
                            ks = (1,) if t % TB == 0 else (0, 1)
                            for k in ks:
                                for j in range(2):
                                    hh = 2 * pair + j
                                    c = 256 * j + P * k
                                    ins = M(ps[64 * j:64 * j + 64, 4 + t % 2, P * pair:P * pair + P],
                                            qkvD[:, t - 1 + k, 1024 + DHD * hh:1024 + DHD * hh + DHD],
                                            probTD[:, v % 2, c:c + P], start=(k == ks[0]), stop=(k == 1))
                            ins.then_inc(sem["pvD"], 1)
                for t in range(TB, T):
                    project_o(t)
                for t in range(T + 3):
                    if t < T:
                        if t % TB == 0:
                            b = t // TB
                            pe.wait_ge(sem["lnD"], B * l + b + 1)
                            transposes(f"e{l}", lambda t: devL[:, t, :], tiles=range(TB * b, TB * b + TB))
                            pe.wait_ge(sem["turned_copied"], 2 * TURN[f"e{l}"] + t // TB + 1)
                        if t >= 2:
                            pe.wait_ge(sem["e_ev"], T * l + t - 1)
                        for i in range(2):
                            ins = M(ps[:, 2 * (t % 2) + i, 0:HID], tile_T(t), w_h1[:, l, HID * i:HID * i + HID], start=True, stop=True)
                        ins.then_inc(sem["e_mm"], 1)
                    if 2 <= t < T + 2:
                        v = t - 2
                        pe.wait_ge(sem["hg"], T * l + v + 1)
                        if v >= 2:
                            pe.wait_ge(sem["g_uT"], 2 * (T * l + v - 1))
                        for c in range(3):
                            w = P if c < 2 else HID - 2 * P
                            ins = nc.tensor.transpose(ps[0:w, 4 + v % 2, c * P:(c + 1) * P], hgD[:, v, c * P:c * P + w], ident)
                        ins.then_inc(sem["g_T"], 1)
                    if t >= 3:
                        v = t - 3
                        pe.wait_ge(sem["g_uT"], 2 * (T * l + v + 1))
                        if v >= 2:
                            pe.wait_ge(sem["g_ev"], T * l + v - 1)
                        for c in range(3):
                            w = P if c < 2 else HID - 2 * P
                            ins = M(ps[:, 6 + v % 2, 0:D], hidTD[0:w, c, v * P:(v + 1) * P],
                                    w_h2[0:w, l, c, :], start=(c == 0), stop=(c == 2))
                        ins.then_inc(sem["g_mm"], 1)


def rope_tables():
    f = np.float32
    half = np.arange(0, DHD, 2, dtype=f)
    inv = (f(1.0) / (f(10000.0) ** (half / f(DHD)))).astype(f)
    t = np.arange(S, dtype=f)
    freqs = (t[:, None] * inv[None, :]).astype(f)
    base = ((half + f(0.4 * DHD)) / f(1.4 * DHD)).astype(f)
    power = ((t - f(S // 2)) / f(WINDOW // 2)).astype(f)
    scale = (base[None, :] ** power[:, None]).astype(f)
    cos, sin = np.cos(freqs), np.sin(freqs)

    def both(a, b):
        return np.concatenate([a, b], axis=1).astype(f)
    return np.stack([both(cos * scale, cos * scale), both(-sin * scale, sin * scale),
                     both(cos / scale, cos / scale), both(-sin / scale, sin / scale)])


def masks():
    i = np.arange(P)[:, None]
    causal = np.where(np.arange(P)[None, :] > i, NEG_C, 0.0)
    j = np.arange(256)[None, :] - P
    band = np.where((j > i) | (j < i - WINDOW), NEG_D, 0.0)
    return np.concatenate([np.eye(P), causal, band], axis=1).astype(np.float32)


def lay_out(i):
    a = {k: np.asarray(v) for k, v in i.items()}
    c, q, e, f = "L0_cond_", "L0_attn_", "L0_cond2_", "L0_ffn_"
    parts = {
        "b_ada": a[c + "b_ada"], "b_qkv": np.concatenate([a[c + "b_q"], a[c + "b_k"], a[c + "b_v"]]),
        "b_o": a[c + "b_o"], "b_f1": a[c + "b_f1"], "b_f2": a[c + "b_f2"],
        "c_attn_b": a[e + "c_attn_b"], "c_proj_b": a[e + "c_proj_b"], "uk_b": a[e + "uk_b"], "uv_b": a[e + "uv_b"],
    }
    for n in ("qkv_alpha", "proj_alpha", "proj_b", "bias_q", "bias_k", "q_alpha", "k_alpha", "v_alpha", "q_zp", "k_zp",
              "v_zp", "attn_alpha", "attn_zp"):
        parts[n] = a[q + n]
    for n in ("q_scale", "k_scale", "ln_g", "ln_b", "b1", "b2"):
        parts[n] = a[f + n]
    return {
        "x": a["x"], "condT": a["cond_1024"].T, "maskT": a["mask_Bx1x1xS_ff0"].reshape(T, P).T,
        "vec": np.concatenate([parts[n].reshape(-1) for n, _ in VECTORS])[None, :],
        "cst": masks(), "rope": rope_tables(),
        "w_ada": a[c + "w_ada"], "w_qkv": np.concatenate([a[c + "w_q"], a[c + "w_k"], a[c + "w_v"]], axis=1),
        "w_o": a[c + "w_o"], "w_f1": a[c + "w_f1"], "w_f2": a[c + "w_f2"],
        "w_aqT": a[q + "qkv_w"].T, "w_apT": a[q + "proj_w"].T, "w_ca": a[e + "c_attn_w"], "w_cp": a[e + "c_proj_w"],
        "w_imgT": np.concatenate([a[e + "uk_w"].T, a[e + "uv_w"].T], axis=1),
        "wqkv": a[f + "wqkv"], "wo": a[f + "wo"], "w1": a[f + "w1"], "w2": a[f + "w2"],
    }


def kernel(**inputs):
    import concourse.bacc as bacc
    from concourse.bass_utils import run_bass_kernel_spmd
    arrays = {"in_" + n: np.ascontiguousarray(a) for n, a in lay_out(inputs).items()}
    nc = bacc.Bacc("TRN2", target_bir_lowering=False, num_devices=1)
    d = {n[3:]: nc.dram_tensor(n, a.shape, F32, kind="ExternalInput").ap() for n, a in arrays.items()}
    out = nc.dram_tensor("out", (B, S, D), F32, kind="ExternalOutput").ap()
    build(nc, d, out)
    return run_bass_kernel_spmd(nc, [arrays], core_ids=[0]).results[0]["out"]
```
